# Optimizing a Trainium2 kernel written in Bass

```python
import numpy as np
import jax
import jax.numpy as jnp

def _softmax(x, axis=-1):
    return jax.nn.softmax(x, axis=axis)

def _gelu(x):
    return jax.nn.gelu(x, approximate=True)

def _silu(x):
    return jax.nn.silu(x)

def _sigmoid(x):
    return jax.nn.sigmoid(x)

def _layernorm(x, axis=-1, eps=1e-05):
    m = jnp.mean(x, axis=axis, keepdims=True)
    v = jnp.var(x, axis=axis, keepdims=True)
    return (x - m) / jnp.sqrt(v + eps)

def _scatter_add(tgt, idx, src, axis=0):
    return tgt.at[idx].add(src)

def _segment_sum(src, seg, n):
    return jax.ops.segment_sum(src, seg, n)
kernel_name = 'mk_decoder_preln_d1_seqx_r8_af9605'

def setup_inputs(seed: int=0):
    np.random.seed(seed)
    _w = jnp.asarray

    def _rec_inputs():
        import jax
        import jax.numpy as jnp
        _rk = jax.random.key(seed)
        x = 7.22e-05 + 1 * jax.random.normal(jax.random.fold_in(_rk, 1), (32, 64, 512), jnp.float32)
        _lenS = 64 - jax.random.randint(jax.random.fold_in(_rk, 7), (32,), 0, max(1, 64 // 4) + 1, jnp.int32)
        _lenS2 = 64 - jax.random.randint(jax.random.fold_in(_rk, 8), (32,), 0, max(1, 64 // 4) + 1, jnp.int32)
        _ctx_4096P = jax.random.normal(jax.random.fold_in(_rk, 11), (32, 16, 512), jnp.float32)
        _ctx_4096c = jax.random.dirichlet(jax.random.fold_in(_rk, 511), 0.3 * jnp.ones((16,), jnp.float32), (32, 64))
        _ctx_4096t = jnp.einsum('bsk,bkd->bsd', _ctx_4096c, _ctx_4096P)
        _ctx_4096t = _ctx_4096t * jax.lax.rsqrt(jnp.mean(jnp.square(_ctx_4096t)) + 1e-12) * 0.953939
        ctx_4096 = 4.13588e-05 + 0.999923 * (_ctx_4096t + 0.3 * jax.random.normal(jax.random.fold_in(_rk, 611), (32, 64, 512), jnp.float32))
        return (x, ctx_4096)
    x, ctx_4096 = _rec_inputs()

    def _L0_attn_setup():
        import jax, jax.numpy as jnp
        import numpy as np
        import math
        B, L, D, H = (32, 64, 512, 32)
        HD = D // H
        key = jax.random.key(seed)
        ks = jax.random.split(key, 9)
        s = 1.0 / math.sqrt(D)
        return {'x': jax.random.normal(ks[0], (B, L, D), jnp.float32), 'Wq': jax.random.normal(ks[1], (D, D), jnp.float32) * s, 'bq': jax.random.normal(ks[2], (D,), jnp.float32) * s, 'Wk': jax.random.normal(ks[3], (D, D), jnp.float32) * s, 'bk': jax.random.normal(ks[4], (D,), jnp.float32) * s, 'Wv': jax.random.normal(ks[5], (D, D), jnp.float32) * s, 'bv': jax.random.normal(ks[6], (D,), jnp.float32) * s, 'Wo': jax.random.normal(ks[7], (D, D), jnp.float32) * s, 'bo': jax.random.normal(ks[8], (D,), jnp.float32) * s}
    _L0_attn_all = _L0_attn_setup()
    _L0_attn_in = {k: v for k, v in _L0_attn_all.items() if k in ('Wq', 'bq', 'Wk', 'bk', 'Wv', 'bv', 'Wo', 'bo')}
    del _L0_attn_all

    def _L0_xattn_setup():
        import jax, jax.numpy as jnp
        import numpy as np
        HEADS = 8
        WINDOW = 16

        def _pointwise(W, b, t):
            return jnp.einsum('oc,bct->bot', W, t) + b[None, :, None]
        key = jax.random.key(seed)
        ks = jax.random.split(key, 10)
        B, C, T = (4, 64, 512)
        s = 0.02
        return {'x': jax.random.normal(ks[0], (B, C, T), jnp.float32), 'cond': jax.random.normal(ks[1], (B, C, T), jnp.float32), 'Wq': jax.random.normal(ks[2], (C, C), jnp.float32) * s, 'bq': jnp.zeros((C,), jnp.float32), 'Wk': jax.random.normal(ks[3], (C, C), jnp.float32) * s, 'bk': jnp.zeros((C,), jnp.float32), 'Wv': jax.random.normal(ks[4], (C, C), jnp.float32) * s, 'bv': jnp.zeros((C,), jnp.float32), 'Wo': jax.random.normal(ks[5], (C, C), jnp.float32) * s, 'bo': jnp.zeros((C,), jnp.float32)}
    _L0_xattn_all = _L0_xattn_setup()
    _L0_xattn_in = {k: v for k, v in _L0_xattn_all.items() if k in ('Wq', 'bq', 'Wk', 'bk', 'Wv', 'bv', 'Wo', 'bo')}
    del _L0_xattn_all

    def _L0_ffn_setup():
        import jax, jax.numpy as jnp
        import numpy as np
        HID, INT, LAT, NE, K = (512, 1024, 256, 8, 2)
        LN_EPS = 1e-05

        def _layernorm(x, gamma, beta):
            mu = jnp.mean(x, axis=-1, keepdims=True)
            var = jnp.var(x, axis=-1, keepdims=True)
            return (x - mu) * jax.lax.rsqrt(var + LN_EPS) * gamma + beta
        key = jax.random.key(seed)
        ks = jax.random.split(key, 8)
        s = lambda d: 1.0 / np.sqrt(d)
        return {'hidden_states': jax.random.normal(ks[0], (4, 256, HID), jnp.float32), 'gate_w': jax.random.normal(ks[1], (HID, NE), jnp.float32) * s(HID), 'up_w': jax.random.normal(ks[2], (HID, INT), jnp.float32) * s(HID), 'down_w': jax.random.normal(ks[3], (INT, HID), jnp.float32) * s(INT), 'fc1_w': jax.random.normal(ks[4], (HID, LAT), jnp.float32) * s(HID), 'fc2_w': jax.random.normal(ks[5], (LAT, HID), jnp.float32) * s(LAT), 'expert_w': jax.random.normal(ks[6], (LAT, LAT), jnp.float32), 'ln_gamma': jnp.ones((HID,), jnp.float32), 'ln_beta': jnp.zeros((HID,), jnp.float32)}
    _L0_ffn_all = _L0_ffn_setup()
    _L0_ffn_in = {k: v for k, v in _L0_ffn_all.items() if k in ('gate_w', 'up_w', 'down_w', 'fc1_w', 'fc2_w', 'expert_w', 'ln_gamma', 'ln_beta')}
    del _L0_ffn_all
    return {'x': x, 'ctx_4096': ctx_4096, 'L0_attn_Wq': _L0_attn_in['Wq'], 'L0_attn_bq': _L0_attn_in['bq'], 'L0_attn_Wk': _L0_attn_in['Wk'], 'L0_attn_bk': _L0_attn_in['bk'], 'L0_attn_Wv': _L0_attn_in['Wv'], 'L0_attn_bv': _L0_attn_in['bv'], 'L0_attn_Wo': _L0_attn_in['Wo'], 'L0_attn_bo': _L0_attn_in['bo'], 'L0_xattn_Wq': _L0_xattn_in['Wq'], 'L0_xattn_bq': _L0_xattn_in['bq'], 'L0_xattn_Wk': _L0_xattn_in['Wk'], 'L0_xattn_bk': _L0_xattn_in['bk'], 'L0_xattn_Wv': _L0_xattn_in['Wv'], 'L0_xattn_bv': _L0_xattn_in['bv'], 'L0_xattn_Wo': _L0_xattn_in['Wo'], 'L0_xattn_bo': _L0_xattn_in['bo'], 'L0_ffn_gate_w': _L0_ffn_in['gate_w'], 'L0_ffn_up_w': _L0_ffn_in['up_w'], 'L0_ffn_down_w': _L0_ffn_in['down_w'], 'L0_ffn_fc1_w': _L0_ffn_in['fc1_w'], 'L0_ffn_fc2_w': _L0_ffn_in['fc2_w'], 'L0_ffn_expert_w': _L0_ffn_in['expert_w'], 'L0_ffn_ln_gamma': _L0_ffn_in['ln_gamma'], 'L0_ffn_ln_beta': _L0_ffn_in['ln_beta']}

def reference(x, ctx_4096, L0_attn_Wq, L0_attn_bq, L0_attn_Wk, L0_attn_bk, L0_attn_Wv, L0_attn_bv, L0_attn_Wo, L0_attn_bo, L0_xattn_Wq, L0_xattn_bq, L0_xattn_Wk, L0_xattn_bk, L0_xattn_Wv, L0_xattn_bv, L0_xattn_Wo, L0_xattn_bo, L0_ffn_gate_w, L0_ffn_up_w, L0_ffn_down_w, L0_ffn_fc1_w, L0_ffn_fc2_w, L0_ffn_expert_w, L0_ffn_ln_gamma, L0_ffn_ln_beta):
    import jax
    import jax.numpy as jnp

    def _L0_attn_ref(x, Wq, bq, Wk, bk, Wv, bv, Wo, bo):
        import jax, jax.numpy as jnp
        import numpy as np
        import math
        B, L, D, H = (32, 64, 512, 32)
        HD = D // H
        b, l, d = x.shape
        h, hd = (H, HD)
        q = (x @ Wq.T + bq).reshape(b, l, h, hd).transpose(0, 2, 1, 3)
        k = (x @ Wk.T + bk).reshape(b, l, h, hd).transpose(0, 2, 1, 3)
        v = (x @ Wv.T + bv).reshape(b, l, h, hd).transpose(0, 2, 1, 3)
        scores = jnp.einsum('bhqd,bhkd->bhqk', q, k) / math.sqrt(hd)
        causal = jnp.tril(jnp.ones((l, l), bool))
        scores = jnp.where(causal, scores, -jnp.inf)
        att = jax.nn.softmax(scores, axis=-1)
        out = jnp.einsum('bhqk,bhkd->bhqd', att, v)
        out = out.transpose(0, 2, 1, 3).reshape(b, l, d)
        return out @ Wo.T + bo

    def _L0_xattn_ref(x, cond, Wq, bq, Wk, bk, Wv, bv, Wo, bo):
        import jax, jax.numpy as jnp
        import numpy as np
        HEADS = 8
        WINDOW = 16

        def _pointwise(W, b, t):
            return jnp.einsum('oc,bct->bot', W, t) + b[None, :, None]
        B, C, T = x.shape
        H, W = (HEADS, WINDOW)
        hd = C // H
        scale = hd ** (-0.5)
        pad_left = W // 2
        pad_right = W - pad_left - 1
        q = _pointwise(Wq, bq, x)
        k = _pointwise(Wk, bk, cond)
        v = _pointwise(Wv, bv, cond)
        k = jnp.pad(k, ((0, 0), (0, 0), (pad_left, pad_right)))
        v = jnp.pad(v, ((0, 0), (0, 0), (pad_left, pad_right)))
        idx = jnp.arange(T)[:, None] + jnp.arange(W)[None, :]
        k_win = k[:, :, idx].reshape(B, H, hd, T, W)
        v_win = v[:, :, idx].reshape(B, H, hd, T, W)
        qh = q.reshape(B, H, hd, T)
        dots = jnp.einsum('bhdt,bhdtw->bhtw', qh, k_win) * scale
        attn = jax.nn.softmax(dots, axis=-1)
        out = jnp.einsum('bhtw,bhdtw->bhdt', attn, v_win)
        out = out.reshape(B, C, T)
        return _pointwise(Wo, bo, out)

    def _L0_ffn_ref(hidden_states, gate_w, up_w, down_w, fc1_w, fc2_w, expert_w, ln_gamma, ln_beta):
        import jax, jax.numpy as jnp
        import numpy as np
        HID, INT, LAT, NE, K = (512, 1024, 256, 8, 2)
        LN_EPS = 1e-05

        def _layernorm(x, gamma, beta):
            mu = jnp.mean(x, axis=-1, keepdims=True)
            var = jnp.var(x, axis=-1, keepdims=True)
            return (x - mu) * jax.lax.rsqrt(var + LN_EPS) * gamma + beta
        logits = jnp.einsum('bsh,he->bse', hidden_states, gate_w)
        routing_weights, selected_experts = jax.lax.top_k(logits, K)
        h = jax.nn.relu(jnp.einsum('bsh,hi->bsi', hidden_states, up_w)) ** 2
        shared_out = jnp.einsum('bsi,ih->bsh', h, down_w)
        x_latent = jnp.einsum('bsh,hl->bsl', hidden_states, fc1_w)
        expert_out = jnp.einsum('bsl,lm->bsm', x_latent, expert_w)
        moe_out = expert_out * jnp.sum(routing_weights, axis=-1, keepdims=True)
        routed_out = jnp.einsum('bsl,lh->bsh', moe_out, fc2_w)
        return _layernorm(shared_out + routed_out, ln_gamma, ln_beta)
    x = x + _L0_attn_ref(_layernorm(x, axis=-1), L0_attn_Wq, L0_attn_bq, L0_attn_Wk, L0_attn_bk, L0_attn_Wv, L0_attn_bv, L0_attn_Wo, L0_attn_bo)
    x = x + _L0_xattn_ref(_layernorm(x, axis=-1), ctx_4096, L0_xattn_Wq, L0_xattn_bq, L0_xattn_Wk, L0_xattn_bk, L0_xattn_Wv, L0_xattn_bv, L0_xattn_Wo, L0_xattn_bo)
    x = x + _L0_ffn_ref(_layernorm(x, axis=-1), L0_ffn_gate_w, L0_ffn_up_w, L0_ffn_down_w, L0_ffn_fc1_w, L0_ffn_fc2_w, L0_ffn_expert_w, L0_ffn_ln_gamma, L0_ffn_ln_beta)
    return x

_drawn_inputs = setup_inputs


def setup_inputs(seed=0):
    import zlib

    import numpy as np

    out = dict(_drawn_inputs(seed))
    spreads = {'L0_xattn_bq': (0.0, 0.8),
     'L0_xattn_bk': (0.0, 2.0),
     'L0_xattn_bv': (0.0, 0.786),
     'L0_xattn_bo': (0.0, 0.347),
     'L0_ffn_ln_gamma': (1.0, 0.2),
     'L0_ffn_ln_beta': (0.0, 0.391)}
    factors = {'ctx_4096': 7.119,
     'L0_attn_bq': 4.965,
     'L0_attn_bk': 64.0,
     'L0_xattn_Wq': 8.0,
     'L0_xattn_Wk': 8.0,
     'L0_xattn_Wv': 7.016,
     'L0_xattn_Wo': 3.542,
     'L0_ffn_up_w': 3.751,
     'L0_ffn_down_w': 3.531}
    for name, (base, spread) in spreads.items():
        noise = np.random.default_rng([zlib.crc32(name.encode()), seed]).standard_normal(out[name].shape)
        drawn = base * np.exp(spread * noise) if base else spread * noise
        out[name] = jnp.asarray(drawn.astype(out[name].dtype))
    for name, factor in factors.items():
        out[name] = (out[name] * factor).astype(out[name].dtype)
    return out
```

```python
from contextlib import ExitStack

import concourse.bass as bass
from concourse import mybir

BATCH, SEQ, DIM = 32, 64, 512
P = 128
TOKENS = BATCH * SEQ
PAIRS = TOKENS // P
DUOS = PAIRS // 2
KC = DIM // P
HEADS, HD = 32, 16
GROUPS = HEADS * HD // P
GH = HEADS // GROUPS
XH, XHD, WIN = 8, 8, 16
PADL = WIN // 2
BH = 2 * XH
HALF = P // BH
INT, LAT, NE = 1024, 256, 8
IC, LC = INT // P, LAT // P
LN_EPS = 1e-5
MASKED = -1e30

F32 = mybir.dt.float32
F32R = mybir.dt.float32r
BF16 = mybir.dt.bfloat16
ALU = mybir.AluOpType
ACT = mybir.ActivationFunctionType
AX_X = mybir.AxisListType.X


def wait(eng, sem, value):
    if isinstance(value, int) and value <= 0:
        return
    eng.wait_ge(sem, value)


class Banks:

    def __init__(self, nc, ctx, name, tiles, slot, early, last):
        self.tiles, self.at, self.last = tiles, slot, last
        self.full = [ctx.enter_context(nc.semaphore(f"{name}_full{b}")) for b in range(len(tiles))]
        self.freed = [ctx.enter_context(nc.semaphore(f"{name}_freed{b}")) for b in range(len(tiles))]
        self.early = early
        self.order = list(slot)

    def tile(self, unit):
        return self.tiles[self.at[unit]]

    def before(self, unit, m):
        same = [u for u in self.order if self.at[u] == self.at[unit]]
        ahead = [u for u in same if u in self.early]
        if unit in self.early:
            if isinstance(m, int) and m == 0:
                return ahead.index(unit)
            return (m - 1) * len(same) + len(ahead) + same.index(unit)
        if isinstance(m, int) and m == self.last:
            return m * len(same) + len(ahead) + [u for u in same if u not in ahead].index(unit)
        return m * len(same) + len(ahead) + same.index(unit)

    def wait_free(self, eng, unit, m):
        wait(eng, self.freed[self.at[unit]], self.before(unit, m))

    def wait_full(self, eng, unit, m):
        wait(eng, self.full[self.at[unit]], self.before(unit, m) + 1)

    def wait_read(self, eng, unit, m):
        wait(eng, self.freed[self.at[unit]], self.before(unit, m) + 1)

    def full_sem(self, unit):
        return self.full[self.at[unit]]

    def freed_sem(self, unit):
        return self.freed[self.at[unit]]


def steps(eng, slot, last_full, last):
    slot(0)
    with eng.Fori(1, last_full + 1) as d:
        slot(d)
    for d in range(last_full + 1, last + 1):
        slot(d)


def split3(pe, out, lhs, rhs, chunks, start=True, stop=True):
    passes = [(a, b) for c in range(chunks) for a, b in ((0, 0), (0, 1), (1, 0))]
    last = None
    for n, (a, b) in enumerate(passes):
        c = n // 3
        last = pe.matmul(out, lhs(a, c), rhs(b, c), start=start and n == 0, stop=stop and n == len(passes) - 1)
    return last


def attention_phase(nc, psum, x, wqT, bq, wkT, bk, wvT, bv, woT, bo, y):
    x_d = x.rearrange("(d p t) f -> d t p f", p=2, t=P)
    y_t = y.rearrange("(n t) f -> n t f", t=P)
    with ExitStack() as ctx:
        def sb(name, shape, dt=F32):
            return ctx.enter_context(nc.sbuf_tensor(f"a_{name}", shape, dt))

        def sem(name):
            return ctx.enter_context(nc.semaphore(f"a_{name}"))

        w_hl = {n: [sb(f"w{n}_{part}", [P, KC, DIM], F32R) for part in ("hi", "lo")] for n in "kqvo"}
        stage = [sb(f"stage{i}", [P, KC, DIM]) for i in range(2)]
        bq_col, bk_col = sb("bq_col", [P, GROUPS]), sb("bk_col", [P, GROUPS])
        bv_row, bo_row = sb("bv_row", [P, DIM]), sb("bo_row", [P, DIM])
        ident, ident_b = sb("ident", [P, P]), sb("ident_b", [P, P], BF16)
        causal = sb("causal", [P, SEQ], BF16)
        head_of = sb("head_of", [P, GH])
        pow_half, eps = sb("pow_half", [P, 2]), sb("eps", [P, 2])
        carrier = sb("carrier", [P, 1])
        xin, xres = sb("xin", [P, 2, DIM]), sb("xres", [P, 2, DIM])
        stats, mv = sb("stats", [P, 2, 6]), sb("mv", [P, 2, 2])
        veps, rstd = sb("veps", [P, 2]), sb("rstd", [P, 2])
        xln = sb("xln", [P, 2, DIM])
        xT = [sb(f"xT_{part}", [P, KC, 2 * P], F32R) for part in ("hi", "lo")]
        kT = sb("kT", [P, GROUPS, 2 * P])
        qz = sb("qz", [P, 2, GROUPS, 4, SEQ])
        kbd = sb("kbd", [P, 2, GROUPS, 2, GH, SEQ])
        vbd = sb("vbd", [P, 2, 2, HEADS // 2, 2, HD])
        prob = sb("prob", [P, GROUPS, GH, SEQ])
        mx, sm, rs = (sb(n, [P, GROUPS, GH]) for n in ("mx", "sm", "rs"))
        probT = sb("probT", [P, GROUPS, 4, P])
        oT = [sb(f"oT_{part}", [P, GROUPS, P], F32R) for part in ("hi", "lo")]
        yo = sb("yo", [P, 2, DIM])

        score = psum[0:4]
        A_UNITS = ["X0", "X1", "K0", "K1", "K2", "K3", "Q0", "Q1", "Q2", "Q3", "V0", "V1"]
        ORDER = (["X0", "X1", "K0", "K1", "K2", "K3"] + [f"P0{g}" for g in range(4)] + ["O0"]
                 + ["Q0", "Q1", "Q2", "Q3", "Y0", "V0"] + [f"P1{g}" for g in range(4)] + ["O1", "V1", "Y1"])
        work = Banks(nc, ctx, "a_work", psum[4:8], {u: n % 4 for n, u in enumerate(ORDER)}, A_UNITS, DUOS - 1)

        w_loaded = [sem(f"w_loaded{i}") for i in range(2)]
        w_hi, w_lo = sem("w_hi"), sem("w_lo")
        bias_loaded, bias_scaled = sem("bias_loaded"), sem("bias_scaled")
        const_step, const_ready = sem("const_step"), sem("const_ready")
        zeros_ready, pow_ready = sem("zeros_ready"), sem("pow_ready")
        x_loaded, res_loaded = sem("x_loaded"), [sem(f"res_loaded{p}") for p in range(2)]
        res_biased = [sem(f"res_biased{p}") for p in range(2)]
        stats_done, aggr_done, veps_done, rstd_done = sem("stats_done"), sem("aggr_done"), sem("veps_done"), sem("rstd_done")
        xln_ready, xhi_ready = sem("xln_ready"), sem("xhi_ready")
        kbd_ready = sem("kbd_ready")
        score_full = [sem(f"score_full{g}") for g in range(4)]
        score_freed = [sem(f"score_freed{g}") for g in range(4)]
        mx_ready, exp_done, sum_done, rs_ready, prob_ready = (
            sem(n) for n in ("mx_ready", "exp_done", "sum_done", "rs_ready", "prob_ready"))
        ohi_ready = sem("ohi_ready")
        y_stored = [sem(f"y_stored{p}") for p in range(2)]

        block = ctx.enter_context(nc.Block())

        @block.sync
        def _(sp):
            sp.dma_start(xin[:], x_d[0]).then_inc(x_loaded, 16)
            srcs = (wkT, wqT, wvT, woT)
            for n in range(2):
                sp.dma_start(stage[n][:], srcs[n].rearrange("(k p) n -> p k n", p=P)).then_inc(w_loaded[n], 16)
            sp.dma_start(bk_col[:], bk).then_inc(bias_loaded, 16)
            sp.dma_start(bq_col[:], bq).then_inc(bias_loaded, 16)
            sp.dma_start(bv_row[:], bv.partition_broadcast(P)).then_inc(bias_loaded, 16)
            sp.dma_start(bo_row[:], bo.partition_broadcast(P)).then_inc(bias_loaded, 16)
            for n in range(2, 4):
                wait(sp, w_lo, n - 1)
                sp.dma_start(stage[n % 2][:], srcs[n].rearrange("(k p) n -> p k n", p=P)).then_inc(w_loaded[n % 2], 16)
            wait(sp, xln_ready, 2)
            sp.dma_start(xin[:], x_d[1]).then_inc(x_loaded, 16)
            for p in range(2):
                sp.dma_start(xres[:, p, :], x_d[0][:, p, :]).then_inc(res_loaded[p], 16)

            def slot(d):
                if not isinstance(d, int) or d < DUOS - 2:
                    wait(sp, xln_ready, 2 * d + 4)
                    sp.dma_start(xin[:], x_d[d + 2]).then_inc(x_loaded, 16)
                for p in range(2):
                    work.wait_read(sp, f"Y{p}", d)
                    sp.dma_start(y_t[d * 2 + p], yo[:, p, :]).then_inc(y_stored[p], 16)
                    if not isinstance(d, int) or d < DUOS - 1:
                        sp.dma_start(xres[:, p, :], x_d[d + 1][:, p, :]).then_inc(res_loaded[p], 16)

            steps(sp, slot, DUOS - 3, DUOS - 1)
            for p in range(2):
                sp.wait_ge(y_stored[p], 16 * DUOS)

        @block.gpsimd
        def _(pool):
            pool.memset(ident[:], 0.0).then_inc(const_step, 1)
            pool.memset(causal[:], 0.0).then_inc(const_step, 1)
            pool.memset(head_of[:], 1.0).then_inc(const_step, 1)
            pool.memset(pow_half[:], -0.5).then_inc(pow_ready, 1)
            pool.memset(eps[:], LN_EPS).then_inc(pow_ready, 1)
            pool.wait_ge(const_step, 3)
            pool.affine_select(out=ident[:], in_=ident[:], compare_op=ALU.not_equal, fill=1.0, base=0,
                               pattern=[[-1, P]], channel_multiplier=1).then_inc(const_step, 1)
            for b in range(2):
                half = causal[b * SEQ:(b + 1) * SEQ, :]
                pool.wait_ge(const_step, 4 + b)
                pool.affine_select(out=half, in_=half, compare_op=ALU.is_ge, fill=MASKED, base=0,
                                   pattern=[[-1, SEQ]], channel_multiplier=1).then_inc(const_step, 1)
            pool.wait_ge(const_step, 6)
            pool.affine_select(out=head_of[:], in_=head_of[:], compare_op=ALU.is_ge, fill=0.0, base=0,
                               pattern=[[-HD, GH]], channel_multiplier=1).then_inc(const_step, 1)
            pool.wait_ge(const_step, 7)
            pool.affine_select(out=head_of[:], in_=head_of[:], compare_op=ALU.is_ge, fill=0.0, base=HD - 1,
                               pattern=[[HD, GH]], channel_multiplier=-1).then_inc(const_step, 1)
            pool.tensor_copy(ident_b[:], ident[:]).then_inc(const_step, 1)

            def rstd_of(m):
                wait(pool, aggr_done, 2 * m + 2)
                pool.tensor_tensor(veps[:], mv[:, :, 1], eps[:], ALU.add).then_inc(veps_done, 1)
                wait(pool, veps_done, m + 1)
                pool.tensor_tensor(rstd[:], veps[:], pow_half[:], ALU.pow).then_inc(rstd_done, 1)

            def bias_residual(m, p):
                wait(pool, res_loaded[p], 16 * m + 16)
                wait(pool, bias_loaded, 64)
                pool.tensor_tensor(xres[:, p, :], xres[:, p, :], bo_row[:], ALU.add).then_inc(res_biased[p], 1)

            def normalise(m, p, g):
                wait(pool, rs_ready, 8 * m + 4 * p + g + 1)
                pool.tensor_tensor(prob[:, g], prob[:, g], rs[:, g].unsqueeze(2).to_broadcast([P, GH, SEQ]),
                                   ALU.mult).then_inc(prob_ready, 1)

            pool.wait_ge(pow_ready, 2)
            rstd_of(0)

            def slot(d):
                if not isinstance(d, int) or d < DUOS - 1:
                    rstd_of(d + 1)
                for p in range(2):
                    for g in range(4):
                        normalise(d, p, g)
                    bias_residual(d, p)

            steps(pool, slot, DUOS - 2, DUOS - 1)

        @block.scalar
        def _(act):
            for n, name in enumerate("kqvo"):
                wait(act, w_loaded[n % 2], 16 * (n // 2) + 16)
                act.activation(w_hl[name][0][:], stage[n % 2][:], ACT.Copy).then_inc(w_hi, 1)
            act.wait_ge(bias_loaded, 64)
            act.activation(bq_col[:], bq_col[:], ACT.Copy, scale=HD ** -0.5).then_inc(bias_scaled, 1)
            act.wait_ge(zeros_ready, 2)

            def x_hi(m, p):
                work.wait_full(act, f"X{p}", m)
                act.activation(xT[0][:, :, p * P:(p + 1) * P], work.tile(f"X{p}")[:].rearrange("p (k t) -> p k t", k=KC),
                               ACT.Copy).then_inc(xhi_ready, 1)

            def k_out(m, c):
                if c == 0:
                    wait(act, kbd_ready, 2 * m)
                work.wait_full(act, f"K{c}", m)
                act.activation(kT[:, c, :], work.tile(f"K{c}")[:, 0:2 * P], ACT.Identity,
                               bias=bk_col[:, c:c + 1]).then_inc(work.freed_sem(f"K{c}"), 1)

            def q_out(m, c):
                work.wait_full(act, f"Q{c}", m)
                act.wait_ge(bias_scaled, 1)
                act.activation(qz[:, :, c, 0:4:3, :],
                               work.tile(f"Q{c}")[:, 0:2 * P].rearrange("p (a b t) -> p a b t", a=2, b=2),
                               ACT.Identity, bias=bq_col[:, c:c + 1], scale=HD ** -0.5).then_inc(work.freed_sem(f"Q{c}"), 1)

            def exp(m, p, g):
                wait(act, score_freed[g], 2 * m + p + 1)
                act.activation(prob[:, g], prob[:, g], ACT.Exp).then_inc(exp_done, 1)

            def probT_out(m, p, g):
                u = f"P{p}{g}"
                work.wait_full(act, u, m)
                act.activation(probT[:, g], work.tile(u)[:].rearrange("p (j t) -> p j t", j=4), ACT.Copy)\
                   .then_inc(work.freed_sem(u), 1)

            def o_hi(m, p):
                work.wait_full(act, f"O{p}", m)
                act.activation(oT[0][:], work.tile(f"O{p}")[:].rearrange("p (g t) -> p g t", g=4), ACT.Copy)\
                   .then_inc(ohi_ready, 1)

            def project(m):
                for p in range(2):
                    x_hi(m, p)
                for c in range(4):
                    k_out(m, c)

            project(0)
            for c in range(4):
                q_out(0, c)

            def slot(d):
                more = not isinstance(d, int) or d < DUOS - 1
                for g in range(4):
                    exp(d, 0, g)
                if more:
                    project(d + 1)
                for g in range(4):
                    probT_out(d, 0, g)
                o_hi(d, 0)
                for g in range(4):
                    exp(d, 1, g)
                if more:
                    for c in range(4):
                        q_out(d + 1, c)
                for g in range(4):
                    probT_out(d, 1, g)
                o_hi(d, 1)

            steps(act, slot, DUOS - 2, DUOS - 1)

        @block.vector
        def _(dve):
            dve.memset(qz[:], 0.0).then_inc(zeros_ready, 1)
            dve.memset(vbd[:], 0.0).then_inc(zeros_ready, 1)

            def layernorm(m):
                wait(dve, x_loaded, 16 * m + 16)
                for p in range(2):
                    dve.bn_stats(stats[:, p, :], xin[:, p, :]).then_inc(stats_done, 1)
                wait(dve, stats_done, 2 * m + 2)
                dve.memset(carrier[:, 0:1], 0.0)
                for p in range(2):
                    dve.bn_aggr(mv[:, p, :], stats[:, p, :]).then_inc(aggr_done, 1)

            def apply_norm(m):
                wait(dve, rstd_done, m + 1)
                wait(dve, xhi_ready, 2 * m)
                for p in range(2):
                    dve.tensor_scalar(xln[:, p, :], xin[:, p, :], mv[:, p, 0:1], rstd[:, p:p + 1],
                                      ALU.subtract, ALU.mult).then_inc(xln_ready, 1)

            def x_lo(m, p):
                wait(dve, xhi_ready, 2 * m + p + 1)
                dve.tensor_tensor(xT[1][:, :, p * P:(p + 1) * P], work.tile(f"X{p}")[:].rearrange("p (k t) -> p k t", k=KC),
                                  xT[0][:, :, p * P:(p + 1) * P].bitcast(F32), ALU.subtract)\
                   .then_inc(work.freed_sem(f"X{p}"), 1)

            def spread_keys(m, p):
                work.wait_read(dve, "K3", m)
                if not (isinstance(m, int) and m == 0):
                    wait(dve, score_full[3], 2 * m - 1 + p)
                for h in range(GH):
                    ins = dve.tensor_scalar(kbd[:, p, :, :, h, :],
                                            kT[:, :, p * P:(p + 1) * P].rearrange("p g (b t) -> p g b t", b=2),
                                            head_of[:, h:h + 1], None, ALU.mult)
                ins.then_inc(kbd_ready, 1)

            def values_out(m, p):
                u = f"V{p}"
                work.wait_full(dve, u, m)
                for b in range(2):
                    for par in range(2):
                        cols = slice(b * SEQ, (b + 1) * SEQ)
                        ins = dve.tensor_tensor(
                            vbd[par * SEQ:(par + 1) * SEQ, p, b, :, par, :],
                            work.tile(u)[cols, :].rearrange("p (j r d) -> p j r d", r=2, d=HD)[:, :, par, :],
                            bv_row[cols, :].rearrange("p (j r d) -> p j r d", r=2, d=HD)[:, :, par, :], ALU.add)
                ins.then_inc(work.freed_sem(u), 1)

            def less_max(m, p, g):
                n = 8 * m + 4 * p + g + 1
                wait(dve, score_full[g], 2 * m + p + 1)
                s = score[g][:].rearrange("p (h k) -> p h k", h=GH)
                dve.tensor_reduce(mx[:, g, :], s, AX_X, ALU.max).then_inc(mx_ready, 1)
                wait(dve, mx_ready, n)
                dve.tensor_tensor(prob[:, g], s, mx[:, g].unsqueeze(2).to_broadcast([P, GH, SEQ]),
                                  ALU.subtract).then_inc(score_freed[g], 1)

            def row_sum(m, p, g):
                n = 8 * m + 4 * p + g + 1
                wait(dve, exp_done, n)
                dve.tensor_reduce(sm[:, g, :], prob[:, g], AX_X, ALU.add).then_inc(sum_done, 1)
                wait(dve, sum_done, n)
                dve.reciprocal(rs[:, g, :], sm[:, g, :]).then_inc(rs_ready, 1)

            def softmax(m, p):
                less_max(m, p, 0)
                less_max(m, p, 1)
                row_sum(m, p, 0)
                less_max(m, p, 2)
                row_sum(m, p, 1)
                less_max(m, p, 3)
                row_sum(m, p, 2)
                row_sum(m, p, 3)

            def o_lo(m, p):
                wait(dve, ohi_ready, 2 * m + p + 1)
                dve.tensor_tensor(oT[1][:], work.tile(f"O{p}")[:].rearrange("p (g t) -> p g t", g=4),
                                  oT[0][:].bitcast(F32), ALU.subtract).then_inc(work.freed_sem(f"O{p}"), 1)

            def y_out(m, p):
                u = f"Y{p}"
                work.wait_full(dve, u, m)
                wait(dve, res_biased[p], m + 1)
                wait(dve, y_stored[p], 16 * m)
                dve.tensor_tensor(yo[:, p, :], work.tile(u)[:], xres[:, p, :], ALU.add).then_inc(work.freed_sem(u), 1)

            layernorm(0)
            for n, name in enumerate("kqvo"):
                wait(dve, w_hi, n + 1)
                dve.tensor_tensor(w_hl[name][1][:], stage[n % 2][:], w_hl[name][0][:].bitcast(F32),
                                  ALU.subtract).then_inc(w_lo, 1)
                if n == 0:
                    apply_norm(0)
            for p in range(2):
                x_lo(0, p)
            dve.wait_ge(const_step, 9)
            for p in range(2):
                spread_keys(0, p)
            dve.wait_ge(bias_loaded, 64)
            dve.wait_ge(zeros_ready, 2)
            for p in range(2):
                values_out(0, p)

            def slot(d):
                more = not isinstance(d, int) or d < DUOS - 1
                if more:
                    layernorm(d + 1)
                    apply_norm(d + 1)
                softmax(d, 0)
                if more:
                    x_lo(d + 1, 0)
                    x_lo(d + 1, 1)
                    spread_keys(d + 1, 0)
                o_lo(d, 0)
                softmax(d, 1)
                if more:
                    spread_keys(d + 1, 1)
                y_out(d, 0)
                if more:
                    values_out(d + 1, 0)
                o_lo(d, 1)
                if more:
                    values_out(d + 1, 1)
                y_out(d, 1)

            steps(dve, slot, DUOS - 2, DUOS - 1)

        @block.tensor
        def _(pe):
            def x_transposes(m, p):
                u = f"X{p}"
                wait(pe, xln_ready, 2 * m + p + 1)
                work.wait_free(pe, u, m)
                for c in range(KC):
                    ins = pe.transpose(work.tile(u)[:, c * P:(c + 1) * P], xln[:, p, c * P:(c + 1) * P], ident[:])
                ins.then_inc(work.full_sem(u), 1)

            def transposed(m, name, c):
                u = f"{name}{c}"
                if c == 0:
                    work.wait_read(pe, "X0", m)
                    work.wait_read(pe, "X1", m)
                work.wait_free(pe, u, m)
                w = w_hl[name.lower()]
                split3(pe, work.tile(u)[:, 0:2 * P], lambda a, k: w[a][:, k, c * P:(c + 1) * P],
                       lambda b, k: xT[b][:, k, :], KC).then_inc(work.full_sem(u), 1)

            def values(m, p):
                u = f"V{p}"
                work.wait_free(pe, u, m)
                split3(pe, work.tile(u)[:], lambda a, k: xT[a][:, k, p * P:(p + 1) * P],
                       lambda b, k: w_hl["v"][b][:, k, :], KC).then_inc(work.full_sem(u), 1)

            def scores(m, p):
                wait(pe, kbd_ready, 2 * m + p + 1)
                work.wait_read(pe, "Q3", m)
                for g in range(4):
                    wait(pe, score_freed[g], 2 * m + p)
                    pe.matmul(score[g][:], ident_b[:], causal[:].unsqueeze(1).to_broadcast([P, GH, SEQ]),
                              start=True, stop=False)
                    for b in range(2):
                        ins = pe.matmul(score[g][:], qz[:, p, g, 2 * b:2 * b + 2, :], kbd[:, p, g, b, :, :],
                                        start=False, stop=b == 1)
                    ins.then_inc(score_full[g], 1)

            def prob_transposes(m, p, g):
                u = f"P{p}{g}"
                wait(pe, prob_ready, 8 * m + 4 * p + g + 1)
                work.wait_free(pe, u, m)
                for j in range(4):
                    ins = pe.transpose(work.tile(u)[:, j * P:(j + 1) * P], prob[:, g, 2 * j:2 * j + 2, :], ident[:])
                ins.then_inc(work.full_sem(u), 1)

            def attend(m, p):
                u = f"O{p}"
                work.wait_free(pe, u, m)
                work.wait_read(pe, f"V{p}", m)
                for g in range(4):
                    work.wait_read(pe, f"P{p}{g}", m)
                    for j in range(4):
                        for b in range(2):
                            at = g * P + b * SEQ
                            ins = pe.matmul(work.tile(u)[32 * j:32 * j + 32, at:at + SEQ],
                                            vbd[:, p, b, 4 * g + j, :, :],
                                            probT[:, g, j, b * SEQ:(b + 1) * SEQ], start=True, stop=True)
                ins.then_inc(work.full_sem(u), 1)

            def out_projection(m, p):
                u = f"Y{p}"
                work.wait_read(pe, f"O{p}", m)
                work.wait_free(pe, u, m)
                split3(pe, work.tile(u)[:], lambda a, k: oT[a][:, k, :],
                       lambda b, k: w_hl["o"][b][:, k, :], KC).then_inc(work.full_sem(u), 1)

            pe.wait_ge(const_step, 9)
            for p in range(2):
                x_transposes(0, p)
            wait(pe, w_lo, 1)
            for c in range(4):
                transposed(0, "K", c)
            wait(pe, w_lo, 2)
            for c in range(4):
                transposed(0, "Q", c)
            wait(pe, w_lo, 3)
            for p in range(2):
                values(0, p)
            wait(pe, w_lo, 4)

            def slot(d):
                more = not isinstance(d, int) or d < DUOS - 1
                scores(d, 0)
                if more:
                    for p in range(2):
                        x_transposes(d + 1, p)
                    for c in range(4):
                        transposed(d + 1, "K", c)
                for g in range(4):
                    prob_transposes(d, 0, g)
                attend(d, 0)
                scores(d, 1)
                if more:
                    for c in range(4):
                        transposed(d + 1, "Q", c)
                out_projection(d, 0)
                if more:
                    values(d + 1, 0)
                for g in range(4):
                    prob_transposes(d, 1, g)
                attend(d, 1)
                if more:
                    values(d + 1, 1)
                out_projection(d, 1)

            steps(pe, slot, DUOS - 2, DUOS - 1)


def window_phase(nc, psum, x, cond, wqT, bq, wkT, bk, wvT, bv, woT, bo, y):
    x_t, c_t, y_t = (a.rearrange("(n t) f -> n t f", t=P) for a in (x, cond, y))
    LAST = PAIRS - 1
    with ExitStack() as ctx:
        def sb(name, shape, dt=F32):
            return ctx.enter_context(nc.sbuf_tensor(f"b_{name}", shape, dt))

        def sem(name):
            return ctx.enter_context(nc.semaphore(f"b_{name}"))

        w_two = {n: sb(f"w{n}", [P, P]) for n in "qkvo"}
        bias = {n: sb(f"bias_{n}", [P, 1]) for n in "qkvo"}
        ident = sb("ident", [P, P])
        head_sum = sb("head_sum", [P, 2 * HALF - 1, BH])
        pick_f = sb("pick_f", [P, HALF, P])
        pick = sb("pick", [P, HALF, P], F32R)
        pow_half, eps = sb("pow_half", [P, 1]), sb("eps", [P, 1])
        carrier = sb("carrier", [P, 1])
        xin, cin, cin_v, xres = (sb(n, [P, DIM]) for n in ("xin", "cin", "cin_v", "xres"))
        stats, mv = sb("stats", [P, 6]), sb("mv", [P, 2])
        veps, rstd = sb("veps", [P, 1]), sb("rstd", [P, 1])
        xln, q = sb("xln", [P, DIM]), sb("q", [P, DIM])
        kpad, vpad = sb("kpad", [P, DIM + WIN]), sb("vpad", [P, DIM + WIN])
        prod = sb("prod", [P, WIN, DIM])
        dots = sb("dots", [P, 2, DIM])
        prob = sb("prob", [P, 2, 2, WIN, BH])
        mx, sm, rs = (sb(n, [P, 2, 2, BH]) for n in ("mx", "sm", "rs"))
        probT = [sb(f"probT_{part}", [P, 2, DIM], F32R) for part in ("hi", "lo")]
        pv = sb("pv", [P, WIN, DIM])
        yo = sb("yo", [P, DIM])

        dots_bank, spread_bank, y_bank = psum[0:2], psum[2:4], psum[4]
        work = Banks(nc, ctx, "b_work", psum[5:8],
                     {"T0": 0, "T1": 1, "Q": 2, "K": 0, "V": 1, "R0": 2, "R1": 0}, ["Q", "K"], LAST)

        w_zeroed, w_loaded, bias_loaded = sem("w_zeroed"), sem("w_loaded"), sem("bias_loaded")
        const_step, const_ready, pad_zeroed = sem("const_step"), sem("const_ready"), sem("pad_zeroed")
        pow_ready = sem("pow_ready")
        x_loaded, c_loaded, cv_loaded, res_loaded = sem("x_loaded"), sem("c_loaded"), sem("cv_loaded"), sem("res_loaded")
        stats_done, aggr_done, veps_done, rstd_done = sem("stats_done"), sem("aggr_done"), sem("veps_done"), sem("rstd_done")
        xln_ready = sem("xln_ready")
        prod_dve, prod_pool = sem("prod_dve"), sem("prod_pool")
        summed = sem("summed")
        dots_out = [sem(f"dots_out{h}") for h in range(2)]
        mx_ready, exp_done, sum_done, rs_ready, prob_ready = (
            sem(n) for n in ("mx_ready", "exp_done", "sum_done", "rs_ready", "prob_ready"))
        phi_ready = sem("phi_ready")
        spread_full = [sem(f"spread_full{i}") for i in range(2)]
        pv_ready = [sem(f"pv_ready{i}") for i in range(2)]
        pairs_added, fours_added = sem("pairs_added"), sem("fours_added")
        y_full, y_ready, y_stored = sem("y_full"), sem("y_ready"), sem("y_stored")

        def at_most(m, n):
            return not isinstance(m, int) or m <= n

        block = ctx.enter_context(nc.Block())

        @block.sync
        def _(sp):
            sp.dma_start(xin[:], x_t[0]).then_inc(x_loaded, 16)
            sp.dma_start(cin[:], c_t[0]).then_inc(c_loaded, 16)
            sp.dma_start(cin_v[:], c_t[0]).then_inc(cv_loaded, 16)
            sp.wait_ge(w_zeroed, 4)
            for n, src in zip("qkvo", (wqT, wkT, wvT, woT)):
                for b in range(2):
                    part = slice(b * SEQ, (b + 1) * SEQ)
                    sp.dma_start(w_two[n][part, part], src).then_inc(w_loaded, 16)
            for n, src in zip("qkvo", (bq, bk, bv, bo)):
                for b in range(2):
                    sp.dma_start(bias[n][b * SEQ:(b + 1) * SEQ, :], src).then_inc(bias_loaded, 16)
            sp.dma_start(xres[:], x_t[0]).then_inc(res_loaded, 16)

            def more_input(i):
                if at_most(i, LAST - 3):
                    wait(sp, xln_ready, i + 3)
                    sp.dma_start(xin[:], x_t[i + 3]).then_inc(x_loaded, 16)
                    work.wait_full(sp, "K", i + 2)
                    sp.dma_start(cin[:], c_t[i + 3]).then_inc(c_loaded, 16)
                if at_most(i, LAST - 2):
                    work.wait_full(sp, "V", i + 1)
                    sp.dma_start(cin_v[:], c_t[i + 2]).then_inc(cv_loaded, 16)

            for i in range(-2, 0):
                if i == -2:
                    wait(sp, xln_ready, 1)
                    sp.dma_start(xin[:], x_t[1]).then_inc(x_loaded, 16)
                    work.wait_full(sp, "K", 0)
                    sp.dma_start(cin[:], c_t[1]).then_inc(c_loaded, 16)
                else:
                    more_input(i)

            def slot(i):
                more_input(i)
                wait(sp, y_ready, i + 1)
                sp.dma_start(y_t[i], yo[:]).then_inc(y_stored, 16)
                if at_most(i, LAST - 1):
                    sp.dma_start(xres[:], x_t[i + 1]).then_inc(res_loaded, 16)

            steps(sp, slot, LAST - 3, LAST)
            sp.wait_ge(y_stored, 16 * PAIRS)

        def add_norm_pool(pool, m):
            wait(pool, aggr_done, m + 1)
            pool.tensor_tensor(veps[:], mv[:, 1:2], eps[:], ALU.add).then_inc(veps_done, 1)
            wait(pool, veps_done, m + 1)
            pool.tensor_tensor(rstd[:], veps[:], pow_half[:], ALU.pow).then_inc(rstd_done, 1)

        def product(eng, m, w, done):
            if w < 2:
                work.wait_read(eng, "Q", m)
                work.wait_read(eng, "K", m)
                eng.wait_ge(pad_zeroed, 2)
            if not (isinstance(m, int) and m == 0):
                wait(eng, summed, WIN * m - WIN + w + 1)
            eng.tensor_tensor(prod[:, w, :], q[:], kpad[:, w:w + DIM], ALU.mult).then_inc(done, 1)

        @block.gpsimd
        def _(pool):
            for n in "qkvo":
                pool.memset(w_two[n][:], 0.0).then_inc(w_zeroed, 1)
            pool.memset(pow_half[:], -0.5).then_inc(pow_ready, 1)
            pool.memset(eps[:], LN_EPS).then_inc(pow_ready, 1)
            pool.memset(ident[:], 0.0).then_inc(const_step, 1)
            pool.memset(head_sum[:], 0.0).then_inc(const_step, 1)
            pool.memset(pick_f[:], 0.0).then_inc(const_step, 1)
            pool.wait_ge(const_step, 3)
            pool.memset(head_sum[:, HALF - 1, :], 1.0).then_inc(const_step, 1)
            pool.wait_ge(const_step, 4)
            pool.wait_ge(pow_ready, 2)
            add_norm_pool(pool, 0)
            pool.affine_select(out=ident[:], in_=ident[:], compare_op=ALU.not_equal, fill=1.0, base=0,
                               pattern=[[-1, P]], channel_multiplier=1).then_inc(const_step, 1)
            mid = head_sum[:, HALF - 1, :]
            pool.affine_select(out=mid, in_=mid, compare_op=ALU.is_ge, fill=0.0, base=0,
                               pattern=[[-XHD, BH]], channel_multiplier=1).then_inc(const_step, 1)
            pool.wait_ge(const_step, 6)
            pool.affine_select(out=mid, in_=mid, compare_op=ALU.is_ge, fill=0.0, base=XHD - 1,
                               pattern=[[XHD, BH]], channel_multiplier=-1).then_inc(const_step, 1)
            sel = pick_f[:].rearrange("p w (h d) -> p w h d", d=XHD)
            pool.affine_select(out=sel, in_=sel, compare_op=ALU.not_equal, fill=1.0, base=0,
                               pattern=[[-BH, HALF], [-1, BH], [0, XHD]], channel_multiplier=1).then_inc(const_step, 1)
            pool.wait_ge(const_step, 8)
            pool.tensor_copy(pick[:], pick_f[:]).then_inc(const_ready, 1)
            add_norm_pool(pool, 1)
            for w in range(1, WIN, 2):
                product(pool, 0, w, prod_pool)

            def normalise(m):
                for a in range(2):
                    wait(pool, rs_ready, 2 * m + a + 1)
                    pool.tensor_tensor(prob[:, a], prob[:, a],
                                       rs[:, a].unsqueeze(2).to_broadcast([P, 2, WIN, BH]), ALU.mult)\
                        .then_inc(prob_ready, 1)

            def slot(i):
                for w in range(1, WIN, 2):
                    if at_most(i, LAST - 1):
                        product(pool, i + 1, w, prod_pool)
                    for par in range(2):
                        wait(pool, pv_ready[par], 8 * i + w // 2 + 1)
                    pool.tensor_tensor(pv[:, w - 1, :], pv[:, w - 1, :], pv[:, w, :], ALU.add).then_inc(pairs_added, 1)
                    if w == 1 and at_most(i, LAST - 2):
                        add_norm_pool(pool, i + 2)
                if at_most(i, LAST - 1):
                    normalise(i + 1)

            normalise(0)
            steps(pool, slot, LAST - 2, LAST)

        @block.scalar
        def _(act):
            act.wait_ge(bias_loaded, 128)
            act.wait_ge(pad_zeroed, 2)

            def q_out(m):
                work.wait_full(act, "Q", m)
                wait(act, prod_dve, 8 * m)
                wait(act, prod_pool, 8 * m)
                act.activation(q[:], work.tile("Q")[:], ACT.Identity, bias=bias["q"][:, 0:1])\
                   .then_inc(work.freed_sem("Q"), 1)

            def k_out(m):
                work.wait_full(act, "K", m)
                act.activation(kpad[:, PADL:PADL + DIM], work.tile("K")[:], ACT.Identity, bias=bias["k"][:, 0:1])\
                   .then_inc(work.freed_sem("K"), 1)

            def v_out(m):
                work.wait_full(act, "V", m)
                for par in range(2):
                    wait(act, pv_ready[par], 8 * m)
                act.activation(vpad[:, PADL:PADL + DIM], work.tile("V")[:], ACT.Identity, bias=bias["v"][:, 0:1])\
                   .then_inc(work.freed_sem("V"), 1)

            def dots_to_sbuf(m):
                for h in range(2):
                    wait(act, summed, WIN * m + HALF * (h + 1))
                    act.activation(dots[:, h, :], dots_bank[h][:], ACT.Copy).then_inc(dots_out[h], 1)

            def exp(m):
                for a in range(2):
                    work.wait_read(act, f"T{a}", m)
                    act.activation(prob[:, a], prob[:, a], ACT.Exp, scale=XHD ** -0.5).then_inc(exp_done, 1)

            def prob_hi(m):
                for h in range(2):
                    work.wait_full(act, f"R{h}", m)
                    act.activation(probT[0][:, h, :], work.tile(f"R{h}")[:], ACT.Copy).then_inc(phi_ready, 1)

            q_out(0)
            k_out(0)

            def slot(i):
                if at_most(i, LAST - 1):
                    dots_to_sbuf(i + 1)
                    exp(i + 1)
                if at_most(i, LAST - 2):
                    q_out(i + 2)
                    k_out(i + 2)
                if at_most(i, LAST - 1):
                    v_out(i + 1)
                    prob_hi(i + 1)

            slot(-1)
            steps(act, slot, LAST - 2, LAST)

        @block.vector
        def _(dve):
            dve.memset(kpad[:], 0.0).then_inc(pad_zeroed, 1)
            dve.memset(vpad[:], 0.0).then_inc(pad_zeroed, 1)

            def layernorm(m):
                wait(dve, x_loaded, 16 * m + 16)
                dve.bn_stats(stats[:], xin[:]).then_inc(stats_done, 1)
                wait(dve, stats_done, m + 1)
                dve.memset(carrier[:], 0.0)
                dve.bn_aggr(mv[:], stats[:]).then_inc(aggr_done, 1)

            def apply_norm(m):
                wait(dve, rstd_done, m + 1)
                if not (isinstance(m, int) and m == 0):
                    work.wait_full(dve, "Q", m - 1)
                dve.tensor_scalar(xln[:], xin[:], mv[:, 0:1], rstd[:, 0:1], ALU.subtract, ALU.mult)\
                   .then_inc(xln_ready, 1)

            def softmax(m):
                for a in range(2):
                    u = f"T{a}"
                    work.wait_full(dve, u, m)
                    s = work.tile(u)[:].rearrange("p (t w b) -> p t w b", t=2, w=WIN)
                    dve.tensor_reduce(mx[:, a], s.transpose([0, 1, 3, 2]), AX_X, ALU.max).then_inc(mx_ready, 1)
                    wait(dve, mx_ready, 2 * m + a + 1)
                    dve.tensor_tensor(prob[:, a], s, mx[:, a].unsqueeze(2).to_broadcast([P, 2, WIN, BH]), ALU.subtract)\
                       .then_inc(work.freed_sem(u), 1)
                for a in range(2):
                    wait(dve, exp_done, 2 * m + a + 1)
                    dve.tensor_reduce(sm[:, a], prob[:, a].transpose([0, 1, 3, 2]), AX_X, ALU.add).then_inc(sum_done, 1)
                    wait(dve, sum_done, 2 * m + a + 1)
                    dve.reciprocal(rs[:, a], sm[:, a]).then_inc(rs_ready, 1)

            def prob_lo(m):
                for h in range(2):
                    u = f"R{h}"
                    wait(dve, phi_ready, 2 * m + h + 1)
                    dve.tensor_tensor(probT[1][:, h, :], work.tile(u)[:], probT[0][:, h, :].bitcast(F32),
                                      ALU.subtract).then_inc(work.freed_sem(u), 1)

            def weigh(i, w):
                wait(dve, spread_full[w % 2], 8 * i + w // 2 + 1)
                if w == 0:
                    work.wait_read(dve, "V", i)
                dve.tensor_tensor(pv[:, w, :], spread_bank[w % 2][:], vpad[:, w:w + DIM], ALU.mult)\
                   .then_inc(pv_ready[w % 2], 1)

            def add_fours(i, j):
                wait(dve, pairs_added, 8 * i + 2 * j + 2)
                dve.tensor_tensor(pv[:, 4 * j, :], pv[:, 4 * j, :], pv[:, 4 * j + 2, :], ALU.add).then_inc(fours_added, 1)

            def y_out(i):
                wait(dve, y_full, i + 1)
                wait(dve, res_loaded, 16 * i + 16)
                wait(dve, y_stored, 16 * i)
                dve.scalar_tensor_tensor(yo[:], y_bank[:], bias["o"][:, 0:1], xres[:], ALU.add, ALU.add)\
                   .then_inc(y_ready, 1)

            layernorm(0)
            apply_norm(0)
            layernorm(1)
            apply_norm(1)
            for w in range(0, WIN, 2):
                product(dve, 0, w, prod_dve)
            softmax(0)
            prob_lo(0)
            dve.wait_ge(bias_loaded, 128)

            def slot(i):
                for w in range(WIN):
                    if w % 2 == 0 and at_most(i, LAST - 1):
                        product(dve, i + 1, w, prod_dve)
                    weigh(i, w)
                    if w == 1 and at_most(i, LAST - 2):
                        layernorm(i + 2)
                    if w == 5 and at_most(i, LAST - 2):
                        apply_norm(i + 2)
                    if w >= 6 and w % 4 == 2:
                        add_fours(i, (w - 6) // 4)
                if at_most(i, LAST - 1):
                    softmax(i + 1)
                add_fours(i, 3)
                if at_most(i, LAST - 1):
                    prob_lo(i + 1)
                y_out(i)

            steps(dve, slot, LAST - 2, LAST)

        @block.tensor
        def _(pe):
            def pointwise(m, u, rhs):
                work.wait_free(pe, u, m)
                pe.matmul(work.tile(u)[:], w_two[u.lower()][:], rhs[:], start=True, stop=True)\
                  .then_inc(work.full_sem(u), 1)

            def query_key(m):
                wait(pe, xln_ready, m + 1)
                pointwise(m, "Q", xln)
                wait(pe, c_loaded, 16 * m + 16)
                pointwise(m, "K", cin)

            def value(m):
                wait(pe, cv_loaded, 16 * m + 16)
                pointwise(m, "V", cin_v)

            def head_sums(m, w):
                h, r = w // HALF, w % HALF
                if r == 0:
                    wait(pe, dots_out[h], m)
                done = prod_pool if w % 2 else prod_dve
                wait(pe, done, 8 * m + w // 2 + 1)
                pe.matmul(dots_bank[h][:], head_sum[:, HALF - 1 - r:2 * HALF - 1 - r, :], prod[:, w, :],
                          start=r == 0, stop=r == HALF - 1).then_inc(summed, 1)

            def turn(m):
                for h in range(2):
                    wait(pe, dots_out[h], m + 1)
                for a in range(2):
                    u = f"T{a}"
                    work.wait_free(pe, u, m)
                    for t in range(2):
                        for h in range(2):
                            ins = pe.transpose(work.tile(u)[:, (2 * t + h) * P:(2 * t + h + 1) * P],
                                               dots[:, h, (2 * a + t) * P:(2 * a + t + 1) * P], ident[:])
                    ins.then_inc(work.full_sem(u), 1)

            def turn_back(m):
                wait(pe, prob_ready, 2 * m + 2)
                for h in range(2):
                    u = f"R{h}"
                    work.wait_free(pe, u, m)
                    for a in range(2):
                        for t in range(2):
                            ins = pe.transpose(work.tile(u)[:, (2 * a + t) * P:(2 * a + t + 1) * P],
                                               prob[:, a, t, h * HALF:(h + 1) * HALF, :], ident[:])
                    ins.then_inc(work.full_sem(u), 1)

            def spread(i, w):
                h, r = w // HALF, w % HALF
                if r == 0:
                    work.wait_read(pe, f"R{h}", i)
                wait(pe, pv_ready[w % 2], 8 * i + w // 2)
                pe.matmul(spread_bank[w % 2][:], pick[:, r, :], probT[0][:, h, :], start=True, stop=False)
                pe.matmul(spread_bank[w % 2][:], pick[:, r, :], probT[1][:, h, :], start=False, stop=True)\
                  .then_inc(spread_full[w % 2], 1)

            def project(i, j):
                wait(pe, fours_added, 4 * i + j + 1)
                if j == 0:
                    wait(pe, y_ready, i)
                ins = pe.matmul(y_bank[:], w_two["o"][:], pv[:, 4 * j, :], start=j == 0, stop=j == 3)
                if j == 3:
                    ins.then_inc(y_full, 1)

            pe.wait_ge(w_loaded, 128)
            query_key(0)
            pe.wait_ge(const_step, 8)
            for w in range(WIN):
                head_sums(0, w)
            turn(0)
            query_key(1)
            value(0)
            pe.wait_ge(const_ready, 1)
            turn_back(0)

            def slot(i):
                for w in range(WIN):
                    spread(i, w)
                    if at_most(i, LAST - 1):
                        head_sums(i + 1, w)
                    if w >= 8 and w % 4 == 0:
                        project(i, (w - 8) // 4)
                if at_most(i, LAST - 1):
                    turn(i + 1)
                project(i, 2)
                if at_most(i, LAST - 2):
                    query_key(i + 2)
                if at_most(i, LAST - 1):
                    value(i + 1)
                project(i, 3)
                if at_most(i, LAST - 1):
                    turn_back(i + 1)

            steps(pe, slot, LAST - 2, LAST)


def expert_phase(nc, psum, x, gate, up, down, fc1T, expertT, fc2, gamma, beta, y):
    x_d = x.rearrange("(d p t) f -> d t p f", p=2, t=P)
    y_t = y.rearrange("(n t) f -> n t f", t=P)
    with ExitStack() as ctx:
        def sb(name, shape, dt=F32):
            return ctx.enter_context(nc.sbuf_tensor(f"c_{name}", shape, dt))

        def sem(name):
            return ctx.enter_context(nc.semaphore(f"c_{name}"))

        PARTS = ("hi", "lo")
        up_w = [sb(f"up_{s}", [P, KC, INT], F32R) for s in PARTS]
        down_w = [sb(f"down_{s}", [P, IC, DIM], F32R) for s in PARTS]
        gate_w = [sb(f"gate_{s}", [P, KC, NE], F32R) for s in PARTS]
        lat_w = [sb(f"lat_{s}", [P, KC, DIM], F32R) for s in PARTS]
        HSTAGE = KC * INT // 2
        stage = [sb(f"stage{i}", [P, HSTAGE]) for i in range(3)]
        gate_f = sb("gate_f", [P, KC, NE])
        fc1_f, expert_f, fc2_f = sb("fc1_f", [P, LC, DIM]), sb("expert_f", [P, LC, LAT]), sb("fc2_f", [P, LC, DIM])
        tail_f = sb("tail_f", [P, LC, DIM])
        gamma_row, beta_row = sb("gamma_row", [P, DIM]), sb("beta_row", [P, DIM])
        ident, pow_half, eps = sb("ident", [P, P]), sb("pow_half", [P, 2]), sb("eps", [P, 2])
        carrier = sb("carrier", [P, 5])
        xin, xres, xln = (sb(n, [P, 2, DIM]) for n in ("xin", "xres", "xln"))
        stats, mv = sb("stats", [P, 2, 6]), sb("mv", [P, 2, 2])
        veps, rstd = sb("veps", [P, 2]), sb("rstd", [P, 2])
        xT = [sb(f"xT_{s}", [P, KC, 2 * P], F32R) for s in PARTS]
        relu = sb("relu", [P, 2, 2 * P])
        hidden = sb("hidden", [P, 2, 2 * P])
        hid = [sb(f"hid_{s}", [P, IC, 2 * P], F32R) for s in PARTS]
        top, route = sb("top", [P, 2, NE]), sb("route", [P, 2])
        routed, z = sb("routed", [P, 2, DIM]), sb("z", [P, 2, DIM])
        zstats, zmv = sb("zstats", [P, 2, 6]), sb("zmv", [P, 2, 2])
        zveps, zrstd = sb("zveps", [P, 2]), sb("zrstd", [P, 2])
        yo = sb("yo", [P, 2, DIM])

        bank_of = {f"H{c}": c % 4 for c in range(IC)}
        bank_of.update({"G0": 6, "R0": 4, "G1": 6, "R1": 5, "X0": 4, "X1": 5, "D0": 7, "D1": 6})
        work = Banks(nc, ctx, "c_work", psum, bank_of, ["X0", "X1"], DUOS - 1)

        const_step, pow_ready = sem("const_step"), sem("pow_ready")
        small_loaded, row_loaded = sem("small_loaded"), sem("row_loaded")
        stage_loaded = [sem(f"stage_loaded{i}") for i in range(3)]
        w_hi, w_lo = sem("w_hi"), sem("w_lo")
        tail_full, tail_out, lat_full = sem("tail_full"), sem("tail_out"), sem("lat_full")
        lat_hi, lat_lo = sem("lat_hi"), sem("lat_lo")
        x_loaded, res_loaded = sem("x_loaded"), [sem(f"res_loaded{p}") for p in range(2)]
        res_biased = [sem(f"res_biased{p}") for p in range(2)]
        stats_done, aggr_done, veps_done, rstd_done = sem("stats_done"), sem("aggr_done"), sem("veps_done"), sem("rstd_done")
        xln_ready, xhi_ready = sem("xln_ready"), sem("xhi_ready")
        relu_done = sem("relu_done")
        hhi_ready, hlo_ready = sem("hhi_ready"), sem("hlo_ready")
        route_ready = sem("route_ready")
        zstats_done, zaggr_done, zveps_done, zrstd_done = sem("zstats_done"), sem("zaggr_done"), sem("zveps_done"), sem("zrstd_done")
        z_norm, z_scaled = sem("z_norm"), sem("z_scaled")
        y_ready, y_stored = [sem(f"y_ready{p}") for p in range(2)], [sem(f"y_stored{p}") for p in range(2)]

        def halves(w):
            flat = [part[:].rearrange("p k n -> p (k n)") for part in w]
            return [[part[:, h * HSTAGE:(h + 1) * HSTAGE] for part in flat] for h in range(2)]

        up_src = up.rearrange("(k p) n -> p k n", p=P)
        down_src = down.rearrange("(k p) n -> p k n", p=P)
        loads = ([(dst, up_src[:, h * KC // 2:(h + 1) * KC // 2, :]) for h, dst in enumerate(halves(up_w))]
                 + [(dst, down_src[:, h * IC // 2:(h + 1) * IC // 2, :]) for h, dst in enumerate(halves(down_w))])

        block = ctx.enter_context(nc.Block())

        @block.sync
        def _(sp):
            sp.dma_start(xin[:], x_d[0]).then_inc(x_loaded, 16)
            sp.dma_start(expert_f[:], expertT.rearrange("(k p) n -> p k n", p=P)).then_inc(small_loaded, 16)
            sp.dma_start(fc2_f[:], fc2.rearrange("(k p) n -> p k n", p=P)).then_inc(small_loaded, 16)
            sp.dma_start(fc1_f[:], fc1T.rearrange("(k p) n -> p k n", p=P)).then_inc(small_loaded, 16)
            sp.dma_start(gate_f[:], gate.rearrange("(k p) n -> p k n", p=P)).then_inc(small_loaded, 16)
            for n, (_, src) in enumerate(loads):
                if n >= 3:
                    wait(sp, w_lo, n - 3 + 2)
                sp.dma_start(stage[n % 3][:].rearrange("p (k n) -> p k n", n=src.shape[2]), src)\
                  .then_inc(stage_loaded[n % 3], 16)
            sp.dma_start(gamma_row[:], gamma.partition_broadcast(P)).then_inc(row_loaded, 16)
            sp.dma_start(beta_row[:], beta.partition_broadcast(P)).then_inc(row_loaded, 16)
            wait(sp, xln_ready, 2)
            sp.dma_start(xin[:], x_d[1]).then_inc(x_loaded, 16)
            for p in range(2):
                sp.dma_start(xres[:, p, :], x_d[0][:, p, :]).then_inc(res_loaded[p], 16)

            def slot(d):
                if not isinstance(d, int) or d < DUOS - 2:
                    wait(sp, xln_ready, 2 * d + 4)
                    sp.dma_start(xin[:], x_d[d + 2]).then_inc(x_loaded, 16)
                for p in range(2):
                    wait(sp, y_ready[p], d + 1)
                    sp.dma_start(y_t[d * 2 + p], yo[:, p, :]).then_inc(y_stored[p], 16)
                    if not isinstance(d, int) or d < DUOS - 1:
                        sp.dma_start(xres[:, p, :], x_d[d + 1][:, p, :]).then_inc(res_loaded[p], 16)

            steps(sp, slot, DUOS - 3, DUOS - 1)
            for p in range(2):
                sp.wait_ge(y_stored[p], 16 * DUOS)

        @block.gpsimd
        def _(pool):
            pool.memset(pow_half[:], -0.5).then_inc(pow_ready, 1)
            pool.memset(eps[:], LN_EPS).then_inc(pow_ready, 1)
            pool.memset(ident[:], 0.0).then_inc(const_step, 1)
            pool.wait_ge(const_step, 1)
            pool.affine_select(out=ident[:], in_=ident[:], compare_op=ALU.not_equal, fill=1.0, base=0,
                               pattern=[[-1, P]], channel_multiplier=1).then_inc(const_step, 1)

            def rstd_of(m):
                wait(pool, aggr_done, 2 * m + 2)
                pool.tensor_tensor(veps[:], mv[:, :, 1], eps[:], ALU.add).then_inc(veps_done, 1)
                wait(pool, veps_done, m + 1)
                pool.tensor_tensor(rstd[:], veps[:], pow_half[:], ALU.pow).then_inc(rstd_done, 1)

            def hidden_lo(m, c):
                wait(pool, hhi_ready, 8 * m + c + 1)
                pool.tensor_tensor(hid[1][:, c, :], hidden[:, c % 2, :], hid[0][:, c, :].bitcast(F32), ALU.subtract)\
                    .then_inc(hlo_ready, 1)

            def bias_residual(m, p):
                wait(pool, res_loaded[p], 16 * m + 16)
                wait(pool, row_loaded, 32)
                pool.tensor_tensor(xres[:, p, :], xres[:, p, :], beta_row[:], ALU.add).then_inc(res_biased[p], 1)

            def z_rstd(m, p):
                wait(pool, zaggr_done, 2 * m + p + 1)
                pool.tensor_tensor(zveps[:, p:p + 1], zmv[:, p, 1:2], eps[:, 0:1], ALU.add).then_inc(zveps_done, 1)
                wait(pool, zveps_done, 2 * m + p + 1)
                pool.tensor_tensor(zrstd[:, p:p + 1], zveps[:, p:p + 1], pow_half[:, 0:1], ALU.pow).then_inc(zrstd_done, 1)

            def z_gamma(m, p):
                wait(pool, z_norm, 2 * m + p + 1)
                pool.tensor_tensor(z[:, p, :], z[:, p, :], gamma_row[:], ALU.mult).then_inc(z_scaled, 1)

            pool.wait_ge(pow_ready, 2)
            rstd_of(0)

            def slot(d):
                for c in range(IC):
                    hidden_lo(d, c)
                for p in range(2):
                    bias_residual(d, p)
                if not isinstance(d, int) or d < DUOS - 1:
                    rstd_of(d + 1)
                for p in range(2):
                    z_rstd(d, p)
                    z_gamma(d, p)

            steps(pool, slot, DUOS - 2, DUOS - 1)

        @block.scalar
        def _(act):
            def tail_to_sbuf():
                for c in range(LC):
                    wait(act, tail_full, c + 1)
                    act.activation(tail_f[:, c, :], psum[c][:], ACT.Copy).then_inc(tail_out, 1)

            def lat_high():
                for c in range(KC):
                    wait(act, lat_full, c + 1)
                    act.activation(lat_w[0][:, c, :], psum[c][:], ACT.Copy).then_inc(lat_hi, 1)

            def x_hi(m, p):
                work.wait_full(act, f"X{p}", m)
                act.activation(xT[0][:, :, p * P:(p + 1) * P], work.tile(f"X{p}")[:].rearrange("p (k t) -> p k t", k=KC),
                               ACT.Copy).then_inc(xhi_ready, 1)

            act.wait_ge(small_loaded, 64)
            act.activation(gate_w[0][:], gate_f[:], ACT.Copy).then_inc(w_hi, 1)
            tail_to_sbuf()
            lat_high()
            for p in range(2):
                x_hi(0, p)
            for n, (dst, _) in enumerate(loads):
                wait(act, stage_loaded[n % 3], 16 * (n // 3) + 16)
                act.activation(dst[0], stage[n % 3][:], ACT.Copy).then_inc(w_hi, 1)

            def relu_out(m, c):
                work.wait_full(act, f"H{c}", m)
                act.activation(relu[:, c % 2, :], work.tile(f"H{c}")[:, 0:2 * P], ACT.Relu).then_inc(relu_done, 1)

            def hidden_hi(m, c):
                work.wait_read(act, f"H{c}", m)
                act.activation(hid[0][:, c, :], hidden[:, c % 2, :], ACT.Copy).then_inc(hhi_ready, 1)

            def routed_out(m, p):
                work.wait_full(act, f"R{p}", m)
                wait(act, route_ready, 2 * m + p + 1)
                act.activation(routed[:, p, :], work.tile(f"R{p}")[:], ACT.Copy, scale=route[:, p:p + 1])\
                   .then_inc(work.freed_sem(f"R{p}"), 1)

            def slot(d):
                relu_out(d, 0)
                for c in range(1, IC):
                    relu_out(d, c)
                    hidden_hi(d, c - 1)
                hidden_hi(d, IC - 1)
                for p in range(2):
                    routed_out(d, p)
                if not isinstance(d, int) or d < DUOS - 1:
                    for p in range(2):
                        x_hi(d + 1, p)

            steps(act, slot, DUOS - 2, DUOS - 1)

        @block.vector
        def _(dve):
            def layernorm(m):
                wait(dve, x_loaded, 16 * m + 16)
                for p in range(2):
                    dve.bn_stats(stats[:, p, :], xin[:, p, :]).then_inc(stats_done, 1)
                wait(dve, stats_done, 2 * m + 2)
                dve.memset(carrier[:, 0:1], 0.0)
                for p in range(2):
                    dve.bn_aggr(mv[:, p, :], stats[:, p, :]).then_inc(aggr_done, 1)

            def apply_norm(m):
                wait(dve, rstd_done, m + 1)
                wait(dve, xhi_ready, 2 * m)
                for p in range(2):
                    dve.tensor_scalar(xln[:, p, :], xin[:, p, :], mv[:, p, 0:1], rstd[:, p:p + 1],
                                      ALU.subtract, ALU.mult).then_inc(xln_ready, 1)

            def x_lo(m, p):
                wait(dve, xhi_ready, 2 * m + p + 1)
                dve.tensor_tensor(xT[1][:, :, p * P:(p + 1) * P], work.tile(f"X{p}")[:].rearrange("p (k t) -> p k t", k=KC),
                                  xT[0][:, :, p * P:(p + 1) * P].bitcast(F32), ALU.subtract)\
                   .then_inc(work.freed_sem(f"X{p}"), 1)

            layernorm(0)
            wait(dve, w_hi, 1)
            dve.tensor_tensor(gate_w[1][:], gate_f[:], gate_w[0][:].bitcast(F32), ALU.subtract).then_inc(w_lo, 1)
            apply_norm(0)
            for c in range(KC):
                wait(dve, lat_hi, c + 1)
                dve.tensor_tensor(lat_w[1][:, c, :], psum[c][:], lat_w[0][:, c, :].bitcast(F32), ALU.subtract)\
                   .then_inc(lat_lo, 1)
            for p in range(2):
                x_lo(0, p)
            for n, (dst, _) in enumerate(loads):
                wait(dve, w_hi, n + 2)
                dve.tensor_tensor(dst[1], stage[n % 3][:], dst[0].bitcast(F32), ALU.subtract).then_inc(w_lo, 1)

            def square(m, c):
                u = f"H{c}"
                wait(dve, relu_done, 8 * m + c + 1)
                if c >= 2:
                    wait(dve, hlo_ready, 8 * m + c - 1)
                dve.scalar_tensor_tensor(hidden[:, c % 2, :], work.tile(u)[:, 0:2 * P], 0.0, relu[:, c % 2, :],
                                         ALU.max, ALU.mult).then_inc(work.freed_sem(u), 1)

            def gate_top(m, p):
                u = f"G{p}"
                work.wait_full(dve, u, m)
                dve.memset(carrier[:, 3 + p:4 + p], 0.0)
                dve.max(top[:, p, :], work.tile(u)[:, 0:NE]).then_inc(work.freed_sem(u), 1)
                work.wait_read(dve, u, m)
                dve.tensor_tensor(route[:, p:p + 1], top[:, p, 0:1], top[:, p, 1:2], ALU.add).then_inc(route_ready, 1)

            def sum_out(m, p):
                u = f"D{p}"
                work.wait_full(dve, u, m)
                work.wait_read(dve, f"R{p}", m)
                dve.tensor_tensor(z[:, p, :], work.tile(u)[:], routed[:, p, :], ALU.add).then_inc(work.freed_sem(u), 1)
                work.wait_read(dve, u, m)
                dve.bn_stats(zstats[:, p, :], z[:, p, :]).then_inc(zstats_done, 1)
                wait(dve, zstats_done, 2 * m + p + 1)
                dve.memset(carrier[:, 1 + p:2 + p], 0.0)
                dve.bn_aggr(zmv[:, p, :], zstats[:, p, :]).then_inc(zaggr_done, 1)
                wait(dve, zrstd_done, 2 * m + p + 1)
                dve.tensor_scalar(z[:, p, :], z[:, p, :], zmv[:, p, 0:1], zrstd[:, p:p + 1],
                                  ALU.subtract, ALU.mult).then_inc(z_norm, 1)

            def y_out(m, p):
                wait(dve, z_scaled, 2 * m + p + 1)
                wait(dve, res_biased[p], m + 1)
                wait(dve, y_stored[p], 16 * m)
                dve.tensor_tensor(yo[:, p, :], z[:, p, :], xres[:, p, :], ALU.add).then_inc(y_ready[p], 1)

            def slot(d):
                more = not isinstance(d, int) or d < DUOS - 1
                for c in range(IC):
                    square(d, c)
                for p in range(2):
                    gate_top(d, p)
                if more:
                    layernorm(d + 1)
                    apply_norm(d + 1)
                    for p in range(2):
                        x_lo(d + 1, p)
                for p in range(2):
                    sum_out(d, p)
                for p in range(2):
                    y_out(d, p)

            steps(dve, slot, DUOS - 2, DUOS - 1)

        @block.tensor
        def _(pe):
            def x_transposes(m, p):
                u = f"X{p}"
                wait(pe, xln_ready, 2 * m + p + 1)
                work.wait_free(pe, u, m)
                for c in range(KC):
                    ins = pe.transpose(work.tile(u)[:, c * P:(c + 1) * P], xln[:, p, c * P:(c + 1) * P], ident[:])
                ins.then_inc(work.full_sem(u), 1)

            def up_chunk(m, c):
                u = f"H{c}"
                work.wait_free(pe, u, m)
                if c == 0:
                    for p in range(2):
                        work.wait_read(pe, f"X{p}", m)
                split3(pe, work.tile(u)[:, 0:2 * P], lambda a, k: up_w[a][:, k, c * P:(c + 1) * P],
                       lambda b, k: xT[b][:, k, :], KC).then_inc(work.full_sem(u), 1)

            def from_tokens(m, p, u, w, n, left, chunks):
                work.wait_free(pe, u, m)
                split3(pe, work.tile(u)[:, 0:n], lambda a, k: left[a][:, k, p * P:(p + 1) * P],
                       lambda b, k: w[b][:, k, :], chunks).then_inc(work.full_sem(u), 1)

            pe.wait_ge(small_loaded, 64)
            for c in range(LC):
                for k in range(LC):
                    ins = pe.matmul(psum[c][:], expert_f[:, k, c * P:(c + 1) * P], fc2_f[:, k, :],
                                    start=k == 0, stop=k == LC - 1)
                ins.then_inc(tail_full, 1)
            pe.wait_ge(tail_out, LC)
            for c in range(KC):
                for k in range(LC):
                    ins = pe.matmul(psum[c][:], fc1_f[:, k, c * P:(c + 1) * P], tail_f[:, k, :],
                                    start=k == 0, stop=k == LC - 1)
                ins.then_inc(lat_full, 1)
            pe.wait_ge(const_step, 2)
            for p in range(2):
                x_transposes(0, p)
            pe.wait_ge(lat_lo, KC)
            pe.wait_ge(w_lo, 5)

            def slot(d):
                for c in range(IC):
                    up_chunk(d, c)
                for p in range(2):
                    from_tokens(d, p, f"G{p}", gate_w, NE, xT, KC)
                    from_tokens(d, p, f"R{p}", lat_w, DIM, xT, KC)
                if not isinstance(d, int) or d < DUOS - 1:
                    for p in range(2):
                        x_transposes(d + 1, p)
                for p in range(2):
                    if p == 0:
                        wait(pe, hlo_ready, 8 * d + IC)
                    from_tokens(d, p, f"D{p}", down_w, DIM, hid, IC)

            steps(pe, slot, DUOS - 2, DUOS - 1)


def decoder_layer(nc, x, ctx_4096, a_wqT, a_bq, a_wkT, a_bk, a_wvT, a_bv, a_woT, a_bo,
                  x_wqT, x_bq, x_wkT, x_bk, x_wvT, x_bv, x_woT, x_bo,
                  gate, up, down, fc1T, expertT, fc2, gamma, beta, out):
    after_attention = nc.dram_tensor("after_attention", [TOKENS, DIM], F32, kind="Internal").ap()
    after_window = nc.dram_tensor("after_window", [TOKENS, DIM], F32, kind="Internal").ap()
    with ExitStack() as ctx:
        psum = [ctx.enter_context(nc.psum_tensor(f"bank{b}", [P, 512], F32)) for b in range(8)]
        attention_phase(nc, psum, x, a_wqT, a_bq, a_wkT, a_bk, a_wvT, a_bv, a_woT, a_bo, after_attention)
        window_phase(nc, psum, after_attention, ctx_4096, x_wqT, x_bq, x_wkT, x_bk, x_wvT, x_bv, x_woT, x_bo,
                     after_window)
        expert_phase(nc, psum, after_window, gate, up, down, fc1T, expertT, fc2, gamma, beta, out)


def kernel(**inputs):
    import numpy as _np
    import concourse.bacc as _bacc
    from concourse import mybir as _mybir
    from concourse.bass_utils import run_bass_kernel_spmd as _run

    given = {n: _np.asarray(a) for n, a in inputs.items()}

    def turned(name):
        return _np.ascontiguousarray(given[name].T)

    laid = {
        "x": given["x"].reshape(TOKENS, DIM),
        "ctx_4096": given["ctx_4096"].reshape(TOKENS, DIM),
        "a_wqT": turned("L0_attn_Wq"), "a_bq": _np.ascontiguousarray(given["L0_attn_bq"].reshape(GROUPS, P).T),
        "a_wkT": turned("L0_attn_Wk"), "a_bk": _np.ascontiguousarray(given["L0_attn_bk"].reshape(GROUPS, P).T),
        "a_wvT": turned("L0_attn_Wv"), "a_bv": given["L0_attn_bv"],
        "a_woT": turned("L0_attn_Wo"), "a_bo": given["L0_attn_bo"],
        "x_wqT": turned("L0_xattn_Wq"), "x_bq": given["L0_xattn_bq"].reshape(SEQ, 1),
        "x_wkT": turned("L0_xattn_Wk"), "x_bk": given["L0_xattn_bk"].reshape(SEQ, 1),
        "x_wvT": turned("L0_xattn_Wv"), "x_bv": given["L0_xattn_bv"].reshape(SEQ, 1),
        "x_woT": turned("L0_xattn_Wo"), "x_bo": given["L0_xattn_bo"].reshape(SEQ, 1),
        "gate": given["L0_ffn_gate_w"], "up": given["L0_ffn_up_w"], "down": given["L0_ffn_down_w"],
        "fc1T": turned("L0_ffn_fc1_w"), "expertT": turned("L0_ffn_expert_w"), "fc2": given["L0_ffn_fc2_w"],
        "gamma": given["L0_ffn_ln_gamma"], "beta": given["L0_ffn_ln_beta"],
    }
    nc = _bacc.Bacc("TRN2", target_bir_lowering=False, num_devices=1)
    arrays, args = {}, []
    for name, a in laid.items():
        arrays[f"in_{name}"] = a
        args.append(nc.dram_tensor(f"in_{name}", a.shape, _mybir.dt.from_np(a.dtype), kind="ExternalInput").ap())
    args.append(nc.dram_tensor("out_rows", [TOKENS, DIM], F32, kind="ExternalOutput").ap())
    decoder_layer(nc, *args)
    r = _run(nc, [arrays], core_ids=[0])
    return r.results[0]["out_rows"].reshape(BATCH, SEQ, DIM)
```

```python
from contextlib import ExitStack

import concourse.bass as bass
from concourse import mybir

BATCH, SEQ, DIM = 32, 64, 512
P = 128
TOKENS = BATCH * SEQ
PAIRS = TOKENS // P
DUOS = PAIRS // 2
KC = DIM // P
HEADS, HD = 32, 16
GROUPS = HEADS * HD // P
GH = HEADS // GROUPS
XH, XHD, WIN = 8, 8, 16
PADL = WIN // 2
BH = 2 * XH
HALF = P // BH
INT, LAT, NE = 1024, 256, 8
IC, LC = INT // P, LAT // P
LN_EPS = 1e-5
MASKED = -1e30

F32 = mybir.dt.float32
F32R = mybir.dt.float32r
BF16 = mybir.dt.bfloat16
ALU = mybir.AluOpType
ACT = mybir.ActivationFunctionType
AX_X = mybir.AxisListType.X


def wait(eng, sem, value):
    if isinstance(value, int) and value <= 0:
        return
    eng.wait_ge(sem, value)


class Banks:

    def __init__(self, nc, ctx, name, tiles, slot, ahead, last):
        self.tiles, self.at, self.last = tiles, slot, last
        self.full = [ctx.enter_context(nc.semaphore(f"{name}_full{b}")) for b in range(len(tiles))]
        self.freed = [ctx.enter_context(nc.semaphore(f"{name}_freed{b}")) for b in range(len(tiles))]
        self.ahead = {u: ahead.get(u, 0) for u in slot}
        self.order = list(slot)

    def tile(self, unit):
        return self.tiles[self.at[unit]]

    def before(self, unit, m):
        shifts = [self.ahead[o] - self.ahead[unit] + (1 if self.order.index(o) < self.order.index(unit) else 0)
                  for o in self.order if self.at[o] == self.at[unit]]
        if isinstance(m, int):
            return sum(min(max(m + s, 0), self.last + 1) for s in shifts)
        return m * len(shifts) + sum(shifts)

    def wait_free(self, eng, unit, m):
        wait(eng, self.freed[self.at[unit]], self.before(unit, m))

    def wait_full(self, eng, unit, m):
        wait(eng, self.full[self.at[unit]], self.before(unit, m) + 1)

    def wait_read(self, eng, unit, m):
        wait(eng, self.freed[self.at[unit]], self.before(unit, m) + 1)

    def full_sem(self, unit):
        return self.full[self.at[unit]]

    def freed_sem(self, unit):
        return self.freed[self.at[unit]]


def steps(eng, slot, last_full, last, first=0, first_full=1):
    for d in range(first, first_full):
        slot(d)
    with eng.Fori(first_full, last_full + 1) as d:
        slot(d)
    for d in range(last_full + 1, last + 1):
        slot(d)


def split3(pe, out, lhs, rhs, chunks, start=True, stop=True):
    passes = [(a, b) for c in range(chunks) for a, b in ((0, 0), (0, 1), (1, 0))]
    last = None
    for n, (a, b) in enumerate(passes):
        c = n // 3
        last = pe.matmul(out, lhs(a, c), rhs(b, c), start=start and n == 0, stop=stop and n == len(passes) - 1)
    return last


def attention_phase(nc, psum, x, wqT, bq, wkT, bk, wvT, bv, woT, bo, y):
    x_d = x.rearrange("(d p t) f -> d t p f", p=2, t=P)
    y_t = y.rearrange("(n t) f -> n t f", t=P)
    with ExitStack() as ctx:
        def sb(name, shape, dt=F32):
            return ctx.enter_context(nc.sbuf_tensor(f"a_{name}", shape, dt))

        def sem(name):
            return ctx.enter_context(nc.semaphore(f"a_{name}"))

        w_hl = {n: [sb(f"w{n}_{part}", [P, KC, DIM], F32R) for part in ("hi", "lo")] for n in "kqvo"}
        stage = [sb(f"stage{i}", [P, KC, DIM]) for i in range(2)]
        bq_col, bk_col = sb("bq_col", [P, GROUPS]), sb("bk_col", [P, GROUPS])
        bv_row, bo_row = sb("bv_row", [P, DIM]), sb("bo_row", [P, DIM])
        ident, ident_b = sb("ident", [P, P]), sb("ident_b", [P, P], BF16)
        causal = sb("causal", [P, SEQ], BF16)
        head_of = sb("head_of", [P, GH])
        pow_half, eps = sb("pow_half", [P, 2]), sb("eps", [P, 2])
        carrier = sb("carrier", [P, 1])
        xin, xres = sb("xin", [P, 2, DIM]), sb("xres", [P, 2, DIM])
        stats, mv = sb("stats", [P, 2, 6]), sb("mv", [P, 2, 2])
        veps, rstd = sb("veps", [P, 2]), sb("rstd", [P, 2])
        xln = sb("xln", [P, 2, DIM])
        xT = [sb(f"xT_{part}", [P, KC, 2 * P], F32R) for part in ("hi", "lo")]
        kT = sb("kT", [P, GROUPS, 2 * P])
        qz = sb("qz", [P, 2, GROUPS, 4, SEQ])
        kbd = sb("kbd", [P, 2, GROUPS, 2, GH, SEQ])
        vbd = sb("vbd", [P, 2, 2, HEADS // 2, 2, HD])
        prob = sb("prob", [P, GROUPS, GH, SEQ])
        mx, sm, rs = (sb(n, [P, GROUPS, GH]) for n in ("mx", "sm", "rs"))
        probT = sb("probT", [P, GROUPS, 4, P])
        oT = [sb(f"oT_{part}", [P, GROUPS, P], F32R) for part in ("hi", "lo")]
        yo = sb("yo", [P, 2, DIM])

        score = psum[0:4]
        A_UNITS = ["X0", "X1", "K0", "K1", "K2", "K3", "Q0", "Q1", "Q2", "Q3", "V0", "V1"]
        ORDER = (["X0", "X1", "K0", "K1", "K2", "K3"] + [f"P0{g}" for g in range(4)] + ["O0"]
                 + ["Q0", "Q1", "Q2", "Q3", "Y0", "V0"] + [f"P1{g}" for g in range(4)] + ["O1", "V1", "Y1"])
        work = Banks(nc, ctx, "a_work", psum[4:8], {u: n % 4 for n, u in enumerate(ORDER)}, {u: 1 for u in A_UNITS}, DUOS - 1)

        w_loaded = [sem(f"w_loaded{i}") for i in range(2)]
        w_hi, w_lo = sem("w_hi"), sem("w_lo")
        bias_loaded, bias_scaled = sem("bias_loaded"), sem("bias_scaled")
        const_step, const_ready = sem("const_step"), sem("const_ready")
        zeros_ready, pow_ready = sem("zeros_ready"), sem("pow_ready")
        x_loaded, res_loaded = sem("x_loaded"), [sem(f"res_loaded{p}") for p in range(2)]
        res_biased = [sem(f"res_biased{p}") for p in range(2)]
        stats_done, aggr_done, veps_done, rstd_done = sem("stats_done"), sem("aggr_done"), sem("veps_done"), sem("rstd_done")
        xln_ready, xhi_ready = sem("xln_ready"), sem("xhi_ready")
        kbd_ready = sem("kbd_ready")
        score_full = [sem(f"score_full{g}") for g in range(4)]
        score_freed = [sem(f"score_freed{g}") for g in range(4)]
        mx_ready, exp_done, sum_done, rs_ready, prob_ready = (
            sem(n) for n in ("mx_ready", "exp_done", "sum_done", "rs_ready", "prob_ready"))
        ohi_ready = sem("ohi_ready")
        y_stored = [sem(f"y_stored{p}") for p in range(2)]

        block = ctx.enter_context(nc.Block())

        @block.sync
        def _(sp):
            sp.dma_start(xin[:], x_d[0]).then_inc(x_loaded, 16)
            srcs = (wkT, wqT, wvT, woT)
            for n in range(2):
                sp.dma_start(stage[n][:], srcs[n].rearrange("(k p) n -> p k n", p=P)).then_inc(w_loaded[n], 16)
            sp.dma_start(bk_col[:], bk).then_inc(bias_loaded, 16)
            sp.dma_start(bq_col[:], bq).then_inc(bias_loaded, 16)
            sp.dma_start(bv_row[:], bv.partition_broadcast(P)).then_inc(bias_loaded, 16)
            sp.dma_start(bo_row[:], bo.partition_broadcast(P)).then_inc(bias_loaded, 16)
            for n in range(2, 4):
                wait(sp, w_lo, n - 1)
                sp.dma_start(stage[n % 2][:], srcs[n].rearrange("(k p) n -> p k n", p=P)).then_inc(w_loaded[n % 2], 16)
            for m in range(1, 3):
                wait(sp, xln_ready, 2 * m)
                sp.dma_start(xin[:], x_d[m]).then_inc(x_loaded, 16)
            for p in range(2):
                sp.dma_start(xres[:, p, :], x_d[0][:, p, :]).then_inc(res_loaded[p], 16)

            def slot(d):
                if not isinstance(d, int) or d < DUOS - 3:
                    wait(sp, xln_ready, 2 * d + 6)
                    sp.dma_start(xin[:], x_d[d + 3]).then_inc(x_loaded, 16)
                for p in range(2):
                    work.wait_read(sp, f"Y{p}", d)
                    sp.dma_start(y_t[d * 2 + p], yo[:, p, :]).then_inc(y_stored[p], 16)
                    if not isinstance(d, int) or d < DUOS - 1:
                        sp.dma_start(xres[:, p, :], x_d[d + 1][:, p, :]).then_inc(res_loaded[p], 16)

            steps(sp, slot, DUOS - 4, DUOS - 1)
            for p in range(2):
                sp.wait_ge(y_stored[p], 16 * DUOS)

        @block.gpsimd
        def _(pool):
            pool.memset(ident[:], 0.0).then_inc(const_step, 1)
            pool.memset(causal[:], 0.0).then_inc(const_step, 1)
            pool.memset(head_of[:], 1.0).then_inc(const_step, 1)
            pool.memset(pow_half[:], -0.5).then_inc(pow_ready, 1)
            pool.memset(eps[:], LN_EPS).then_inc(pow_ready, 1)
            pool.wait_ge(const_step, 3)
            pool.affine_select(out=ident[:], in_=ident[:], compare_op=ALU.not_equal, fill=1.0, base=0,
                               pattern=[[-1, P]], channel_multiplier=1).then_inc(const_step, 1)
            for b in range(2):
                half = causal[b * SEQ:(b + 1) * SEQ, :]
                pool.wait_ge(const_step, 4 + b)
                pool.affine_select(out=half, in_=half, compare_op=ALU.is_ge, fill=MASKED, base=0,
                                   pattern=[[-1, SEQ]], channel_multiplier=1).then_inc(const_step, 1)
            pool.wait_ge(const_step, 6)
            pool.affine_select(out=head_of[:], in_=head_of[:], compare_op=ALU.is_ge, fill=0.0, base=0,
                               pattern=[[-HD, GH]], channel_multiplier=1).then_inc(const_step, 1)
            pool.wait_ge(const_step, 7)
            pool.affine_select(out=head_of[:], in_=head_of[:], compare_op=ALU.is_ge, fill=0.0, base=HD - 1,
                               pattern=[[HD, GH]], channel_multiplier=-1).then_inc(const_step, 1)
            pool.tensor_copy(ident_b[:], ident[:]).then_inc(const_step, 1)

            def rstd_of(m):
                wait(pool, aggr_done, 2 * m + 2)
                pool.tensor_tensor(veps[:], mv[:, :, 1], eps[:], ALU.add).then_inc(veps_done, 1)
                wait(pool, veps_done, m + 1)
                pool.tensor_tensor(rstd[:], veps[:], pow_half[:], ALU.pow).then_inc(rstd_done, 1)

            def bias_residual(m, p):
                wait(pool, res_loaded[p], 16 * m + 16)
                wait(pool, bias_loaded, 64)
                pool.tensor_tensor(xres[:, p, :], xres[:, p, :], bo_row[:], ALU.add).then_inc(res_biased[p], 1)

            def normalise(m, p, g):
                wait(pool, rs_ready, 8 * m + 4 * p + g + 1)
                pool.tensor_tensor(prob[:, g], prob[:, g], rs[:, g].unsqueeze(2).to_broadcast([P, GH, SEQ]),
                                   ALU.mult).then_inc(prob_ready, 1)

            pool.wait_ge(pow_ready, 2)
            rstd_of(0)
            rstd_of(1)

            def slot(d):
                for p in range(2):
                    bias_residual(d, p)
                    for g in range(4):
                        normalise(d, p, g)
                if not isinstance(d, int) or d < DUOS - 2:
                    rstd_of(d + 2)

            steps(pool, slot, DUOS - 3, DUOS - 1)

        @block.scalar
        def _(act):
            for n, name in enumerate("kqvo"):
                wait(act, w_loaded[n % 2], 16 * (n // 2) + 16)
                act.activation(w_hl[name][0][:], stage[n % 2][:], ACT.Copy).then_inc(w_hi, 1)
            act.wait_ge(bias_loaded, 64)
            act.activation(bq_col[:], bq_col[:], ACT.Copy, scale=HD ** -0.5).then_inc(bias_scaled, 1)
            act.wait_ge(zeros_ready, 2)

            def x_hi(m, p):
                work.wait_full(act, f"X{p}", m)
                act.activation(xT[0][:, :, p * P:(p + 1) * P], work.tile(f"X{p}")[:].rearrange("p (k t) -> p k t", k=KC),
                               ACT.Copy).then_inc(xhi_ready, 1)

            def k_out(m, c):
                if c == 0:
                    wait(act, kbd_ready, 2 * m)
                work.wait_full(act, f"K{c}", m)
                act.activation(kT[:, c, :], work.tile(f"K{c}")[:, 0:2 * P], ACT.Identity,
                               bias=bk_col[:, c:c + 1]).then_inc(work.freed_sem(f"K{c}"), 1)

            def q_out(m, c):
                work.wait_full(act, f"Q{c}", m)
                act.wait_ge(bias_scaled, 1)
                act.activation(qz[:, :, c, 0:4:3, :],
                               work.tile(f"Q{c}")[:, 0:2 * P].rearrange("p (a b t) -> p a b t", a=2, b=2),
                               ACT.Identity, bias=bq_col[:, c:c + 1], scale=HD ** -0.5).then_inc(work.freed_sem(f"Q{c}"), 1)

            def exp(m, p, g):
                wait(act, score_freed[g], 2 * m + p + 1)
                act.activation(prob[:, g], prob[:, g], ACT.Exp).then_inc(exp_done, 1)

            def probT_out(m, p, g):
                u = f"P{p}{g}"
                work.wait_full(act, u, m)
                act.activation(probT[:, g], work.tile(u)[:].rearrange("p (j t) -> p j t", j=4), ACT.Copy)\
                   .then_inc(work.freed_sem(u), 1)

            def o_hi(m, p):
                work.wait_full(act, f"O{p}", m)
                act.activation(oT[0][:], work.tile(f"O{p}")[:].rearrange("p (g t) -> p g t", g=4), ACT.Copy)\
                   .then_inc(ohi_ready, 1)

            for p in range(2):
                x_hi(0, p)
            for c in range(4):
                k_out(0, c)
            for c in range(4):
                q_out(0, c)

            def slot(d):
                more = not isinstance(d, int) or d < DUOS - 1
                for g in range(4):
                    exp(d, 0, g)
                    if more and g in (1, 2):
                        x_hi(d + 1, g - 1)
                if more:
                    for c in range(4):
                        k_out(d + 1, c)
                for g in range(4):
                    probT_out(d, 0, g)
                o_hi(d, 0)
                for g in range(4):
                    exp(d, 1, g)
                if more:
                    for c in range(4):
                        q_out(d + 1, c)
                for g in range(4):
                    probT_out(d, 1, g)
                o_hi(d, 1)

            steps(act, slot, DUOS - 2, DUOS - 1)

        @block.vector
        def _(dve):
            dve.memset(qz[:], 0.0).then_inc(zeros_ready, 1)
            dve.memset(vbd[:], 0.0).then_inc(zeros_ready, 1)

            def layernorm(m):
                wait(dve, x_loaded, 16 * m + 16)
                for p in range(2):
                    dve.bn_stats(stats[:, p, :], xin[:, p, :]).then_inc(stats_done, 1)
                wait(dve, stats_done, 2 * m + 2)
                dve.memset(carrier[:, 0:1], 0.0)
                for p in range(2):
                    dve.bn_aggr(mv[:, p, :], stats[:, p, :]).then_inc(aggr_done, 1)

            def apply_norm(m):
                wait(dve, rstd_done, m + 1)
                wait(dve, xhi_ready, 2 * m)
                for p in range(2):
                    dve.tensor_scalar(xln[:, p, :], xin[:, p, :], mv[:, p, 0:1], rstd[:, p:p + 1],
                                      ALU.subtract, ALU.mult).then_inc(xln_ready, 1)

            def x_lo(m, p):
                wait(dve, xhi_ready, 2 * m + p + 1)
                dve.tensor_tensor(xT[1][:, :, p * P:(p + 1) * P], work.tile(f"X{p}")[:].rearrange("p (k t) -> p k t", k=KC),
                                  xT[0][:, :, p * P:(p + 1) * P].bitcast(F32), ALU.subtract)\
                   .then_inc(work.freed_sem(f"X{p}"), 1)

            def spread_keys(m, p):
                work.wait_read(dve, "K3", m)
                if not (isinstance(m, int) and m == 0):
                    wait(dve, score_full[3], 2 * m - 1 + p)
                for h in range(GH):
                    ins = dve.tensor_scalar(kbd[:, p, :, :, h, :],
                                            kT[:, :, p * P:(p + 1) * P].rearrange("p g (b t) -> p g b t", b=2),
                                            head_of[:, h:h + 1], None, ALU.mult)
                ins.then_inc(kbd_ready, 1)

            def values_out(m, p):
                u = f"V{p}"
                work.wait_full(dve, u, m)
                for b in range(2):
                    for par in range(2):
                        cols = slice(b * SEQ, (b + 1) * SEQ)
                        ins = dve.tensor_tensor(
                            vbd[par * SEQ:(par + 1) * SEQ, p, b, :, par, :],
                            work.tile(u)[cols, :].rearrange("p (j r d) -> p j r d", r=2, d=HD)[:, :, par, :],
                            bv_row[cols, :].rearrange("p (j r d) -> p j r d", r=2, d=HD)[:, :, par, :], ALU.add)
                ins.then_inc(work.freed_sem(u), 1)

            def less_max(m, p, g):
                n = 8 * m + 4 * p + g + 1
                wait(dve, score_full[g], 2 * m + p + 1)
                s = score[g][:].rearrange("p (h k) -> p h k", h=GH)
                dve.tensor_reduce(mx[:, g, :], s, AX_X, ALU.max).then_inc(mx_ready, 1)
                wait(dve, mx_ready, n)
                dve.tensor_tensor(prob[:, g], s, mx[:, g].unsqueeze(2).to_broadcast([P, GH, SEQ]),
                                  ALU.subtract).then_inc(score_freed[g], 1)

            def row_sum(m, p, g):
                n = 8 * m + 4 * p + g + 1
                wait(dve, exp_done, n)
                dve.tensor_reduce(sm[:, g, :], prob[:, g], AX_X, ALU.add).then_inc(sum_done, 1)
                wait(dve, sum_done, n)
                dve.reciprocal(rs[:, g, :], sm[:, g, :]).then_inc(rs_ready, 1)

            def o_lo(m, p):
                wait(dve, ohi_ready, 2 * m + p + 1)
                dve.tensor_tensor(oT[1][:], work.tile(f"O{p}")[:].rearrange("p (g t) -> p g t", g=4),
                                  oT[0][:].bitcast(F32), ALU.subtract).then_inc(work.freed_sem(f"O{p}"), 1)

            def y_out(m, p):
                u = f"Y{p}"
                work.wait_full(dve, u, m)
                wait(dve, res_biased[p], m + 1)
                wait(dve, y_stored[p], 16 * m)
                dve.tensor_tensor(yo[:, p, :], work.tile(u)[:], xres[:, p, :], ALU.add).then_inc(work.freed_sem(u), 1)

            layernorm(0)
            for n, name in enumerate("kqvo"):
                wait(dve, w_hi, n + 1)
                dve.tensor_tensor(w_hl[name][1][:], stage[n % 2][:], w_hl[name][0][:].bitcast(F32),
                                  ALU.subtract).then_inc(w_lo, 1)
                if n == 0:
                    apply_norm(0)
            for p in range(2):
                x_lo(0, p)
            layernorm(1)
            dve.wait_ge(const_step, 9)
            for p in range(2):
                spread_keys(0, p)
            apply_norm(1)
            dve.wait_ge(bias_loaded, 64)
            dve.wait_ge(zeros_ready, 2)
            for p in range(2):
                values_out(0, p)

            def slot(d):
                more = not isinstance(d, int) or d < DUOS - 1
                less_max(d, 0, 0)
                less_max(d, 0, 1)
                row_sum(d, 0, 0)
                less_max(d, 0, 2)
                if more:
                    x_lo(d + 1, 0)
                row_sum(d, 0, 1)
                less_max(d, 0, 3)
                if more:
                    x_lo(d + 1, 1)
                row_sum(d, 0, 2)
                row_sum(d, 0, 3)
                if more:
                    spread_keys(d + 1, 0)
                o_lo(d, 0)
                less_max(d, 1, 0)
                less_max(d, 1, 1)
                row_sum(d, 1, 0)
                less_max(d, 1, 2)
                row_sum(d, 1, 1)
                less_max(d, 1, 3)
                row_sum(d, 1, 2)
                row_sum(d, 1, 3)
                if more:
                    spread_keys(d + 1, 1)
                if not isinstance(d, int) or d < DUOS - 2:
                    layernorm(d + 2)
                y_out(d, 0)
                if more:
                    values_out(d + 1, 0)
                if not isinstance(d, int) or d < DUOS - 2:
                    apply_norm(d + 2)
                o_lo(d, 1)
                if more:
                    values_out(d + 1, 1)
                y_out(d, 1)

            steps(dve, slot, DUOS - 3, DUOS - 1)

        @block.tensor
        def _(pe):
            def x_transposes(m, p):
                u = f"X{p}"
                wait(pe, xln_ready, 2 * m + p + 1)
                work.wait_free(pe, u, m)
                for c in range(KC):
                    ins = pe.transpose(work.tile(u)[:, c * P:(c + 1) * P], xln[:, p, c * P:(c + 1) * P], ident[:])
                ins.then_inc(work.full_sem(u), 1)

            def transposed(m, name, c):
                u = f"{name}{c}"
                if c == 0:
                    work.wait_read(pe, "X0", m)
                    work.wait_read(pe, "X1", m)
                work.wait_free(pe, u, m)
                w = w_hl[name.lower()]
                split3(pe, work.tile(u)[:, 0:2 * P], lambda a, k: w[a][:, k, c * P:(c + 1) * P],
                       lambda b, k: xT[b][:, k, :], KC).then_inc(work.full_sem(u), 1)

            def values(m, p):
                u = f"V{p}"
                work.wait_free(pe, u, m)
                split3(pe, work.tile(u)[:], lambda a, k: xT[a][:, k, p * P:(p + 1) * P],
                       lambda b, k: w_hl["v"][b][:, k, :], KC).then_inc(work.full_sem(u), 1)

            def scores(m, p):
                wait(pe, kbd_ready, 2 * m + p + 1)
                work.wait_read(pe, "Q3", m)
                for g in range(4):
                    wait(pe, score_freed[g], 2 * m + p)
                    pe.matmul(score[g][:], ident_b[:], causal[:].unsqueeze(1).to_broadcast([P, GH, SEQ]),
                              start=True, stop=False)
                    for b in range(2):
                        ins = pe.matmul(score[g][:], qz[:, p, g, 2 * b:2 * b + 2, :], kbd[:, p, g, b, :, :],
                                        start=False, stop=b == 1)
                    ins.then_inc(score_full[g], 1)

            def prob_transposes(m, p, g):
                u = f"P{p}{g}"
                wait(pe, prob_ready, 8 * m + 4 * p + g + 1)
                work.wait_free(pe, u, m)
                for j in range(4):
                    ins = pe.transpose(work.tile(u)[:, j * P:(j + 1) * P], prob[:, g, 2 * j:2 * j + 2, :], ident[:])
                ins.then_inc(work.full_sem(u), 1)

            def attend(m, p):
                u = f"O{p}"
                work.wait_free(pe, u, m)
                work.wait_read(pe, f"V{p}", m)
                for g in range(4):
                    work.wait_read(pe, f"P{p}{g}", m)
                    for j in range(4):
                        for b in range(2):
                            at = g * P + b * SEQ
                            ins = pe.matmul(work.tile(u)[32 * j:32 * j + 32, at:at + SEQ],
                                            vbd[:, p, b, 4 * g + j, :, :],
                                            probT[:, g, j, b * SEQ:(b + 1) * SEQ], start=True, stop=True)
                ins.then_inc(work.full_sem(u), 1)

            def out_projection(m, p):
                u = f"Y{p}"
                work.wait_read(pe, f"O{p}", m)
                work.wait_free(pe, u, m)
                split3(pe, work.tile(u)[:], lambda a, k: oT[a][:, k, :],
                       lambda b, k: w_hl["o"][b][:, k, :], KC).then_inc(work.full_sem(u), 1)

            pe.wait_ge(const_step, 9)
            for p in range(2):
                x_transposes(0, p)
            wait(pe, w_lo, 1)
            for c in range(4):
                transposed(0, "K", c)
            wait(pe, w_lo, 2)
            for c in range(4):
                transposed(0, "Q", c)
            wait(pe, w_lo, 3)
            for p in range(2):
                values(0, p)
            wait(pe, w_lo, 4)

            def slot(d):
                more = not isinstance(d, int) or d < DUOS - 1
                scores(d, 0)
                if more:
                    for p in range(2):
                        x_transposes(d + 1, p)
                    for c in range(4):
                        transposed(d + 1, "K", c)
                for g in range(4):
                    prob_transposes(d, 0, g)
                attend(d, 0)
                scores(d, 1)
                if more:
                    for c in range(4):
                        transposed(d + 1, "Q", c)
                out_projection(d, 0)
                if more:
                    values(d + 1, 0)
                for g in range(4):
                    prob_transposes(d, 1, g)
                attend(d, 1)
                if more:
                    values(d + 1, 1)
                out_projection(d, 1)

            steps(pe, slot, DUOS - 2, DUOS - 1)


def window_phase(nc, psum, x, cond, wqT, bq, wkT, bk, wvT, bv, woT, bo, y):
    x_t, c_t, y_t = (a.rearrange("(n t) f -> n t f", t=P) for a in (x, cond, y))
    LAST = PAIRS - 1
    with ExitStack() as ctx:
        def sb(name, shape, dt=F32):
            return ctx.enter_context(nc.sbuf_tensor(f"b_{name}", shape, dt))

        def sem(name):
            return ctx.enter_context(nc.semaphore(f"b_{name}"))

        w_two = {n: sb(f"w{n}", [P, P]) for n in "qkvo"}
        bias = {n: sb(f"bias_{n}", [P, 1]) for n in "qkvo"}
        ident = sb("ident", [P, P])
        head_sum = sb("head_sum", [P, 2 * HALF - 1, BH])
        pick_f = sb("pick_f", [P, HALF, P])
        pick = sb("pick", [P, HALF, P], F32R)
        pow_half, eps = sb("pow_half", [P, 1]), sb("eps", [P, 1])
        carrier = sb("carrier", [P, 1])
        xin, cin, cin_v, xres = (sb(n, [P, DIM]) for n in ("xin", "cin", "cin_v", "xres"))
        stats, mv = sb("stats", [P, 6]), sb("mv", [P, 2])
        veps, rstd = sb("veps", [P, 1]), sb("rstd", [P, 1])
        xln, q = sb("xln", [P, DIM]), sb("q", [P, DIM])
        kpad, vpad = sb("kpad", [P, DIM + WIN]), sb("vpad", [P, DIM + WIN])
        prod = sb("prod", [P, WIN, DIM])
        dots = sb("dots", [P, 2, DIM])
        prob = sb("prob", [P, 2, 2, WIN, BH])
        mx, sm, rs = (sb(n, [P, 2, 2, BH]) for n in ("mx", "sm", "rs"))
        probT = [sb(f"probT_{part}", [P, 2, DIM], F32R) for part in ("hi", "lo")]
        pv = sb("pv", [P, WIN, DIM])
        yo = sb("yo", [P, DIM])

        dots_bank, spread_bank, y_bank = psum[0:2], psum[2:4], psum[4]
        work = Banks(nc, ctx, "b_work", psum[5:8],
                     {"Q": 0, "K": 1, "T0": 2, "T1": 0, "V": 1, "R0": 2, "R1": 0},
                     {"Q": 2, "K": 2, "T0": 1, "T1": 1, "V": 1, "R0": 1, "R1": 1}, LAST)

        w_zeroed, w_loaded, bias_loaded = sem("w_zeroed"), sem("w_loaded"), sem("bias_loaded")
        const_step, const_ready, pad_zeroed = sem("const_step"), sem("const_ready"), sem("pad_zeroed")
        pow_ready = sem("pow_ready")
        x_loaded, c_loaded, cv_loaded, res_loaded = sem("x_loaded"), sem("c_loaded"), sem("cv_loaded"), sem("res_loaded")
        stats_done, aggr_done, veps_done, rstd_done = sem("stats_done"), sem("aggr_done"), sem("veps_done"), sem("rstd_done")
        xln_ready = sem("xln_ready")
        prod_dve, prod_pool = sem("prod_dve"), sem("prod_pool")
        summed = sem("summed")
        dots_out = [sem(f"dots_out{h}") for h in range(2)]
        mx_ready, exp_done, sum_done, rs_ready, prob_ready = (
            sem(n) for n in ("mx_ready", "exp_done", "sum_done", "rs_ready", "prob_ready"))
        phi_ready = sem("phi_ready")
        spread_full = [sem(f"spread_full{i}") for i in range(2)]
        pv_ready = [sem(f"pv_ready{i}") for i in range(2)]
        pairs_added, fours_added = sem("pairs_added"), sem("fours_added")
        y_full, y_ready, y_stored = sem("y_full"), sem("y_ready"), sem("y_stored")

        SUM_AHEAD, PROD_AHEAD = WIN + 10, WIN + 14

        def real(m):
            return not isinstance(m, int) or 0 <= m <= LAST

        def ahead(i, w, by):
            return i + (w + by) // WIN, (w + by) % WIN

        block = ctx.enter_context(nc.Block())

        @block.sync
        def _(sp):
            sp.dma_start(xin[:], x_t[0]).then_inc(x_loaded, 16)
            sp.dma_start(cin[:], c_t[0]).then_inc(c_loaded, 16)
            sp.dma_start(cin_v[:], c_t[0]).then_inc(cv_loaded, 16)
            sp.wait_ge(w_zeroed, 4)
            for n, src in zip("qkvo", (wqT, wkT, wvT, woT)):
                for b in range(2):
                    part = slice(b * SEQ, (b + 1) * SEQ)
                    sp.dma_start(w_two[n][part, part], src).then_inc(w_loaded, 16)
            for n, src in zip("qkvo", (bq, bk, bv, bo)):
                for b in range(2):
                    sp.dma_start(bias[n][b * SEQ:(b + 1) * SEQ, :], src).then_inc(bias_loaded, 16)
            sp.dma_start(xres[:], x_t[0]).then_inc(res_loaded, 16)

            def slot(i):
                if not isinstance(i, int) or 1 <= i + 4 <= LAST:
                    wait(sp, xln_ready, i + 4)
                    sp.dma_start(xin[:], x_t[i + 4]).then_inc(x_loaded, 16)
                if not isinstance(i, int) or 1 <= i + 3 <= LAST:
                    work.wait_full(sp, "K", i + 2)
                    sp.dma_start(cin[:], c_t[i + 3]).then_inc(c_loaded, 16)
                if real(i - 1):
                    wait(sp, y_ready, i)
                    sp.dma_start(y_t[i - 1], yo[:]).then_inc(y_stored, 16)
                    if real(i):
                        sp.dma_start(xres[:], x_t[i]).then_inc(res_loaded, 16)
                if not isinstance(i, int) or 1 <= i + 2 <= LAST:
                    work.wait_full(sp, "V", i + 1)
                    sp.dma_start(cin_v[:], c_t[i + 2]).then_inc(cv_loaded, 16)

            steps(sp, slot, LAST - 4, LAST + 1, first=-3, first_full=2)
            sp.wait_ge(y_stored, 16 * PAIRS)

        def add_norm_pool(pool, m):
            wait(pool, aggr_done, m + 1)
            pool.tensor_tensor(veps[:], mv[:, 1:2], eps[:], ALU.add).then_inc(veps_done, 1)
            wait(pool, veps_done, m + 1)
            pool.tensor_tensor(rstd[:], veps[:], pow_half[:], ALU.pow).then_inc(rstd_done, 1)

        def product(eng, m, w, done):
            if w < 2:
                work.wait_read(eng, "Q", m)
                work.wait_read(eng, "K", m)
                eng.wait_ge(pad_zeroed, 2)
            if not (isinstance(m, int) and m == 0):
                wait(eng, summed, WIN * m - WIN + w + 1)
            eng.tensor_tensor(prod[:, w, :], q[:], kpad[:, w:w + DIM], ALU.mult).then_inc(done, 1)

        @block.gpsimd
        def _(pool):
            for n in "qkvo":
                pool.memset(w_two[n][:], 0.0).then_inc(w_zeroed, 1)
            pool.memset(pow_half[:], -0.5).then_inc(pow_ready, 1)
            pool.memset(eps[:], LN_EPS).then_inc(pow_ready, 1)
            pool.memset(ident[:], 0.0).then_inc(const_step, 1)
            pool.memset(head_sum[:], 0.0).then_inc(const_step, 1)
            pool.memset(pick_f[:], 0.0).then_inc(const_step, 1)
            pool.wait_ge(const_step, 3)
            pool.memset(head_sum[:, HALF - 1, :], 1.0).then_inc(const_step, 1)
            pool.wait_ge(const_step, 4)
            pool.wait_ge(pow_ready, 2)
            add_norm_pool(pool, 0)
            pool.affine_select(out=ident[:], in_=ident[:], compare_op=ALU.not_equal, fill=1.0, base=0,
                               pattern=[[-1, P]], channel_multiplier=1).then_inc(const_step, 1)
            mid = head_sum[:, HALF - 1, :]
            pool.affine_select(out=mid, in_=mid, compare_op=ALU.is_ge, fill=0.0, base=0,
                               pattern=[[-XHD, BH]], channel_multiplier=1).then_inc(const_step, 1)
            pool.wait_ge(const_step, 6)
            pool.affine_select(out=mid, in_=mid, compare_op=ALU.is_ge, fill=0.0, base=XHD - 1,
                               pattern=[[XHD, BH]], channel_multiplier=-1).then_inc(const_step, 1)
            sel = pick_f[:].rearrange("p w (h d) -> p w h d", d=XHD)
            pool.affine_select(out=sel, in_=sel, compare_op=ALU.not_equal, fill=1.0, base=0,
                               pattern=[[-BH, HALF], [-1, BH], [0, XHD]], channel_multiplier=1).then_inc(const_step, 1)
            pool.wait_ge(const_step, 8)
            pool.tensor_copy(pick[:], pick_f[:]).then_inc(const_ready, 1)

            def normalise(m, a):
                wait(pool, rs_ready, 2 * m + a + 1)
                pool.tensor_tensor(prob[:, a], prob[:, a],
                                   rs[:, a].unsqueeze(2).to_broadcast([P, 2, WIN, BH]), ALU.mult)\
                    .then_inc(prob_ready, 1)

            def slot(i):
                for w in range(1, WIN, 2):
                    m, at = ahead(i, w, PROD_AHEAD)
                    if real(m):
                        product(pool, m, at, prod_pool)
                    if w in (9, 11) and real(i + 1):
                        normalise(i + 1, (w - 9) // 2)
                    if real(i):
                        for par in range(2):
                            wait(pool, pv_ready[par], 8 * i + w // 2 + 1)
                        pool.tensor_tensor(pv[:, w - 1, :], pv[:, w - 1, :], pv[:, w, :], ALU.add)\
                            .then_inc(pairs_added, 1)
                    if w == 3 and real(i + 3):
                        add_norm_pool(pool, i + 3)

            steps(pool, slot, LAST - 3, LAST, first=-2, first_full=1)

        @block.scalar
        def _(act):
            act.wait_ge(bias_loaded, 128)
            act.wait_ge(pad_zeroed, 2)

            def q_out(m):
                work.wait_full(act, "Q", m)
                wait(act, prod_dve, 8 * m)
                wait(act, prod_pool, 8 * m)
                act.activation(q[:], work.tile("Q")[:], ACT.Identity, bias=bias["q"][:, 0:1])\
                   .then_inc(work.freed_sem("Q"), 1)

            def k_out(m):
                work.wait_full(act, "K", m)
                act.activation(kpad[:, PADL:PADL + DIM], work.tile("K")[:], ACT.Identity, bias=bias["k"][:, 0:1])\
                   .then_inc(work.freed_sem("K"), 1)

            def v_out(m):
                work.wait_full(act, "V", m)
                for par in range(2):
                    wait(act, pv_ready[par], 8 * m)
                act.activation(vpad[:, PADL:PADL + DIM], work.tile("V")[:], ACT.Identity, bias=bias["v"][:, 0:1])\
                   .then_inc(work.freed_sem("V"), 1)

            def dots_to_sbuf(m, h):
                wait(act, summed, WIN * m + HALF * (h + 1))
                act.activation(dots[:, h, :], dots_bank[h][:], ACT.Copy).then_inc(dots_out[h], 1)

            def exp(m):
                for a in range(2):
                    work.wait_read(act, f"T{a}", m)
                    act.activation(prob[:, a], prob[:, a], ACT.Exp, scale=XHD ** -0.5).then_inc(exp_done, 1)

            def prob_hi(m):
                for h in range(2):
                    work.wait_full(act, f"R{h}", m)
                    act.activation(probT[0][:, h, :], work.tile(f"R{h}")[:], ACT.Copy).then_inc(phi_ready, 1)

            def slot(i):
                if real(i + 1):
                    dots_to_sbuf(i + 1, 0)
                if real(i + 2):
                    q_out(i + 2)
                    k_out(i + 2)
                if real(i + 1):
                    dots_to_sbuf(i + 1, 1)
                    exp(i + 1)
                    prob_hi(i + 1)
                    v_out(i + 1)

            steps(act, slot, LAST - 2, LAST, first=-2, first_full=1)

        @block.vector
        def _(dve):
            dve.memset(kpad[:], 0.0).then_inc(pad_zeroed, 1)
            dve.memset(vpad[:], 0.0).then_inc(pad_zeroed, 1)

            def layernorm(m):
                wait(dve, x_loaded, 16 * m + 16)
                dve.bn_stats(stats[:], xin[:]).then_inc(stats_done, 1)
                wait(dve, stats_done, m + 1)
                dve.memset(carrier[:], 0.0)
                dve.bn_aggr(mv[:], stats[:]).then_inc(aggr_done, 1)

            def apply_norm(m):
                wait(dve, rstd_done, m + 1)
                if not (isinstance(m, int) and m == 0):
                    work.wait_full(dve, "Q", m - 1)
                dve.tensor_scalar(xln[:], xin[:], mv[:, 0:1], rstd[:, 0:1], ALU.subtract, ALU.mult)\
                   .then_inc(xln_ready, 1)

            def less_max(m, a):
                u = f"T{a}"
                work.wait_full(dve, u, m)
                s = work.tile(u)[:].rearrange("p (t w b) -> p t w b", t=2, w=WIN)
                dve.tensor_reduce(mx[:, a], s.transpose([0, 1, 3, 2]), AX_X, ALU.max).then_inc(mx_ready, 1)
                wait(dve, mx_ready, 2 * m + a + 1)
                dve.tensor_tensor(prob[:, a], s, mx[:, a].unsqueeze(2).to_broadcast([P, 2, WIN, BH]), ALU.subtract)\
                   .then_inc(work.freed_sem(u), 1)

            def row_sum(m, a):
                wait(dve, exp_done, 2 * m + a + 1)
                dve.tensor_reduce(sm[:, a], prob[:, a].transpose([0, 1, 3, 2]), AX_X, ALU.add).then_inc(sum_done, 1)
                wait(dve, sum_done, 2 * m + a + 1)
                dve.reciprocal(rs[:, a], sm[:, a]).then_inc(rs_ready, 1)

            def prob_lo(m):
                for h in range(2):
                    u = f"R{h}"
                    wait(dve, phi_ready, 2 * m + h + 1)
                    dve.tensor_tensor(probT[1][:, h, :], work.tile(u)[:], probT[0][:, h, :].bitcast(F32),
                                      ALU.subtract).then_inc(work.freed_sem(u), 1)

            def weigh(i, w):
                wait(dve, spread_full[w % 2], 8 * i + w // 2 + 1)
                if w == 0:
                    work.wait_read(dve, "V", i)
                dve.tensor_tensor(pv[:, w, :], spread_bank[w % 2][:], vpad[:, w:w + DIM], ALU.mult)\
                   .then_inc(pv_ready[w % 2], 1)

            def add_fours(i, j):
                wait(dve, pairs_added, 8 * i + 2 * j + 2)
                dve.tensor_tensor(pv[:, 4 * j, :], pv[:, 4 * j, :], pv[:, 4 * j + 2, :], ALU.add).then_inc(fours_added, 1)

            def y_out(i):
                wait(dve, y_full, i + 1)
                wait(dve, res_loaded, 16 * i + 16)
                wait(dve, y_stored, 16 * i)
                dve.scalar_tensor_tensor(yo[:], y_bank[:], bias["o"][:, 0:1], xres[:], ALU.add, ALU.add)\
                   .then_inc(y_ready, 1)

            def slot(i):
                for w in range(WIN):
                    m, at = ahead(i, w, PROD_AHEAD)
                    if w % 2 == 0 and real(m):
                        product(dve, m, at, prod_dve)
                    if real(i):
                        weigh(i, w)
                    if w == 2 and real(i - 1):
                        add_fours(i - 1, 3)
                    if w == 1 and real(i + 3):
                        layernorm(i + 3)
                    if w >= 6 and w % 4 == 2 and real(i):
                        add_fours(i, (w - 6) // 4)
                    if w == 7 and real(i - 1):
                        y_out(i - 1)
                    if w == 5 and real(i + 3):
                        apply_norm(i + 3)
                    if w in (8, 9) and real(i + 1):
                        less_max(i + 1, w - 8)
                    if w in (9, 10) and real(i + 1):
                        row_sum(i + 1, w - 9)
                if real(i + 1):
                    prob_lo(i + 1)

            steps(dve, slot, LAST - 3, LAST, first=-3, first_full=2)
            add_fours(LAST, 3)
            y_out(LAST)

        @block.tensor
        def _(pe):
            def pointwise(m, u, rhs):
                work.wait_free(pe, u, m)
                pe.matmul(work.tile(u)[:], w_two[u.lower()][:], rhs[:], start=True, stop=True)\
                  .then_inc(work.full_sem(u), 1)

            def query_key(m):
                wait(pe, xln_ready, m + 1)
                pointwise(m, "Q", xln)
                wait(pe, c_loaded, 16 * m + 16)
                pointwise(m, "K", cin)

            def value(m):
                wait(pe, cv_loaded, 16 * m + 16)
                pointwise(m, "V", cin_v)

            def head_sums(m, w):
                h, r = w // HALF, w % HALF
                if r == 0:
                    wait(pe, dots_out[h], m)
                done = prod_pool if w % 2 else prod_dve
                wait(pe, done, 8 * m + w // 2 + 1)
                pe.matmul(dots_bank[h][:], head_sum[:, HALF - 1 - r:2 * HALF - 1 - r, :], prod[:, w, :],
                          start=r == 0, stop=r == HALF - 1).then_inc(summed, 1)

            def turn(m):
                for h in range(2):
                    wait(pe, dots_out[h], m + 1)
                for a in range(2):
                    u = f"T{a}"
                    work.wait_free(pe, u, m)
                    for t in range(2):
                        for h in range(2):
                            ins = pe.transpose(work.tile(u)[:, (2 * t + h) * P:(2 * t + h + 1) * P],
                                               dots[:, h, (2 * a + t) * P:(2 * a + t + 1) * P], ident[:])
                    ins.then_inc(work.full_sem(u), 1)

            def turn_back(m, h):
                wait(pe, prob_ready, 2 * m + 2)
                u = f"R{h}"
                work.wait_free(pe, u, m)
                for a in range(2):
                    for t in range(2):
                        ins = pe.transpose(work.tile(u)[:, (2 * a + t) * P:(2 * a + t + 1) * P],
                                           prob[:, a, t, h * HALF:(h + 1) * HALF, :], ident[:])
                ins.then_inc(work.full_sem(u), 1)

            def spread(i, w):
                h, r = w // HALF, w % HALF
                if r == 0:
                    work.wait_read(pe, f"R{h}", i)
                    if isinstance(i, int):
                        pe.wait_ge(const_ready, 1)
                wait(pe, pv_ready[w % 2], 8 * i + w // 2)
                pe.matmul(spread_bank[w % 2][:], pick[:, r, :], probT[0][:, h, :], start=True, stop=False)
                pe.matmul(spread_bank[w % 2][:], pick[:, r, :], probT[1][:, h, :], start=False, stop=True)\
                  .then_inc(spread_full[w % 2], 1)

            def project(i, j):
                wait(pe, fours_added, 4 * i + j + 1)
                if j == 0:
                    wait(pe, y_ready, i)
                ins = pe.matmul(y_bank[:], w_two["o"][:], pv[:, 4 * j, :], start=j == 0, stop=j == 3)
                if j == 3:
                    ins.then_inc(y_full, 1)

            pe.wait_ge(w_loaded, 128)
            pe.wait_ge(const_step, 8)

            def slot(i):
                for w in range(WIN):
                    m, at = ahead(i, w, SUM_AHEAD)
                    if real(m):
                        head_sums(m, at)
                    if w % 4 == 0 and w < 8 and real(i - 1):
                        project(i - 1, 2 + w // 4)
                    if w % 4 == 1 and w >= 8 and real(i):
                        project(i, w // 4 - 2)
                    if w == 15 and real(i + 1):
                        turn_back(i + 1, 0)
                    if real(i):
                        spread(i, w)
                    if w == 1 and real(i + 2):
                        query_key(i + 2)
                    if w == 7 and real(i + 1):
                        turn(i + 1)
                    if w == 12 and real(i + 1):
                        value(i + 1)
                if real(i + 1):
                    turn_back(i + 1, 1)

            steps(pe, slot, LAST - 2, LAST, first=-2, first_full=2)
            project(LAST, 2)
            project(LAST, 3)


def expert_phase(nc, psum, x, gate, up, down, fc1T, expertT, fc2, gamma, beta, y):
    x_d = x.rearrange("(d p t) f -> d t p f", p=2, t=P)
    y_t = y.rearrange("(n t) f -> n t f", t=P)
    with ExitStack() as ctx:
        def sb(name, shape, dt=F32):
            return ctx.enter_context(nc.sbuf_tensor(f"c_{name}", shape, dt))

        def sem(name):
            return ctx.enter_context(nc.semaphore(f"c_{name}"))

        PARTS = ("hi", "lo")
        up_w = [sb(f"up_{s}", [P, KC, INT], F32R) for s in PARTS]
        down_w = [sb(f"down_{s}", [P, IC, DIM], F32R) for s in PARTS]
        gate_w = [sb(f"gate_{s}", [P, KC, NE], F32R) for s in PARTS]
        lat_w = [sb(f"lat_{s}", [P, KC, DIM], F32R) for s in PARTS]
        HSTAGE = KC * INT // 2
        stage = [sb(f"stage{i}", [P, HSTAGE]) for i in range(3)]
        gate_f = sb("gate_f", [P, KC, NE])
        fc1_f, expert_f, fc2_f = sb("fc1_f", [P, LC, DIM]), sb("expert_f", [P, LC, LAT]), sb("fc2_f", [P, LC, DIM])
        tail_f = sb("tail_f", [P, LC, DIM])
        gamma_row, beta_row = sb("gamma_row", [P, DIM]), sb("beta_row", [P, DIM])
        ident, pow_half, eps = sb("ident", [P, P]), sb("pow_half", [P, 2]), sb("eps", [P, 2])
        carrier = sb("carrier", [P, 5])
        xin, xres, xln = (sb(n, [P, 2, DIM]) for n in ("xin", "xres", "xln"))
        stats, mv = sb("stats", [P, 2, 6]), sb("mv", [P, 2, 2])
        veps, rstd = sb("veps", [P, 2]), sb("rstd", [P, 2])
        xT = [sb(f"xT_{s}", [P, KC, 2 * P], F32R) for s in PARTS]
        relu = sb("relu", [P, 2, 2 * P])
        hidden = sb("hidden", [P, 2, 2 * P])
        hid = [sb(f"hid_{s}", [P, IC, 2 * P], F32R) for s in PARTS]
        top, route = sb("top", [P, 2, NE]), sb("route", [P, 2])
        routed, z = sb("routed", [P, 2, DIM]), sb("z", [P, 2, DIM])
        zstats, zmv = sb("zstats", [P, 2, 6]), sb("zmv", [P, 2, 2])
        zveps, zrstd = sb("zveps", [P, 2]), sb("zrstd", [P, 2])
        yo = sb("yo", [P, 2, DIM])

        bank_of = {f"H{c}": c % 4 for c in range(IC)}
        bank_of.update({"G0": 6, "R0": 4, "G1": 6, "R1": 5, "X0": 4, "X1": 5, "D0": 7, "D1": 6})
        work = Banks(nc, ctx, "c_work", psum, bank_of, {"X0": 1, "X1": 1}, DUOS - 1)

        const_step, pow_ready = sem("const_step"), sem("pow_ready")
        small_loaded, row_loaded = sem("small_loaded"), sem("row_loaded")
        stage_loaded = [sem(f"stage_loaded{i}") for i in range(3)]
        w_hi, w_lo = sem("w_hi"), sem("w_lo")
        tail_full, tail_out, lat_full = sem("tail_full"), sem("tail_out"), sem("lat_full")
        lat_hi, lat_lo = sem("lat_hi"), sem("lat_lo")
        x_loaded, res_loaded = sem("x_loaded"), [sem(f"res_loaded{p}") for p in range(2)]
        res_biased = [sem(f"res_biased{p}") for p in range(2)]
        stats_done, aggr_done, veps_done, rstd_done = sem("stats_done"), sem("aggr_done"), sem("veps_done"), sem("rstd_done")
        xln_ready, xhi_ready = sem("xln_ready"), sem("xhi_ready")
        relu_done = sem("relu_done")
        hhi_ready, hlo_ready = sem("hhi_ready"), sem("hlo_ready")
        route_ready = sem("route_ready")
        zstats_done, zaggr_done, zveps_done, zrstd_done = sem("zstats_done"), sem("zaggr_done"), sem("zveps_done"), sem("zrstd_done")
        z_norm, z_scaled = sem("z_norm"), sem("z_scaled")
        y_ready, y_stored = [sem(f"y_ready{p}") for p in range(2)], [sem(f"y_stored{p}") for p in range(2)]

        def halves(w):
            flat = [part[:].rearrange("p k n -> p (k n)") for part in w]
            return [[part[:, h * HSTAGE:(h + 1) * HSTAGE] for part in flat] for h in range(2)]

        up_src = up.rearrange("(k p) n -> p k n", p=P)
        down_src = down.rearrange("(k p) n -> p k n", p=P)
        loads = ([(dst, up_src[:, h * KC // 2:(h + 1) * KC // 2, :]) for h, dst in enumerate(halves(up_w))]
                 + [(dst, down_src[:, h * IC // 2:(h + 1) * IC // 2, :]) for h, dst in enumerate(halves(down_w))])

        block = ctx.enter_context(nc.Block())

        @block.sync
        def _(sp):
            sp.dma_start(xin[:], x_d[0]).then_inc(x_loaded, 16)
            sp.dma_start(expert_f[:], expertT.rearrange("(k p) n -> p k n", p=P)).then_inc(small_loaded, 16)
            sp.dma_start(fc2_f[:], fc2.rearrange("(k p) n -> p k n", p=P)).then_inc(small_loaded, 16)
            sp.dma_start(fc1_f[:], fc1T.rearrange("(k p) n -> p k n", p=P)).then_inc(small_loaded, 16)
            sp.dma_start(gate_f[:], gate.rearrange("(k p) n -> p k n", p=P)).then_inc(small_loaded, 16)
            for n, (_, src) in enumerate(loads):
                if n >= 3:
                    wait(sp, w_lo, n - 3 + 2)
                sp.dma_start(stage[n % 3][:].rearrange("p (k n) -> p k n", n=src.shape[2]), src)\
                  .then_inc(stage_loaded[n % 3], 16)
            sp.dma_start(gamma_row[:], gamma.partition_broadcast(P)).then_inc(row_loaded, 16)
            sp.dma_start(beta_row[:], beta.partition_broadcast(P)).then_inc(row_loaded, 16)
            wait(sp, xln_ready, 2)
            sp.dma_start(xin[:], x_d[1]).then_inc(x_loaded, 16)
            for p in range(2):
                sp.dma_start(xres[:, p, :], x_d[0][:, p, :]).then_inc(res_loaded[p], 16)

            def slot(d):
                if not isinstance(d, int) or d < DUOS - 2:
                    wait(sp, xln_ready, 2 * d + 4)
                    sp.dma_start(xin[:], x_d[d + 2]).then_inc(x_loaded, 16)
                for p in range(2):
                    wait(sp, y_ready[p], d + 1)
                    sp.dma_start(y_t[d * 2 + p], yo[:, p, :]).then_inc(y_stored[p], 16)
                    if not isinstance(d, int) or d < DUOS - 1:
                        sp.dma_start(xres[:, p, :], x_d[d + 1][:, p, :]).then_inc(res_loaded[p], 16)

            steps(sp, slot, DUOS - 3, DUOS - 1)
            for p in range(2):
                sp.wait_ge(y_stored[p], 16 * DUOS)

        @block.gpsimd
        def _(pool):
            pool.memset(pow_half[:], -0.5).then_inc(pow_ready, 1)
            pool.memset(eps[:], LN_EPS).then_inc(pow_ready, 1)
            pool.memset(ident[:], 0.0).then_inc(const_step, 1)
            pool.wait_ge(const_step, 1)
            pool.affine_select(out=ident[:], in_=ident[:], compare_op=ALU.not_equal, fill=1.0, base=0,
                               pattern=[[-1, P]], channel_multiplier=1).then_inc(const_step, 1)

            def rstd_of(m):
                wait(pool, aggr_done, 2 * m + 2)
                pool.tensor_tensor(veps[:], mv[:, :, 1], eps[:], ALU.add).then_inc(veps_done, 1)
                wait(pool, veps_done, m + 1)
                pool.tensor_tensor(rstd[:], veps[:], pow_half[:], ALU.pow).then_inc(rstd_done, 1)

            def hidden_lo(m, c):
                wait(pool, hhi_ready, 8 * m + c + 1)
                pool.tensor_tensor(hid[1][:, c, :], hidden[:, c % 2, :], hid[0][:, c, :].bitcast(F32), ALU.subtract)\
                    .then_inc(hlo_ready, 1)

            def bias_residual(m, p):
                wait(pool, res_loaded[p], 16 * m + 16)
                wait(pool, row_loaded, 32)
                pool.tensor_tensor(xres[:, p, :], xres[:, p, :], beta_row[:], ALU.add).then_inc(res_biased[p], 1)

            def z_rstd(m, p):
                wait(pool, zaggr_done, 2 * m + p + 1)
                pool.tensor_tensor(zveps[:, p:p + 1], zmv[:, p, 1:2], eps[:, 0:1], ALU.add).then_inc(zveps_done, 1)
                wait(pool, zveps_done, 2 * m + p + 1)
                pool.tensor_tensor(zrstd[:, p:p + 1], zveps[:, p:p + 1], pow_half[:, 0:1], ALU.pow).then_inc(zrstd_done, 1)

            def z_gamma(m, p):
                wait(pool, z_norm, 2 * m + p + 1)
                pool.tensor_tensor(z[:, p, :], z[:, p, :], gamma_row[:], ALU.mult).then_inc(z_scaled, 1)

            pool.wait_ge(pow_ready, 2)
            rstd_of(0)

            def slot(d):
                for c in range(IC):
                    hidden_lo(d, c)
                for p in range(2):
                    bias_residual(d, p)
                if not isinstance(d, int) or d < DUOS - 1:
                    rstd_of(d + 1)
                for p in range(2):
                    z_rstd(d, p)
                    z_gamma(d, p)

            steps(pool, slot, DUOS - 2, DUOS - 1)

        @block.scalar
        def _(act):
            def tail_to_sbuf():
                for c in range(LC):
                    wait(act, tail_full, c + 1)
                    act.activation(tail_f[:, c, :], psum[c][:], ACT.Copy).then_inc(tail_out, 1)

            def lat_high():
                for c in range(KC):
                    wait(act, lat_full, c + 1)
                    act.activation(lat_w[0][:, c, :], psum[c][:], ACT.Copy).then_inc(lat_hi, 1)

            def x_hi(m, p):
                work.wait_full(act, f"X{p}", m)
                act.activation(xT[0][:, :, p * P:(p + 1) * P], work.tile(f"X{p}")[:].rearrange("p (k t) -> p k t", k=KC),
                               ACT.Copy).then_inc(xhi_ready, 1)

            act.wait_ge(small_loaded, 64)
            act.activation(gate_w[0][:], gate_f[:], ACT.Copy).then_inc(w_hi, 1)
            tail_to_sbuf()
            lat_high()
            for p in range(2):
                x_hi(0, p)
            for n, (dst, _) in enumerate(loads):
                wait(act, stage_loaded[n % 3], 16 * (n // 3) + 16)
                act.activation(dst[0], stage[n % 3][:], ACT.Copy).then_inc(w_hi, 1)

            def relu_out(m, c):
                work.wait_full(act, f"H{c}", m)
                act.activation(relu[:, c % 2, :], work.tile(f"H{c}")[:, 0:2 * P], ACT.Relu).then_inc(relu_done, 1)

            def hidden_hi(m, c):
                work.wait_read(act, f"H{c}", m)
                act.activation(hid[0][:, c, :], hidden[:, c % 2, :], ACT.Copy).then_inc(hhi_ready, 1)

            def routed_out(m, p):
                work.wait_full(act, f"R{p}", m)
                wait(act, route_ready, 2 * m + p + 1)
                act.activation(routed[:, p, :], work.tile(f"R{p}")[:], ACT.Copy, scale=route[:, p:p + 1])\
                   .then_inc(work.freed_sem(f"R{p}"), 1)

            def slot(d):
                relu_out(d, 0)
                for c in range(1, IC):
                    relu_out(d, c)
                    hidden_hi(d, c - 1)
                hidden_hi(d, IC - 1)
                for p in range(2):
                    routed_out(d, p)
                if not isinstance(d, int) or d < DUOS - 1:
                    for p in range(2):
                        x_hi(d + 1, p)

            steps(act, slot, DUOS - 2, DUOS - 1)

        @block.vector
        def _(dve):
            def layernorm(m):
                wait(dve, x_loaded, 16 * m + 16)
                for p in range(2):
                    dve.bn_stats(stats[:, p, :], xin[:, p, :]).then_inc(stats_done, 1)
                wait(dve, stats_done, 2 * m + 2)
                dve.memset(carrier[:, 0:1], 0.0)
                for p in range(2):
                    dve.bn_aggr(mv[:, p, :], stats[:, p, :]).then_inc(aggr_done, 1)

            def apply_norm(m):
                wait(dve, rstd_done, m + 1)
                wait(dve, xhi_ready, 2 * m)
                for p in range(2):
                    dve.tensor_scalar(xln[:, p, :], xin[:, p, :], mv[:, p, 0:1], rstd[:, p:p + 1],
                                      ALU.subtract, ALU.mult).then_inc(xln_ready, 1)

            def x_lo(m, p):
                wait(dve, xhi_ready, 2 * m + p + 1)
                dve.tensor_tensor(xT[1][:, :, p * P:(p + 1) * P], work.tile(f"X{p}")[:].rearrange("p (k t) -> p k t", k=KC),
                                  xT[0][:, :, p * P:(p + 1) * P].bitcast(F32), ALU.subtract)\
                   .then_inc(work.freed_sem(f"X{p}"), 1)

            layernorm(0)
            wait(dve, w_hi, 1)
            dve.tensor_tensor(gate_w[1][:], gate_f[:], gate_w[0][:].bitcast(F32), ALU.subtract).then_inc(w_lo, 1)
            apply_norm(0)
            for c in range(KC):
                wait(dve, lat_hi, c + 1)
                dve.tensor_tensor(lat_w[1][:, c, :], psum[c][:], lat_w[0][:, c, :].bitcast(F32), ALU.subtract)\
                   .then_inc(lat_lo, 1)
            for p in range(2):
                x_lo(0, p)
            for n, (dst, _) in enumerate(loads):
                wait(dve, w_hi, n + 2)
                dve.tensor_tensor(dst[1], stage[n % 3][:], dst[0].bitcast(F32), ALU.subtract).then_inc(w_lo, 1)

            def square(m, c):
                u = f"H{c}"
                wait(dve, relu_done, 8 * m + c + 1)
                if c >= 2:
                    wait(dve, hlo_ready, 8 * m + c - 1)
                dve.scalar_tensor_tensor(hidden[:, c % 2, :], work.tile(u)[:, 0:2 * P], 0.0, relu[:, c % 2, :],
                                         ALU.max, ALU.mult).then_inc(work.freed_sem(u), 1)

            def gate_top(m, p):
                u = f"G{p}"
                work.wait_full(dve, u, m)
                dve.memset(carrier[:, 3 + p:4 + p], 0.0)
                dve.max(top[:, p, :], work.tile(u)[:, 0:NE]).then_inc(work.freed_sem(u), 1)
                work.wait_read(dve, u, m)
                dve.tensor_tensor(route[:, p:p + 1], top[:, p, 0:1], top[:, p, 1:2], ALU.add).then_inc(route_ready, 1)

            def sum_out(m, p):
                u = f"D{p}"
                work.wait_full(dve, u, m)
                work.wait_read(dve, f"R{p}", m)
                dve.tensor_tensor(z[:, p, :], work.tile(u)[:], routed[:, p, :], ALU.add).then_inc(work.freed_sem(u), 1)
                work.wait_read(dve, u, m)
                dve.bn_stats(zstats[:, p, :], z[:, p, :]).then_inc(zstats_done, 1)
                wait(dve, zstats_done, 2 * m + p + 1)
                dve.memset(carrier[:, 1 + p:2 + p], 0.0)
                dve.bn_aggr(zmv[:, p, :], zstats[:, p, :]).then_inc(zaggr_done, 1)
                wait(dve, zrstd_done, 2 * m + p + 1)
                dve.tensor_scalar(z[:, p, :], z[:, p, :], zmv[:, p, 0:1], zrstd[:, p:p + 1],
                                  ALU.subtract, ALU.mult).then_inc(z_norm, 1)

            def y_out(m, p):
                wait(dve, z_scaled, 2 * m + p + 1)
                wait(dve, res_biased[p], m + 1)
                wait(dve, y_stored[p], 16 * m)
                dve.tensor_tensor(yo[:, p, :], z[:, p, :], xres[:, p, :], ALU.add).then_inc(y_ready[p], 1)

            def slot(d):
                more = not isinstance(d, int) or d < DUOS - 1
                for c in range(IC):
                    square(d, c)
                for p in range(2):
                    gate_top(d, p)
                if more:
                    layernorm(d + 1)
                    apply_norm(d + 1)
                    for p in range(2):
                        x_lo(d + 1, p)
                for p in range(2):
                    sum_out(d, p)
                for p in range(2):
                    y_out(d, p)

            steps(dve, slot, DUOS - 2, DUOS - 1)

        @block.tensor
        def _(pe):
            def x_transposes(m, p):
                u = f"X{p}"
                wait(pe, xln_ready, 2 * m + p + 1)
                work.wait_free(pe, u, m)
                for c in range(KC):
                    ins = pe.transpose(work.tile(u)[:, c * P:(c + 1) * P], xln[:, p, c * P:(c + 1) * P], ident[:])
                ins.then_inc(work.full_sem(u), 1)

            def up_chunk(m, c):
                u = f"H{c}"
                work.wait_free(pe, u, m)
                if c == 0:
                    for p in range(2):
                        work.wait_read(pe, f"X{p}", m)
                split3(pe, work.tile(u)[:, 0:2 * P], lambda a, k: up_w[a][:, k, c * P:(c + 1) * P],
                       lambda b, k: xT[b][:, k, :], KC).then_inc(work.full_sem(u), 1)

            def from_tokens(m, p, u, w, n, left, chunks):
                work.wait_free(pe, u, m)
                split3(pe, work.tile(u)[:, 0:n], lambda a, k: left[a][:, k, p * P:(p + 1) * P],
                       lambda b, k: w[b][:, k, :], chunks).then_inc(work.full_sem(u), 1)

            pe.wait_ge(small_loaded, 64)
            for c in range(LC):
                for k in range(LC):
                    ins = pe.matmul(psum[c][:], expert_f[:, k, c * P:(c + 1) * P], fc2_f[:, k, :],
                                    start=k == 0, stop=k == LC - 1)
                ins.then_inc(tail_full, 1)
            pe.wait_ge(tail_out, LC)
            for c in range(KC):
                for k in range(LC):
                    ins = pe.matmul(psum[c][:], fc1_f[:, k, c * P:(c + 1) * P], tail_f[:, k, :],
                                    start=k == 0, stop=k == LC - 1)
                ins.then_inc(lat_full, 1)
            pe.wait_ge(const_step, 2)
            for p in range(2):
                x_transposes(0, p)
            pe.wait_ge(lat_lo, KC)
            pe.wait_ge(w_lo, 5)

            def slot(d):
                for c in range(IC):
                    up_chunk(d, c)
                for p in range(2):
                    from_tokens(d, p, f"G{p}", gate_w, NE, xT, KC)
                    from_tokens(d, p, f"R{p}", lat_w, DIM, xT, KC)
                if not isinstance(d, int) or d < DUOS - 1:
                    for p in range(2):
                        x_transposes(d + 1, p)
                for p in range(2):
                    if p == 0:
                        wait(pe, hlo_ready, 8 * d + IC)
                    from_tokens(d, p, f"D{p}", down_w, DIM, hid, IC)

            steps(pe, slot, DUOS - 2, DUOS - 1)


def decoder_layer(nc, x, ctx_4096, a_wqT, a_bq, a_wkT, a_bk, a_wvT, a_bv, a_woT, a_bo,
                  x_wqT, x_bq, x_wkT, x_bk, x_wvT, x_bv, x_woT, x_bo,
                  gate, up, down, fc1T, expertT, fc2, gamma, beta, out):
    after_attention = nc.dram_tensor("after_attention", [TOKENS, DIM], F32, kind="Internal").ap()
    after_window = nc.dram_tensor("after_window", [TOKENS, DIM], F32, kind="Internal").ap()
    with ExitStack() as ctx:
        psum = [ctx.enter_context(nc.psum_tensor(f"bank{b}", [P, 512], F32)) for b in range(8)]
        attention_phase(nc, psum, x, a_wqT, a_bq, a_wkT, a_bk, a_wvT, a_bv, a_woT, a_bo, after_attention)
        window_phase(nc, psum, after_attention, ctx_4096, x_wqT, x_bq, x_wkT, x_bk, x_wvT, x_bv, x_woT, x_bo,
                     after_window)
        expert_phase(nc, psum, after_window, gate, up, down, fc1T, expertT, fc2, gamma, beta, out)


def kernel(**inputs):
    import numpy as _np
    import concourse.bacc as _bacc
    from concourse import mybir as _mybir
    from concourse.bass_utils import run_bass_kernel_spmd as _run

    given = {n: _np.asarray(a) for n, a in inputs.items()}

    def turned(name):
        return _np.ascontiguousarray(given[name].T)

    laid = {
        "x": given["x"].reshape(TOKENS, DIM),
        "ctx_4096": given["ctx_4096"].reshape(TOKENS, DIM),
        "a_wqT": turned("L0_attn_Wq"), "a_bq": _np.ascontiguousarray(given["L0_attn_bq"].reshape(GROUPS, P).T),
        "a_wkT": turned("L0_attn_Wk"), "a_bk": _np.ascontiguousarray(given["L0_attn_bk"].reshape(GROUPS, P).T),
        "a_wvT": turned("L0_attn_Wv"), "a_bv": given["L0_attn_bv"],
        "a_woT": turned("L0_attn_Wo"), "a_bo": given["L0_attn_bo"],
        "x_wqT": turned("L0_xattn_Wq"), "x_bq": given["L0_xattn_bq"].reshape(SEQ, 1),
        "x_wkT": turned("L0_xattn_Wk"), "x_bk": given["L0_xattn_bk"].reshape(SEQ, 1),
        "x_wvT": turned("L0_xattn_Wv"), "x_bv": given["L0_xattn_bv"].reshape(SEQ, 1),
        "x_woT": turned("L0_xattn_Wo"), "x_bo": given["L0_xattn_bo"].reshape(SEQ, 1),
        "gate": given["L0_ffn_gate_w"], "up": given["L0_ffn_up_w"], "down": given["L0_ffn_down_w"],
        "fc1T": turned("L0_ffn_fc1_w"), "expertT": turned("L0_ffn_expert_w"), "fc2": given["L0_ffn_fc2_w"],
        "gamma": given["L0_ffn_ln_gamma"], "beta": given["L0_ffn_ln_beta"],
    }
    nc = _bacc.Bacc("TRN2", target_bir_lowering=False, num_devices=1)
    arrays, args = {}, []
    for name, a in laid.items():
        arrays[f"in_{name}"] = a
        args.append(nc.dram_tensor(f"in_{name}", a.shape, _mybir.dt.from_np(a.dtype), kind="ExternalInput").ap())
    args.append(nc.dram_tensor("out_rows", [TOKENS, DIM], F32, kind="ExternalOutput").ap())
    decoder_layer(nc, *args)
    r = _run(nc, [arrays], core_ids=[0])
    return r.results[0]["out_rows"].reshape(BATCH, SEQ, DIM)
```

```python
from contextlib import ExitStack

import concourse.bass as bass
from concourse import mybir

BATCH, SEQ, DIM = 32, 64, 512
P = 128
TOKENS = BATCH * SEQ
PAIRS = TOKENS // P
DUOS = PAIRS // 2
KC = DIM // P
HEADS, HD = 32, 16
GROUPS = HEADS * HD // P
GH = HEADS // GROUPS
XH, XHD, WIN = 8, 8, 16
PADL = WIN // 2
BH = 2 * XH
HALF = P // BH
QUAD = HALF // 2
INT, LAT, NE = 1024, 256, 8
IC, LC = INT // P, LAT // P
LN_EPS = 1e-5
MASKED = -1e30

F32 = mybir.dt.float32
F32R = mybir.dt.float32r
BF16 = mybir.dt.bfloat16
ALU = mybir.AluOpType
ACT = mybir.ActivationFunctionType
AX_X = mybir.AxisListType.X


def wait(eng, sem, value):
    if isinstance(value, int) and value <= 0:
        return
    eng.wait_ge(sem, value)


class Banks:

    def __init__(self, nc, ctx, name, tiles, slot, ahead, last):
        self.tiles, self.at, self.last = tiles, slot, last
        self.full = [ctx.enter_context(nc.semaphore(f"{name}_full{b}")) for b in range(len(tiles))]
        self.freed = [ctx.enter_context(nc.semaphore(f"{name}_freed{b}")) for b in range(len(tiles))]
        self.ahead = {u: ahead.get(u, 0) for u in slot}
        self.order = list(slot)

    def tile(self, unit):
        return self.tiles[self.at[unit]]

    def before(self, unit, m):
        shifts = [self.ahead[o] - self.ahead[unit] + (1 if self.order.index(o) < self.order.index(unit) else 0)
                  for o in self.order if self.at[o] == self.at[unit]]
        if isinstance(m, int):
            return sum(min(max(m + s, 0), self.last + 1) for s in shifts)
        return m * len(shifts) + sum(shifts)

    def wait_free(self, eng, unit, m):
        wait(eng, self.freed[self.at[unit]], self.before(unit, m))

    def wait_full(self, eng, unit, m):
        wait(eng, self.full[self.at[unit]], self.before(unit, m) + 1)

    def wait_read(self, eng, unit, m):
        wait(eng, self.freed[self.at[unit]], self.before(unit, m) + 1)

    def full_sem(self, unit):
        return self.full[self.at[unit]]

    def freed_sem(self, unit):
        return self.freed[self.at[unit]]


def steps(eng, slot, last_full, last, first=0, first_full=1):
    for d in range(first, first_full):
        slot(d)
    with eng.Fori(first_full, last_full + 1) as d:
        slot(d)
    for d in range(last_full + 1, last + 1):
        slot(d)


class RowsOut:

    def __init__(self, nc, ctx, name, tiles):
        self.rows = ctx.enter_context(nc.sbuf_tensor(f"{name}_yo", [P, tiles, DIM], F32))
        self.stored = [ctx.enter_context(nc.semaphore(f"{name}_y_stored{i}")) for i in range(tiles)]


def split3(pe, out, lhs, rhs, chunks, start=True, stop=True):
    passes = [(a, b) for c in range(chunks) for a, b in ((0, 0), (0, 1), (1, 0))]
    last = None
    for n, (a, b) in enumerate(passes):
        c = n // 3
        last = pe.matmul(out, lhs(a, c), rhs(b, c), start=start and n == 0, stop=stop and n == len(passes) - 1)
    return last


def attention_phase(nc, psum, x, wqT, bq, wkT, bk, wvT, bv, woT, bo, y, out, window):
    x_d = x.rearrange("(d p t) f -> d t p f", p=2, t=P)
    y_t = y.rearrange("(n t) f -> n t f", t=P)
    with ExitStack() as ctx:
        def sb(name, shape, dt=F32):
            return ctx.enter_context(nc.sbuf_tensor(f"a_{name}", shape, dt))

        def sem(name):
            return ctx.enter_context(nc.semaphore(f"a_{name}"))

        w_hl = {n: [sb(f"w{n}_{part}", [P, KC, DIM], F32R) for part in ("hi", "lo")] for n in "kqvo"}
        stage = [sb(f"stage{i}", [P, KC, DIM]) for i in range(2)]
        bq_col, bk_col = sb("bq_col", [P, GROUPS]), sb("bk_col", [P, GROUPS])
        bv_row, bo_row = sb("bv_row", [P, DIM]), sb("bo_row", [P, DIM])
        ident, ident_b = sb("ident", [P, P]), sb("ident_b", [P, P], BF16)
        causal = sb("causal", [P, SEQ], BF16)
        head_of = sb("head_of", [P, GH])
        pow_half, eps = sb("pow_half", [P, 2]), sb("eps", [P, 2])
        carrier = sb("carrier", [P, 1])
        xin, xres = sb("xin", [P, 2, DIM]), sb("xres", [P, 2, DIM])
        stats, mv = sb("stats", [P, 2, 6]), sb("mv", [P, 2, 2])
        veps, rstd = sb("veps", [P, 2]), sb("rstd", [P, 2])
        xln = sb("xln", [P, 2, DIM])
        xT = [sb(f"xT_{part}", [P, KC, 2 * P], F32R) for part in ("hi", "lo")]
        kT, kT_lo = sb("kT", [P, GROUPS, 2 * P]), sb("kT_lo", [P, GROUPS, 2 * P])
        kT_hi = sb("kT_hi", [P, GROUPS, 2 * P], F32R)
        qT = sb("qT", [P, GROUPS, 2 * P])
        qz = [sb(f"qz_{part}", [P, 2, GROUPS, 4, SEQ], F32R) for part in ("hi", "lo")]
        kbd = [sb(f"kbd_{part}", [P, GROUPS, 2, GH, SEQ], F32R) for part in ("hi", "lo")]
        vbd = sb("vbd", [P, 2, 2, HEADS // 2, 2, HD])
        prob = stage[0][:].rearrange("p g (h s) -> p g h s", s=SEQ)
        mx, sm, rs = (sb(n, [P, GROUPS, GH]) for n in ("mx", "sm", "rs"))
        probT = stage[1][:].rearrange("p g (j t) -> p g j t", t=P)
        oT = [sb(f"oT_{part}", [P, GROUPS, P], F32R) for part in ("hi", "lo")]
        yo, y_stored = out.rows, out.stored

        DVE_HEADS = 3
        score = psum[0:4]
        A_UNITS = ["X0", "X1", "K0", "K1", "K2", "K3", "Q0", "Q1", "Q2", "Q3", "V0", "V1"]
        ORDER = (["X0", "X1", "K0", "K1", "K2", "K3"] + [f"P0{g}" for g in range(4)] + ["O0"]
                 + ["Q0", "Q1", "Q2", "Q3", "Y0", "V0"] + [f"P1{g}" for g in range(4)] + ["O1", "V1", "Y1"])
        work = Banks(nc, ctx, "a_work", psum[4:8], {u: n % 4 for n, u in enumerate(ORDER)}, {u: 1 for u in A_UNITS}, DUOS - 1)

        w_loaded = [sem(f"w_loaded{i}") for i in range(2)]
        w_hi, w_lo = sem("w_hi"), sem("w_lo")
        bias_loaded, bias_scaled = sem("bias_loaded"), sem("bias_scaled")
        const_step, const_ready = sem("const_step"), sem("const_ready")
        zeros_ready, pow_ready = sem("zeros_ready"), sem("pow_ready")
        x_loaded, res_loaded = sem("x_loaded"), [sem(f"res_loaded{p}") for p in range(2)]
        res_biased = [sem(f"res_biased{p}") for p in range(2)]
        stats_done, aggr_done, veps_done, rstd_done = sem("stats_done"), sem("aggr_done"), sem("veps_done"), sem("rstd_done")
        xln_ready, xhi_ready = sem("xln_ready"), sem("xhi_ready")
        khi_ready, klo_ready = sem("khi_ready"), sem("klo_ready")
        kbd_dve, kbd_act = sem("kbd_dve"), sem("kbd_act")
        qhi_ready, qlo_ready = sem("qhi_ready"), sem("qlo_ready")
        score_full = [sem(f"score_full{g}") for g in range(4)]
        score_freed = [sem(f"score_freed{g}") for g in range(4)]
        mx_ready, exp_done, sum_done, rs_ready, prob_ready = (
            sem(n) for n in ("mx_ready", "exp_done", "sum_done", "rs_ready", "prob_ready"))
        ohi_ready = sem("ohi_ready")

        block = ctx.enter_context(nc.Block())

        @block.sync
        def _(sp):
            sp.dma_start(xin[:], x_d[0]).then_inc(x_loaded, 16)
            srcs = (wkT, wqT, wvT, woT)
            for n in range(2):
                sp.dma_start(stage[n][:], srcs[n].rearrange("(k p) n -> p k n", p=P)).then_inc(w_loaded[n], 16)
            sp.dma_start(bk_col[:], bk).then_inc(bias_loaded, 16)
            sp.dma_start(bq_col[:], bq).then_inc(bias_loaded, 16)
            sp.dma_start(bv_row[:], bv.partition_broadcast(P)).then_inc(bias_loaded, 16)
            sp.dma_start(bo_row[:], bo.partition_broadcast(P)).then_inc(bias_loaded, 16)
            for n in range(2, 4):
                wait(sp, w_lo, n - 1)
                sp.dma_start(stage[n % 2][:], srcs[n].rearrange("(k p) n -> p k n", p=P)).then_inc(w_loaded[n % 2], 16)
                m = n - 1
                wait(sp, xln_ready, 2 * m)
                sp.dma_start(xin[:], x_d[m]).then_inc(x_loaded, 16)
            for p in range(2):
                sp.dma_start(xres[:, p, :], x_d[0][:, p, :]).then_inc(res_loaded[p], 16)

            def slot(d):
                if not isinstance(d, int) or d < DUOS - 3:
                    wait(sp, xln_ready, 2 * d + 6)
                    sp.dma_start(xin[:], x_d[d + 3]).then_inc(x_loaded, 16)
                for p in range(2):
                    work.wait_read(sp, f"Y{p}", d)
                    sp.dma_start(y_t[d * 2 + p], yo[:, p, :]).then_inc(y_stored[p], 16)
                    if not isinstance(d, int) or d < DUOS - 1:
                        sp.dma_start(xres[:, p, :], x_d[d + 1][:, p, :]).then_inc(res_loaded[p], 16)

            steps(sp, slot, DUOS - 4, DUOS - 2)
            window.load(sp, y_stored[0])
            slot(DUOS - 1)

        @block.gpsimd
        def _(pool):
            pool.memset(ident[:], 0.0).then_inc(const_step, 1)
            pool.memset(causal[:], 0.0).then_inc(const_step, 1)
            pool.memset(head_of[:], 1.0).then_inc(const_step, 1)
            pool.memset(pow_half[:], -0.5).then_inc(pow_ready, 1)
            pool.memset(eps[:], LN_EPS).then_inc(pow_ready, 1)
            pool.wait_ge(const_step, 3)
            pool.affine_select(out=ident[:], in_=ident[:], compare_op=ALU.not_equal, fill=1.0, base=0,
                               pattern=[[-1, P]], channel_multiplier=1).then_inc(const_step, 1)
            for b in range(2):
                half = causal[b * SEQ:(b + 1) * SEQ, :]
                pool.wait_ge(const_step, 4 + b)
                pool.affine_select(out=half, in_=half, compare_op=ALU.is_ge, fill=MASKED, base=0,
                                   pattern=[[-1, SEQ]], channel_multiplier=1).then_inc(const_step, 1)
            pool.wait_ge(const_step, 6)
            pool.affine_select(out=head_of[:], in_=head_of[:], compare_op=ALU.is_ge, fill=0.0, base=0,
                               pattern=[[-HD, GH]], channel_multiplier=1).then_inc(const_step, 1)
            pool.wait_ge(const_step, 7)
            pool.affine_select(out=head_of[:], in_=head_of[:], compare_op=ALU.is_ge, fill=0.0, base=HD - 1,
                               pattern=[[HD, GH]], channel_multiplier=-1).then_inc(const_step, 1)
            pool.tensor_copy(ident_b[:], ident[:]).then_inc(const_step, 1)

            def rstd_of(m):
                wait(pool, aggr_done, 2 * m + 2)
                pool.tensor_tensor(veps[:], mv[:, :, 1], eps[:], ALU.add).then_inc(veps_done, 1)
                wait(pool, veps_done, m + 1)
                pool.tensor_tensor(rstd[:], veps[:], pow_half[:], ALU.pow).then_inc(rstd_done, 1)

            def bias_residual(m, p):
                wait(pool, res_loaded[p], 16 * m + 16)
                wait(pool, bias_loaded, 64)
                pool.tensor_tensor(xres[:, p, :], xres[:, p, :], bo_row[:], ALU.add).then_inc(res_biased[p], 1)

            def key_low(m):
                wait(pool, khi_ready, m + 1)
                if not (isinstance(m, int) and m == 0):
                    wait(pool, kbd_act, 2 * m)
                    wait(pool, kbd_dve, 2 * m)
                pool.tensor_tensor(kT_lo[:], kT[:], kT_hi[:].bitcast(F32), ALU.subtract).then_inc(klo_ready, 1)

            def query_low(m, c):
                wait(pool, qhi_ready, 4 * m + c + 1)
                pool.tensor_tensor(qz[1][:, :, c, 0:4:3, :], qT[:, c, :].rearrange("p (a b t) -> p a b t", a=2, b=2),
                                   qz[0][:, :, c, 0:4:3, :].bitcast(F32), ALU.subtract).then_inc(qlo_ready, 1)

            def normalise(m, p, g):
                wait(pool, rs_ready, 8 * m + 4 * p + g + 1)
                pool.tensor_tensor(prob[:, g], prob[:, g], rs[:, g].unsqueeze(2).to_broadcast([P, GH, SEQ]),
                                   ALU.mult).then_inc(prob_ready, 1)

            pool.wait_ge(pow_ready, 2)
            rstd_of(0)
            pool.memset(vbd[:], 0.0).then_inc(zeros_ready, 1)
            rstd_of(1)
            key_low(0)
            for c in range(4):
                query_low(0, c)

            def slot(d):
                more = not isinstance(d, int) or d < DUOS - 1
                bias_residual(d, 0)
                for g in range(4):
                    normalise(d, 0, g)
                if more:
                    key_low(d + 1)
                for g in range(3):
                    normalise(d, 1, g)
                bias_residual(d, 1)
                normalise(d, 1, 3)
                if not isinstance(d, int) or d < DUOS - 2:
                    rstd_of(d + 2)
                if more:
                    for c in range(4):
                        query_low(d + 1, c)

            steps(pool, slot, DUOS - 3, DUOS - 1)

        @block.scalar
        def _(act):
            def x_hi(m, p):
                work.wait_full(act, f"X{p}", m)
                act.activation(xT[0][:, :, p * P:(p + 1) * P], work.tile(f"X{p}")[:].rearrange("p (k t) -> p k t", k=KC),
                               ACT.Copy).then_inc(xhi_ready, 1)

            def split_weight(n):
                name = "kqvo"[n]
                wait(act, w_loaded[n % 2], 16 * (n // 2) + 16)
                act.activation(w_hl[name][0][:], stage[n % 2][:], ACT.Copy).then_inc(w_hi, 1)

            split_weight(0)
            for p in range(2):
                x_hi(0, p)
            for n in range(1, 3):
                split_weight(n)
            act.wait_ge(bias_loaded, 64)
            act.activation(bq_col[:], bq_col[:], ACT.Copy, scale=HD ** -0.5).then_inc(bias_scaled, 1)
            act.wait_ge(zeros_ready, 3)

            def k_out(m, c):
                if c == 0:
                    wait(act, klo_ready, m)
                work.wait_full(act, f"K{c}", m)
                act.activation(kT[:, c, :], work.tile(f"K{c}")[:, 0:2 * P], ACT.Identity,
                               bias=bk_col[:, c:c + 1]).then_inc(work.freed_sem(f"K{c}"), 1)

            def q_out(m, c):
                work.wait_full(act, f"Q{c}", m)
                act.wait_ge(bias_scaled, 1)
                if c == 0:
                    wait(act, qlo_ready, 4 * m)
                act.activation(qT[:, c, :], work.tile(f"Q{c}")[:, 0:2 * P], ACT.Identity,
                               bias=bq_col[:, c:c + 1], scale=HD ** -0.5).then_inc(work.freed_sem(f"Q{c}"), 1)

            def query_high(m, c):
                work.wait_read(act, f"Q{c}", m)
                act.activation(qz[0][:, :, c, 0:4:3, :], qT[:, c, :].rearrange("p (a b t) -> p a b t", a=2, b=2),
                               ACT.Copy).then_inc(qhi_ready, 1)

            def key_high(m):
                work.wait_read(act, "K3", m)
                wait(act, kbd_dve, 2 * m)
                act.activation(kT_hi[:], kT[:], ACT.Copy).then_inc(khi_ready, 1)

            def spread_low(m, p, heads=range(DVE_HEADS, GH)):
                if heads[0] == DVE_HEADS:
                    wait(act, klo_ready, m + 1)
                    if not (isinstance(m, int) and m == 0 and p == 0):
                        wait(act, score_full[3], 2 * m + p)
                for h in heads:
                    ins = act.activation(kbd[1][:, :, :, h, :],
                                         kT_lo[:, :, p * P:(p + 1) * P].rearrange("p g (b t) -> p g b t", b=2),
                                         ACT.Copy, scale=head_of[:, h:h + 1])
                if heads[-1] == GH - 1:
                    ins.then_inc(kbd_act, 1)

            def exp(m, p, g):
                wait(act, score_freed[g], 2 * m + p + 1)
                act.activation(prob[:, g], prob[:, g], ACT.Exp).then_inc(exp_done, 1)

            def probT_out(m, p, g):
                u = f"P{p}{g}"
                work.wait_full(act, u, m)
                if isinstance(m, int) and m == 0:
                    act.wait_ge(w_lo, 4)
                act.activation(probT[:, g], work.tile(u)[:].rearrange("p (j t) -> p j t", j=4), ACT.Copy)\
                   .then_inc(work.freed_sem(u), 1)

            def o_hi(m, p):
                work.wait_full(act, f"O{p}", m)
                act.activation(oT[0][:], work.tile(f"O{p}")[:].rearrange("p (g t) -> p g t", g=4), ACT.Copy)\
                   .then_inc(ohi_ready, 1)

            for c in range(4):
                k_out(0, c)
            key_high(0)
            for c in range(4):
                q_out(0, c)
            for c in range(4):
                query_high(0, c)
            act.wait_ge(const_step, 9)
            spread_low(0, 0)
            split_weight(3)

            def slot(d):
                more = not isinstance(d, int) or d < DUOS - 1
                if more:
                    for p in range(2):
                        x_hi(d + 1, p)
                for g in range(3):
                    exp(d, 0, g)
                spread_low(d, 1, range(DVE_HEADS, 5))
                if more:
                    k_out(d + 1, 0)
                exp(d, 0, 3)
                if more:
                    k_out(d + 1, 1)
                spread_low(d, 1, range(5, 7))
                if more:
                    k_out(d + 1, 2)
                spread_low(d, 1, range(7, GH))
                if more:
                    k_out(d + 1, 3)
                for g in range(4):
                    probT_out(d, 0, g)
                if more:
                    key_high(d + 1)
                o_hi(d, 0)
                for g in range(3):
                    exp(d, 1, g)
                if more:
                    q_out(d + 1, 0)
                exp(d, 1, 3)
                if more:
                    for c in range(1, 4):
                        q_out(d + 1, c)
                    for c in range(4):
                        query_high(d + 1, c)
                    spread_low(d + 1, 0)
                for g in range(4):
                    probT_out(d, 1, g)
                o_hi(d, 1)

            steps(act, slot, DUOS - 2, DUOS - 1)

        @block.vector
        def _(dve):
            def layernorm(m):
                wait(dve, x_loaded, 16 * m + 16)
                for p in range(2):
                    dve.bn_stats(stats[:, p, :], xin[:, p, :]).then_inc(stats_done, 1)
                wait(dve, stats_done, 2 * m + 2)
                dve.memset(carrier[:, 0:1], 0.0)
                for p in range(2):
                    dve.bn_aggr(mv[:, p, :], stats[:, p, :]).then_inc(aggr_done, 1)

            def apply_norm(m):
                wait(dve, rstd_done, m + 1)
                wait(dve, xhi_ready, 2 * m)
                for p in range(2):
                    dve.tensor_scalar(xln[:, p, :], xin[:, p, :], mv[:, p, 0:1], rstd[:, p:p + 1],
                                      ALU.subtract, ALU.mult).then_inc(xln_ready, 1)

            def x_lo(m, p):
                wait(dve, xhi_ready, 2 * m + p + 1)
                dve.tensor_tensor(xT[1][:, :, p * P:(p + 1) * P], work.tile(f"X{p}")[:].rearrange("p (k t) -> p k t", k=KC),
                                  xT[0][:, :, p * P:(p + 1) * P].bitcast(F32), ALU.subtract)\
                   .then_inc(work.freed_sem(f"X{p}"), 1)

            def spread_high(m, p):
                if p == 0:
                    wait(dve, khi_ready, m + 1)
                if not (isinstance(m, int) and m == 0 and p == 0):
                    wait(dve, score_full[3], 2 * m + p)
                for h in range(GH):
                    ins = dve.tensor_scalar(kbd[0][:, :, :, h, :],
                                            kT_hi[:, :, p * P:(p + 1) * P].bitcast(F32)
                                            .rearrange("p g (b t) -> p g b t", b=2),
                                            head_of[:, h:h + 1], None, ALU.mult)
                if p == 0:
                    wait(dve, klo_ready, m + 1)
                for h in range(DVE_HEADS):
                    ins = dve.tensor_scalar(kbd[1][:, :, :, h, :],
                                            kT_lo[:, :, p * P:(p + 1) * P].rearrange("p g (b t) -> p g b t", b=2),
                                            head_of[:, h:h + 1], None, ALU.mult)
                ins.then_inc(kbd_dve, 1)

            def values_out(m, p):
                u = f"V{p}"
                work.wait_full(dve, u, m)
                for b in range(2):
                    for par in range(2):
                        cols = slice(b * SEQ, (b + 1) * SEQ)
                        ins = dve.tensor_tensor(
                            vbd[par * SEQ:(par + 1) * SEQ, p, b, :, par, :],
                            work.tile(u)[cols, :].rearrange("p (j r d) -> p j r d", r=2, d=HD)[:, :, par, :],
                            bv_row[cols, :].rearrange("p (j r d) -> p j r d", r=2, d=HD)[:, :, par, :], ALU.add)
                ins.then_inc(work.freed_sem(u), 1)

            def less_max(m, p, g):
                n = 8 * m + 4 * p + g + 1
                wait(dve, score_full[g], 2 * m + p + 1)
                s = score[g][:].rearrange("p (h k) -> p h k", h=GH)
                dve.tensor_reduce(mx[:, g, :], s, AX_X, ALU.max).then_inc(mx_ready, 1)
                wait(dve, mx_ready, n)
                dve.tensor_tensor(prob[:, g], s, mx[:, g].unsqueeze(2).to_broadcast([P, GH, SEQ]),
                                  ALU.subtract).then_inc(score_freed[g], 1)

            def row_sum(m, p, g):
                n = 8 * m + 4 * p + g + 1
                wait(dve, exp_done, n)
                dve.tensor_reduce(sm[:, g, :], prob[:, g], AX_X, ALU.add).then_inc(sum_done, 1)
                wait(dve, sum_done, n)
                dve.reciprocal(rs[:, g, :], sm[:, g, :]).then_inc(rs_ready, 1)

            def o_lo(m, p):
                wait(dve, ohi_ready, 2 * m + p + 1)
                dve.tensor_tensor(oT[1][:], work.tile(f"O{p}")[:].rearrange("p (g t) -> p g t", g=4),
                                  oT[0][:].bitcast(F32), ALU.subtract).then_inc(work.freed_sem(f"O{p}"), 1)

            def y_out(m, p):
                u = f"Y{p}"
                work.wait_full(dve, u, m)
                wait(dve, res_biased[p], m + 1)
                wait(dve, y_stored[p], 16 * m)
                dve.tensor_tensor(yo[:, p, :], work.tile(u)[:], xres[:, p, :], ALU.add).then_inc(work.freed_sem(u), 1)

            layernorm(0)
            apply_norm(0)

            def split_low(n):
                name = "kqvo"[n]
                wait(dve, w_hi, n + 1)
                dve.tensor_tensor(w_hl[name][1][:], stage[n % 2][:], w_hl[name][0][:].bitcast(F32),
                                  ALU.subtract).then_inc(w_lo, 1)

            split_low(0)
            for p in range(2):
                x_lo(0, p)
            split_low(1)
            dve.wait_ge(zeros_ready, 1)
            for part in qz:
                dve.tensor_copy(part[:].rearrange("p a g b t -> p (a g b t)"),
                                vbd[:].rearrange("p a b j r d -> p (a b j r d)")).then_inc(zeros_ready, 1)
            split_low(2)
            layernorm(1)
            apply_norm(1)
            dve.wait_ge(const_step, 9)
            spread_high(0, 0)
            dve.wait_ge(bias_loaded, 64)
            dve.wait_ge(zeros_ready, 3)
            for p in range(2):
                values_out(0, p)
            split_low(3)

            def slot(d):
                more = not isinstance(d, int) or d < DUOS - 1
                if more:
                    for p in range(2):
                        x_lo(d + 1, p)
                less_max(d, 0, 0)
                less_max(d, 0, 1)
                less_max(d, 0, 2)
                row_sum(d, 0, 0)
                less_max(d, 0, 3)
                row_sum(d, 0, 1)
                row_sum(d, 0, 2)
                row_sum(d, 0, 3)
                spread_high(d, 1)
                o_lo(d, 0)
                less_max(d, 1, 0)
                less_max(d, 1, 1)
                row_sum(d, 1, 0)
                less_max(d, 1, 2)
                row_sum(d, 1, 1)
                less_max(d, 1, 3)
                if not isinstance(d, int) or d < DUOS - 2:
                    layernorm(d + 2)
                row_sum(d, 1, 2)
                row_sum(d, 1, 3)
                if more:
                    spread_high(d + 1, 0)
                y_out(d, 0)
                if more:
                    values_out(d + 1, 0)
                if not isinstance(d, int) or d < DUOS - 2:
                    apply_norm(d + 2)
                o_lo(d, 1)
                if more:
                    values_out(d + 1, 1)
                y_out(d, 1)

            steps(dve, slot, DUOS - 3, DUOS - 1)

        @block.tensor
        def _(pe):
            def x_transposes(m, p):
                u = f"X{p}"
                wait(pe, xln_ready, 2 * m + p + 1)
                work.wait_free(pe, u, m)
                for c in range(KC):
                    ins = pe.transpose(work.tile(u)[:, c * P:(c + 1) * P], xln[:, p, c * P:(c + 1) * P], ident[:])
                ins.then_inc(work.full_sem(u), 1)

            def transposed(m, name, c):
                u = f"{name}{c}"
                if c == 0:
                    work.wait_read(pe, "X0", m)
                    work.wait_read(pe, "X1", m)
                work.wait_free(pe, u, m)
                w = w_hl[name.lower()]
                split3(pe, work.tile(u)[:, 0:2 * P], lambda a, k: w[a][:, k, c * P:(c + 1) * P],
                       lambda b, k: xT[b][:, k, :], KC).then_inc(work.full_sem(u), 1)

            def values(m, p):
                u = f"V{p}"
                work.wait_free(pe, u, m)
                split3(pe, work.tile(u)[:], lambda a, k: xT[a][:, k, p * P:(p + 1) * P],
                       lambda b, k: w_hl["v"][b][:, k, :], KC).then_inc(work.full_sem(u), 1)

            def scores(m, p):
                wait(pe, kbd_dve, 2 * m + p + 1)
                wait(pe, kbd_act, 2 * m + p + 1)
                wait(pe, qlo_ready, 4 * m + 4)
                for g in range(4):
                    wait(pe, score_freed[g], 2 * m + p)
                    pe.matmul(score[g][:], ident_b[:], causal[:].unsqueeze(1).to_broadcast([P, GH, SEQ]),
                              start=True, stop=False)
                    ins = split3(pe, score[g][:], lambda a, b: qz[a][:, p, g, 2 * b:2 * b + 2, :],
                                 lambda a, b: kbd[a][:, g, b, :, :], 2, start=False)
                    ins.then_inc(score_full[g], 1)

            def prob_transposes(m, p, g):
                u = f"P{p}{g}"
                wait(pe, prob_ready, 8 * m + 4 * p + g + 1)
                work.wait_free(pe, u, m)
                for j in range(4):
                    ins = pe.transpose(work.tile(u)[:, j * P:(j + 1) * P], prob[:, g, 2 * j:2 * j + 2, :], ident[:])
                ins.then_inc(work.full_sem(u), 1)

            def attend(m, p):
                u = f"O{p}"
                work.wait_free(pe, u, m)
                work.wait_read(pe, f"V{p}", m)
                for g in range(4):
                    work.wait_read(pe, f"P{p}{g}", m)
                    for j in range(4):
                        for b in range(2):
                            at = g * P + b * SEQ
                            ins = pe.matmul(work.tile(u)[32 * j:32 * j + 32, at:at + SEQ],
                                            vbd[:, p, b, 4 * g + j, :, :],
                                            probT[:, g, j, b * SEQ:(b + 1) * SEQ], start=True, stop=True)
                ins.then_inc(work.full_sem(u), 1)

            def out_projection(m, p):
                u = f"Y{p}"
                work.wait_read(pe, f"O{p}", m)
                if isinstance(m, int):
                    pe.wait_ge(w_lo, 4)
                work.wait_free(pe, u, m)
                split3(pe, work.tile(u)[:], lambda a, k: oT[a][:, k, :],
                       lambda b, k: w_hl["o"][b][:, k, :], KC).then_inc(work.full_sem(u), 1)

            pe.wait_ge(const_step, 9)
            for p in range(2):
                x_transposes(0, p)
            wait(pe, w_lo, 1)
            for c in range(4):
                transposed(0, "K", c)
            wait(pe, w_lo, 2)
            for c in range(4):
                transposed(0, "Q", c)
            wait(pe, w_lo, 3)
            for p in range(2):
                values(0, p)

            def slot(d):
                more = not isinstance(d, int) or d < DUOS - 1
                if more:
                    for p in range(2):
                        x_transposes(d + 1, p)
                scores(d, 0)
                if more:
                    for c in range(4):
                        transposed(d + 1, "K", c)
                for g in range(4):
                    prob_transposes(d, 0, g)
                attend(d, 0)
                scores(d, 1)
                if more:
                    for c in range(4):
                        transposed(d + 1, "Q", c)
                out_projection(d, 0)
                if more:
                    values(d + 1, 0)
                for g in range(4):
                    prob_transposes(d, 1, g)
                attend(d, 1)
                if more:
                    values(d + 1, 1)
                out_projection(d, 1)

            steps(pe, slot, DUOS - 2, DUOS - 1)


class WindowInputs:

    def __init__(self, nc, ctx, x, cond, w_four, b_four):
        def sb(name, shape):
            return ctx.enter_context(nc.sbuf_tensor(f"b_{name}", shape, F32))

        def sem(name):
            return ctx.enter_context(nc.semaphore(f"b_{name}"))

        self.sources = x.rearrange("(n t) f -> n t f", t=P)[0], cond.rearrange("(n t) f -> n t f", t=P)[0], w_four, b_four
        self.xin, self.cin = sb("xin", [P, DIM]), sb("cin", [P, DIM])
        self.w, self.bias = sb("w", [P, 4, P]), sb("bias", [P, 4])
        self.x_loaded, self.c_loaded, self.w_loaded, self.bias_loaded = (
            sem("x_loaded"), sem("c_loaded"), sem("w_loaded"), sem("bias_loaded"))

    def load(self, sp, stored):
        x, cond, w, bias = self.sources
        sp.wait_ge(stored, 16)
        sp.dma_start(self.xin[:], x).then_inc(self.x_loaded, 16)
        sp.dma_start(self.w[:], w).then_inc(self.w_loaded, 16)
        sp.dma_start(self.cin[:], cond).then_inc(self.c_loaded, 16)
        sp.dma_start(self.bias[:], bias).then_inc(self.bias_loaded, 16)


def window_phase(nc, psum, x, cond, inputs, x_stored, y, out, early):
    x_t, c_t, y_t = (a.rearrange("(n t) f -> n t f", t=P) for a in (x, cond, y))
    LAST = PAIRS - 1
    with ExitStack() as ctx:
        def sb(name, shape, dt=F32):
            return ctx.enter_context(nc.sbuf_tensor(f"b_{name}", shape, dt))

        def sem(name):
            return ctx.enter_context(nc.semaphore(f"b_{name}"))

        w_sb, b_sb, xin, cin = inputs.w, inputs.bias, inputs.xin, inputs.cin
        w_two = {n: w_sb[:, i, :] for i, n in enumerate("qkvo")}
        bias = {n: b_sb[:, i:i + 1] for i, n in enumerate("qkvo")}
        ident = sb("ident", [P, P])
        head_sum = sb("head_sum", [P, 2 * HALF - 1, BH])
        pick_f = sb("pick_f", [P, QUAD, P])
        pick = sb("pick", [P, QUAD, P], F32R)
        pow_half, eps = sb("pow_half", [P, 1]), sb("eps", [P, 1])
        carrier, first = sb("carrier", [P, 1]), sb("first", [P, 1])
        cin_v, xres = sb("cin_v", [P, DIM]), sb("xres", [P, DIM])
        stats, mv = sb("stats", [P, 6]), sb("mv", [P, 2])
        veps, rstd, shift, minus = (sb(n, [P, 1]) for n in ("veps", "rstd", "shift", "minus"))
        xln, q = sb("xln", [P, DIM]), sb("q", [P, DIM])
        kpad, vpad = sb("kpad", [P, DIM + WIN]), sb("vpad", [P, DIM + WIN])
        prod = sb("prod", [P, WIN, DIM])
        dots = sb("dots", [P, 2, DIM])
        prob = sb("prob", [P, 2, 2, WIN, BH])
        mx, sm, rs = (sb(n, [P, 2, 2, BH]) for n in ("mx", "sm", "rs"))
        probT = sb("probT", [P, WIN // QUAD, DIM], F32R)
        pv = sb("pv", [P, WIN, DIM])
        yo, y_stored = out.rows[:, 0, :], out.stored[0]

        dots_bank, spread_bank, y_bank = psum[0:2], psum[2:4], psum[4]
        work = Banks(nc, ctx, "b_work", psum[5:8],
                     {"Q": 0, "K": 1, "T0": 2, "T1": 0, "V": 1, "R0": 0, "R1": 2},
                     {"Q": 2, "K": 2, "T0": 1, "T1": 1, "V": 1, "R0": 1, "R1": 1}, LAST)

        w_loaded, bias_loaded, x_loaded, c_loaded = (
            inputs.w_loaded, inputs.bias_loaded, inputs.x_loaded, inputs.c_loaded)
        const_step, const_ready, pad_zeroed = sem("const_step"), sem("const_ready"), sem("pad_zeroed")
        pow_ready = sem("pow_ready")
        cv_loaded, res_loaded = sem("cv_loaded"), sem("res_loaded")
        stats_done, aggr_done, veps_done, rstd_done = sem("stats_done"), sem("aggr_done"), sem("veps_done"), sem("rstd_done")
        xln_ready = sem("xln_ready")
        prod_dve, prod_pool = sem("prod_dve"), sem("prod_pool")
        summed = sem("summed")
        dots_out = [sem(f"dots_out{h}") for h in range(2)]
        mx_ready, exp_done, sum_done, rs_ready, prob_ready = (
            sem(n) for n in ("mx_ready", "exp_done", "sum_done", "rs_ready", "prob_ready"))
        phi_ready, plo_ready = sem("phi_ready"), sem("plo_ready")
        spread_full = [sem(f"spread_full{i}") for i in range(2)]
        pv_ready = [sem(f"pv_ready{i}") for i in range(2)]
        pairs_added, fours_added = sem("pairs_added"), sem("fours_added")
        y_full, y_ready = sem("y_full"), sem("y_ready")

        SUM_AHEAD, PROD_AHEAD = WIN + 10, WIN + 14

        def real(m):
            return not isinstance(m, int) or 0 <= m <= LAST

        def spread_tile(i, w):
            if isinstance(i, int) and i == LAST:
                return (spread_bank + [work.tile("R0"), work.tile("V")])[w % 4]
            return spread_bank[w % 2]

        def ahead(i, w, by):
            return i + (w + by) // WIN, (w + by) % WIN

        block = ctx.enter_context(nc.Block())

        @block.sync
        def _(sp):
            sp.dma_start(cin_v[:], c_t[0]).then_inc(cv_loaded, 16)
            for stored in x_stored:
                sp.wait_ge(stored, 16 * DUOS)
            sp.dma_start(xres[:], x_t[0]).then_inc(res_loaded, 16)

            def slot(i):
                if not isinstance(i, int) or 1 <= i + 4 <= LAST:
                    wait(sp, xln_ready, i + 4)
                    sp.dma_start(xin[:], x_t[i + 4]).then_inc(x_loaded, 16)
                if not isinstance(i, int) or 1 <= i + 3 <= LAST:
                    work.wait_full(sp, "K", i + 2)
                    sp.dma_start(cin[:], c_t[i + 3]).then_inc(c_loaded, 16)
                if real(i - 1):
                    wait(sp, y_ready, i)
                    sp.dma_start(y_t[i - 1], yo).then_inc(y_stored, 16)
                    if real(i):
                        sp.dma_start(xres[:], x_t[i]).then_inc(res_loaded, 16)
                if not isinstance(i, int) or 1 <= i + 2 <= LAST:
                    work.wait_full(sp, "V", i + 1)
                    sp.dma_start(cin_v[:], c_t[i + 2]).then_inc(cv_loaded, 16)
                if isinstance(i, int) and i == -1:
                    early.load_up(sp, 0)
                    early.load_latent(sp)
                if isinstance(i, int) and i == 1:
                    early.load_up(sp, 1)

            steps(sp, slot, LAST - 4, LAST, first=-3, first_full=2)
            early.load_rows(sp, y_stored)
            slot(LAST + 1)

        def add_norm_pool(pool, m):
            wait(pool, aggr_done, m + 1)
            pool.tensor_tensor(veps[:], mv[:, 1:2], eps[:], ALU.add).then_inc(veps_done, 1)
            wait(pool, veps_done, m + 1)
            pool.tensor_tensor(rstd[:], veps[:], pow_half[:], ALU.pow).then_inc(rstd_done, 1)
            wait(pool, rstd_done, 3 * m + 1)
            pool.tensor_tensor(shift[:], mv[:, 0:1], rstd[:], ALU.mult).then_inc(rstd_done, 1)
            wait(pool, rstd_done, 3 * m + 2)
            pool.tensor_tensor(shift[:], shift[:], minus[:], ALU.mult).then_inc(rstd_done, 1)

        def product(eng, m, w, done):
            if w < 2:
                work.wait_read(eng, "Q", m)
                work.wait_read(eng, "K", m)
                eng.wait_ge(pad_zeroed, 2)
            if not (isinstance(m, int) and m == 0):
                wait(eng, summed, WIN * m - WIN + w + 1)
            eng.tensor_tensor(prod[:, w, :], q[:], kpad[:, w:w + DIM], ALU.mult).then_inc(done, 1)

        @block.gpsimd
        def _(pool):
            pool.memset(pow_half[:], -0.5).then_inc(pow_ready, 1)
            pool.memset(eps[:], LN_EPS).then_inc(pow_ready, 1)
            pool.memset(minus[:], -1.0).then_inc(pow_ready, 1)
            pool.memset(ident[:], 0.0).then_inc(const_step, 1)
            pool.memset(head_sum[:], 0.0).then_inc(const_step, 1)
            pool.memset(pick_f[:], 0.0).then_inc(const_step, 1)
            pool.wait_ge(const_step, 3)
            pool.memset(head_sum[:, HALF - 1, :], 1.0).then_inc(const_step, 1)
            pool.wait_ge(const_step, 4)
            pool.wait_ge(pow_ready, 3)
            add_norm_pool(pool, 0)
            pool.affine_select(out=ident[:], in_=ident[:], compare_op=ALU.not_equal, fill=1.0, base=0,
                               pattern=[[-1, P]], channel_multiplier=1).then_inc(const_step, 1)
            mid = head_sum[:, HALF - 1, :]
            pool.affine_select(out=mid, in_=mid, compare_op=ALU.is_ge, fill=0.0, base=0,
                               pattern=[[-XHD, BH]], channel_multiplier=1).then_inc(const_step, 1)
            pool.wait_ge(const_step, 6)
            pool.affine_select(out=mid, in_=mid, compare_op=ALU.is_ge, fill=0.0, base=XHD - 1,
                               pattern=[[XHD, BH]], channel_multiplier=-1).then_inc(const_step, 1)
            sel = pick_f[:].rearrange("p w (h d) -> p w h d", d=XHD)
            for part in range(2):
                if part:
                    pool.wait_ge(const_step, 8)
                pool.affine_select(out=sel, in_=sel, compare_op=ALU.not_equal, fill=1.0, base=-part * SEQ,
                                   pattern=[[-BH, QUAD], [-1, BH], [0, XHD]], channel_multiplier=1)\
                    .then_inc(const_step, 1)

            def normalise(m, a):
                wait(pool, rs_ready, 2 * m + a + 1)
                pool.tensor_tensor(prob[:, a], prob[:, a],
                                   rs[:, a].unsqueeze(2).to_broadcast([P, 2, WIN, BH]), ALU.mult)\
                    .then_inc(prob_ready, 1)

            def slot(i):
                for w in range(1, WIN, 2):
                    m, at = ahead(i, w, PROD_AHEAD)
                    if real(m):
                        product(pool, m, at, prod_pool)
                    if w in (9, 11) and real(i + 1):
                        normalise(i + 1, (w - 9) // 2)
                    if real(i):
                        for par in range(2):
                            wait(pool, pv_ready[par], 8 * i + w // 2 + 1)
                        pool.tensor_tensor(pv[:, w - 1, :], pv[:, w - 1, :], pv[:, w, :], ALU.add)\
                            .then_inc(pairs_added, 1)
                    if w == 3 and real(i + 3):
                        add_norm_pool(pool, i + 3)
                    if isinstance(i, int) and i == LAST and w <= 2 * KC:
                        early.lat_low(pool, w // 2)

            steps(pool, slot, LAST - 3, LAST, first=-2, first_full=1)

        @block.scalar
        def _(act):
            act.wait_ge(pow_ready, 3)
            act.activation(first[:], eps[:], ACT.Identity)

            def apply_norm(m):
                wait(act, rstd_done, 3 * m + 3)
                if not (isinstance(m, int) and m == 0):
                    work.wait_full(act, "Q", m - 1)
                act.activation(xln[:], xin[:], ACT.Identity, bias=shift[:, 0:1], scale=rstd[:, 0:1])\
                   .then_inc(xln_ready, 1)

            apply_norm(0)
            act.wait_ge(bias_loaded, 16)
            act.wait_ge(pad_zeroed, 2)

            def q_out(m):
                work.wait_full(act, "Q", m)
                wait(act, prod_dve, 8 * m)
                wait(act, prod_pool, 8 * m)
                act.activation(q[:], work.tile("Q")[:], ACT.Identity, bias=bias["q"])\
                   .then_inc(work.freed_sem("Q"), 1)

            def k_out(m):
                work.wait_full(act, "K", m)
                act.activation(kpad[:, PADL:PADL + DIM], work.tile("K")[:], ACT.Identity, bias=bias["k"])\
                   .then_inc(work.freed_sem("K"), 1)

            def v_out(m):
                work.wait_full(act, "V", m)
                for par in range(2):
                    wait(act, pv_ready[par], 8 * m)
                act.activation(vpad[:, PADL:PADL + DIM], work.tile("V")[:], ACT.Identity, bias=bias["v"])\
                   .then_inc(work.freed_sem("V"), 1)

            def dots_to_sbuf(m, h):
                wait(act, summed, WIN * m + HALF * (h + 1))
                act.activation(dots[:, h, :], dots_bank[h][:], ACT.Copy).then_inc(dots_out[h], 1)

            def exp(m):
                for a in range(2):
                    work.wait_read(act, f"T{a}", m)
                    act.activation(prob[:, a], prob[:, a], ACT.Exp, scale=XHD ** -0.5).then_inc(exp_done, 1)

            def prob_hi(m, q):
                u, rows = f"R{q // 2}", slice(q % 2 * SEQ, (q % 2 + 1) * SEQ)
                work.wait_full(act, u, m)
                act.activation(probT[rows, q, :], work.tile(u)[rows, :], ACT.Copy).then_inc(phi_ready, 1)

            def slot(i):
                if real(i + 1):
                    dots_to_sbuf(i + 1, 0)
                if real(i + 2):
                    q_out(i + 2)
                    k_out(i + 2)
                if isinstance(i, int) and i == -2:
                    act.wait_ge(const_step, 9)
                    act.activation(pick[:], pick_f[:], ACT.Copy).then_inc(const_ready, 1)
                if isinstance(i, int) and i in (0, LAST - 1):
                    for k in range(KC // 2):
                        early.up_high(act, k + (KC // 2 if i else 0))
                if real(i + 1):
                    dots_to_sbuf(i + 1, 1)
                if real(i + 3):
                    apply_norm(i + 3)
                if real(i + 1):
                    exp(i + 1)
                    if isinstance(i, int) and i == LAST - 1:
                        for c in range(LC):
                            early.tail_to_sbuf(act, c)
                    for q in range(WIN // QUAD):
                        prob_hi(i + 1, q)
                    v_out(i + 1)

            steps(act, slot, LAST - 3, LAST, first=-2, first_full=1)
            for c in range(KC):
                early.lat_high(act, c)

        @block.vector
        def _(dve):
            def layernorm(m):
                wait(dve, x_loaded, 16 * m + 16)
                dve.bn_stats(stats[:], xin[:]).then_inc(stats_done, 1)
                wait(dve, stats_done, m + 1)
                dve.memset(carrier[:], 0.0)
                dve.bn_aggr(mv[:], stats[:]).then_inc(aggr_done, 1)

            def less_max(m, a):
                u = f"T{a}"
                work.wait_full(dve, u, m)
                s = work.tile(u)[:].rearrange("p (t w b) -> p t w b", t=2, w=WIN)
                dve.tensor_reduce(mx[:, a], s.transpose([0, 1, 3, 2]), AX_X, ALU.max).then_inc(mx_ready, 1)
                wait(dve, mx_ready, 2 * m + a + 1)
                dve.tensor_tensor(prob[:, a], s, mx[:, a].unsqueeze(2).to_broadcast([P, 2, WIN, BH]), ALU.subtract)\
                   .then_inc(work.freed_sem(u), 1)

            def row_sum(m, a):
                wait(dve, exp_done, 2 * m + a + 1)
                dve.tensor_reduce(sm[:, a], prob[:, a].transpose([0, 1, 3, 2]), AX_X, ALU.add).then_inc(sum_done, 1)
                wait(dve, sum_done, 2 * m + a + 1)
                dve.reciprocal(rs[:, a], sm[:, a]).then_inc(rs_ready, 1)

            def prob_lo(m, q):
                u, rows = f"R{q // 2}", slice(q % 2 * SEQ, (q % 2 + 1) * SEQ)
                beside = slice((1 - q % 2) * SEQ, (2 - q % 2) * SEQ)
                wait(dve, phi_ready, 4 * m + q + 1)
                ins = dve.tensor_tensor(probT[beside, q, :], work.tile(u)[rows, :], probT[rows, q, :].bitcast(F32),
                                        ALU.subtract)
                ins.then_inc(work.freed_sem(u) if q % 2 else plo_ready, 1)

            def weigh(i, w):
                wait(dve, spread_full[w % 2], 8 * i + w // 2 + 1)
                if w == 0:
                    work.wait_read(dve, "V", i)
                dve.tensor_tensor(pv[:, w, :], spread_tile(i, w)[:], vpad[:, w:w + DIM], ALU.mult)\
                   .then_inc(pv_ready[w % 2], 1)

            def add_fours(i, j):
                wait(dve, pairs_added, 8 * i + 2 * j + 2)
                dve.tensor_tensor(pv[:, 4 * j, :], pv[:, 4 * j, :], pv[:, 4 * j + 2, :], ALU.add).then_inc(fours_added, 1)

            def y_out(i):
                wait(dve, y_full, i + 1)
                wait(dve, res_loaded, 16 * i + 16)
                wait(dve, y_stored, 16 * i)
                dve.scalar_tensor_tensor(yo, y_bank[:], bias["o"], xres[:], ALU.add, ALU.add)\
                   .then_inc(y_ready, 1)

            def slot(i):
                for w in range(WIN):
                    if isinstance(i, int) and i in (1, LAST) and w < KC // 2:
                        early.up_low(dve, w + (KC // 2 if i > 1 else 0))
                    m, at = ahead(i, w, PROD_AHEAD)
                    if w % 2 == 0 and real(m):
                        product(dve, m, at, prod_dve)
                    if w == 15 and real(i + 1):
                        prob_lo(i + 1, 0)
                    if real(i):
                        weigh(i, w)
                    if w in (1, 4) and real(i):
                        prob_lo(i, 2 + w // 4)
                    if w == 1 and real(i - 1):
                        add_fours(i - 1, 3)
                    if w == 1 and real(i + 3):
                        layernorm(i + 3)
                    if w >= 6 and w % 4 == 2 and real(i):
                        add_fours(i, (w - 6) // 4)
                    if w == 7 and real(i - 1):
                        y_out(i - 1)
                    if w == 5 and isinstance(i, int) and i == -3:
                        dve.memset(kpad[:], 0.0).then_inc(pad_zeroed, 1)
                        dve.memset(vpad[:], 0.0).then_inc(pad_zeroed, 1)
                    if w in (8, 9) and real(i + 1):
                        less_max(i + 1, w - 8)
                    if w in (9, 10) and real(i + 1):
                        row_sum(i + 1, w - 9)
                if real(i + 1):
                    prob_lo(i + 1, 1)

            steps(dve, slot, LAST - 3, LAST, first=-3, first_full=2)
            add_fours(LAST, 3)
            y_out(LAST)

        @block.tensor
        def _(pe):
            def pointwise(m, u, rhs):
                work.wait_free(pe, u, m)
                pe.matmul(work.tile(u)[:], w_two[u.lower()], rhs[:], start=True, stop=True)\
                  .then_inc(work.full_sem(u), 1)

            def query_key(m):
                wait(pe, xln_ready, m + 1)
                pointwise(m, "Q", xln)
                wait(pe, c_loaded, 16 * m + 16)
                pointwise(m, "K", cin)

            def value(m):
                wait(pe, cv_loaded, 16 * m + 16)
                pointwise(m, "V", cin_v)

            def head_sums(m, w):
                h, r = w // HALF, w % HALF
                if r == 0:
                    wait(pe, dots_out[h], m)
                if isinstance(m, int) and m == 0:
                    pe.wait_ge(const_step, 7)
                done = prod_pool if w % 2 else prod_dve
                wait(pe, done, 8 * m + w // 2 + 1)
                pe.matmul(dots_bank[h][:], head_sum[:, HALF - 1 - r:2 * HALF - 1 - r, :], prod[:, w, :],
                          start=r == 0, stop=r == HALF - 1).then_inc(summed, 1)

            def turn(m):
                for h in range(2):
                    wait(pe, dots_out[h], m + 1)
                for a in range(2):
                    u = f"T{a}"
                    work.wait_free(pe, u, m)
                    for t in range(2):
                        for h in range(2):
                            ins = pe.transpose(work.tile(u)[:, (2 * t + h) * P:(2 * t + h + 1) * P],
                                               dots[:, h, (2 * a + t) * P:(2 * a + t + 1) * P], ident[:])
                    ins.then_inc(work.full_sem(u), 1)

            def turn_back(m, h):
                wait(pe, prob_ready, 2 * m + 2)
                u = f"R{h}"
                work.wait_free(pe, u, m)
                for a in range(2):
                    for t in range(2):
                        ins = pe.transpose(work.tile(u)[:, (2 * a + t) * P:(2 * a + t + 1) * P],
                                           prob[:, a, t, h * HALF:(h + 1) * HALF, :], ident[:])
                ins.then_inc(work.full_sem(u), 1)

            def spread(i, w):
                q, r = w // QUAD, w % QUAD
                if r == 0:
                    if q % 2:
                        work.wait_read(pe, f"R{q // 2}", i)
                    else:
                        wait(pe, plo_ready, 2 * i + q // 2 + 1)
                    if isinstance(i, int):
                        pe.wait_ge(const_ready, 1)
                four = isinstance(i, int) and i == LAST
                if four and w in (2, 3):
                    work.wait_read(pe, "R0" if w == 2 else "V", i)
                elif four and w >= 4:
                    wait(pe, pv_ready[w % 2], 8 * i + w // 2 - 1)
                else:
                    wait(pe, pv_ready[w % 2], 8 * i + w // 2)
                pe.matmul(spread_tile(i, w)[:], pick[:, r, :], probT[:, q, :], start=True, stop=True)\
                  .then_inc(spread_full[w % 2], 1)

            def project(i, j):
                wait(pe, fours_added, 4 * i + j + 1)
                if j == 0:
                    wait(pe, y_ready, i)
                ins = pe.matmul(y_bank[:], w_two["o"], pv[:, 4 * j, :], start=j == 0, stop=j == 3)
                if j == 3:
                    ins.then_inc(y_full, 1)

            pe.wait_ge(w_loaded, 16)

            def slot(i):
                for w in range(WIN):
                    m, at = ahead(i, w, SUM_AHEAD)
                    if real(m):
                        head_sums(m, at)
                    if w in (0, 4) and real(i - 1):
                        project(i - 1, 2 if w == 0 else 3)
                    if w in (11, 13) and real(i):
                        project(i, 0 if w == 11 else 1)
                    if w == 15 and real(i + 1):
                        turn_back(i + 1, 0)
                    if real(i):
                        spread(i, w)
                    if w == 1 and real(i + 2):
                        query_key(i + 2)
                    if w == 7 and real(i + 1):
                        turn(i + 1)
                    if isinstance(i, int) and i == LAST - 1 and w in (8, 10):
                        early.tail_product(pe, w // 2 - 4)
                    if isinstance(i, int) and (i, w) in ((LAST - 1, 12), (LAST - 1, 14), (LAST, 1), (LAST, 3)):
                        early.lat_product(pe, [12, 14, 1, 3].index(w))
                    if w == 10 and real(i + 1):
                        value(i + 1)
                if real(i + 1):
                    turn_back(i + 1, 1)

            steps(pe, slot, LAST - 2, LAST, first=-2, first_full=2)
            project(LAST, 2)
            project(LAST, 3)


class ExpertWeights:

    def __init__(self, nc, ctx, psum, up, fc1T, expertT, fc2, x):
        def sb(name, shape, dt=F32):
            return ctx.enter_context(nc.sbuf_tensor(f"e_{name}", shape, dt))

        def sem(name):
            return ctx.enter_context(nc.semaphore(f"e_{name}"))

        self.psum, self.x_d = psum, x.rearrange("(d p t) f -> d t p f", p=2, t=P)
        self.sources = [a.rearrange("(k p) n -> p k n", p=P) for a in (expertT, fc2, fc1T, up)]
        self.up_w = [sb(f"up_{s}", [P, KC, INT], F32R) for s in ("hi", "lo")]
        self.lat_w = [sb(f"lat_{s}", [P, KC, DIM], F32R) for s in ("hi", "lo")]
        self.expert_f, self.fc2_f, self.fc1_f = (
            sb("expert_f", [P, LC, LAT]), sb("fc2_f", [P, LC, DIM]), sb("fc1_f", [P, LC, DIM]))
        self.up_f = sb("up_f", [P, KC // 2, INT])
        self.tail_f, self.lat_f = sb("tail_f", [P, LC, DIM]), sb("lat_f", [P, 2, DIM])
        self.xin = sb("xin", [P, 2, DIM])
        self.latent_loaded, self.up_loaded, self.x_loaded = sem("latent_loaded"), sem("up_loaded"), sem("x_loaded")
        self.up_hi, self.up_lo = sem("up_hi"), sem("up_lo")
        self.tail_full, self.tail_out = sem("tail_full"), sem("tail_out")
        self.lat_full, self.lat_out = sem("lat_full"), sem("lat_out")
        self.lat_hi, self.lat_lo = sem("lat_hi"), sem("lat_lo")

    def load_latent(self, sp):
        expert, fc2, fc1, _ = self.sources
        for dst, src in ((self.expert_f, expert), (self.fc2_f, fc2), (self.fc1_f, fc1)):
            sp.dma_start(dst[:], src).then_inc(self.latent_loaded, 16)

    def load_up(self, sp, h):
        k = slice(h * KC // 2, (h + 1) * KC // 2)
        wait(sp, self.up_lo, h * KC // 2)
        sp.dma_start(self.up_f[:], self.sources[3][:, k, :]).then_inc(self.up_loaded, 16)

    def load_rows(self, sp, stored):
        wait(sp, stored, 32)
        sp.dma_start(self.xin[:], self.x_d[0]).then_inc(self.x_loaded, 16)

    def up_high(self, act, k):
        half = KC // 2
        wait(act, self.up_loaded, 16 * (k // half) + 16)
        act.activation(self.up_w[0][:, k, :], self.up_f[:, k % half, :], ACT.Copy).then_inc(self.up_hi, 1)

    def up_low(self, dve, k):
        wait(dve, self.up_hi, k + 1)
        dve.tensor_tensor(self.up_w[1][:, k, :], self.up_f[:, k % (KC // 2), :],
                          self.up_w[0][:, k, :].bitcast(F32), ALU.subtract).then_inc(self.up_lo, 1)

    def tail_product(self, pe, c):
        if c == 0:
            pe.wait_ge(self.latent_loaded, 48)
        for k in range(LC):
            ins = pe.matmul(self.psum[c][:], self.expert_f[:, k, c * P:(c + 1) * P], self.fc2_f[:, k, :],
                            start=k == 0, stop=k == LC - 1)
        ins.then_inc(self.tail_full, 1)

    def tail_to_sbuf(self, act, c):
        wait(act, self.tail_full, c + 1)
        act.activation(self.tail_f[:, c, :], self.psum[c][:], ACT.Copy).then_inc(self.tail_out, 1)

    def lat_product(self, pe, c):
        pe.wait_ge(self.tail_out, LC)
        wait(pe, self.lat_out, c - 1)
        for k in range(LC):
            ins = pe.matmul(self.psum[c % 2][:], self.fc1_f[:, k, c * P:(c + 1) * P], self.tail_f[:, k, :],
                            start=k == 0, stop=k == LC - 1)
        ins.then_inc(self.lat_full, 1)

    def lat_high(self, act, c):
        wait(act, self.lat_full, c + 1)
        wait(act, self.lat_lo, c - 1)
        act.activation(self.lat_f[:, c % 2, :], self.psum[c % 2][:], ACT.Copy).then_inc(self.lat_out, 1)
        wait(act, self.lat_out, c + 1)
        act.activation(self.lat_w[0][:, c, :], self.lat_f[:, c % 2, :], ACT.Copy).then_inc(self.lat_hi, 1)

    def lat_low(self, pool, c):
        wait(pool, self.lat_hi, c + 1)
        pool.tensor_tensor(self.lat_w[1][:, c, :], self.lat_f[:, c % 2, :], self.lat_w[0][:, c, :].bitcast(F32),
                           ALU.subtract).then_inc(self.lat_lo, 1)


def expert_phase(nc, psum, x, x_stored, early, gate, down, gamma, beta, y):
    x_d = x.rearrange("(d p t) f -> d t p f", p=2, t=P)
    y_t = y.rearrange("(n t) f -> n t f", t=P)
    with ExitStack() as ctx:
        def sb(name, shape, dt=F32):
            return ctx.enter_context(nc.sbuf_tensor(f"c_{name}", shape, dt))

        def sem(name):
            return ctx.enter_context(nc.semaphore(f"c_{name}"))

        PARTS = ("hi", "lo")
        up_w, lat_w, xin, x_loaded = early.up_w, early.lat_w, early.xin, early.x_loaded
        down_w = [sb(f"down_{s}", [P, IC, DIM], F32R) for s in PARTS]
        gate_w = [sb(f"gate_{s}", [P, KC, NE], F32R) for s in PARTS]
        DPARTS = 4
        DK = IC // DPARTS
        stage = [sb(f"stage{i}", [P, DK, DIM]) for i in range(DPARTS)]
        gate_f = sb("gate_f", [P, KC, NE])
        gamma_row, beta_row = sb("gamma_row", [P, DIM]), sb("beta_row", [P, DIM])
        ident, pow_half, eps = sb("ident", [P, P]), sb("pow_half", [P, 2]), sb("eps", [P, 2])
        carrier = sb("carrier", [P, 5])
        xres, xln = (sb(n, [P, 2, DIM]) for n in ("xres", "xln"))
        stats, mv = sb("stats", [P, 2, 6]), sb("mv", [P, 2, 2])
        veps, rstd = sb("veps", [P, 2]), sb("rstd", [P, 2])
        xT = [sb(f"xT_{s}", [P, KC, 2 * P], F32R) for s in PARTS]
        relu = sb("relu", [P, 2, 2 * P])
        hidden = sb("hidden", [P, 2, 2 * P])
        hid = [sb(f"hid_{s}", [P, IC, 2 * P], F32R) for s in PARTS]
        logitsT = sb("logitsT", [P, 2 * P])
        top, route = sb("top", [P, 2, NE]), sb("route", [P, 2])
        routed, z = sb("routed", [P, 2, DIM]), sb("z", [P, 2, DIM])
        zstats, zmv = sb("zstats", [P, 2, 6]), sb("zmv", [P, 2, 2])
        zveps, zrstd = sb("zveps", [P, 2]), sb("zrstd", [P, 2])
        yo = sb("yo", [P, 2, DIM])

        bank_of = {f"H{c}": c % 4 for c in range(IC)}
        bank_of.update({"X0": 4, "X1": 5, "G": 0, "R0": 6, "L": 1, "R1": 7, "D0": 2, "D1": 3})
        work = Banks(nc, ctx, "c_work", psum, bank_of, {"X0": 1, "X1": 1}, DUOS - 1)

        const_step = sem("const_step")
        gate_loaded, row_loaded = sem("gate_loaded"), sem("row_loaded")
        stage_loaded = [sem(f"stage_loaded{i}") for i in range(DPARTS)]
        gate_hi, gate_lo, w_hi, w_lo = sem("gate_hi"), sem("gate_lo"), sem("w_hi"), sem("w_lo")
        res_loaded = [sem(f"res_loaded{p}") for p in range(2)]
        res_biased = [sem(f"res_biased{p}") for p in range(2)]
        stats_done, aggr_done, veps_done, rstd_done = sem("stats_done"), sem("aggr_done"), sem("veps_done"), sem("rstd_done")
        xln_ready, xhi_ready = sem("xln_ready"), sem("xhi_ready")
        relu_done = sem("relu_done")
        hhi_ready, hlo_ready = sem("hhi_ready"), sem("hlo_ready")
        top_ready, route_ready = sem("top_ready"), sem("route_ready")
        zstats_done, zaggr_done, zveps_done, zrstd_done = sem("zstats_done"), sem("zaggr_done"), sem("zveps_done"), sem("zrstd_done")
        z_norm, z_scaled = sem("z_norm"), sem("z_scaled")
        y_ready, y_stored = [sem(f"y_ready{p}") for p in range(2)], [sem(f"y_stored{p}") for p in range(2)]

        down_src = down.rearrange("(k p) n -> p k n", p=P)

        block = ctx.enter_context(nc.Block())

        @block.sync
        def _(sp):
            sp.dma_start(gate_f[:], gate.rearrange("(k p) n -> p k n", p=P)).then_inc(gate_loaded, 16)
            sp.wait_ge(x_stored, 16 * PAIRS)
            wait(sp, xln_ready, 2)
            sp.dma_start(xin[:], x_d[1]).then_inc(x_loaded, 16)
            for n in range(DPARTS):
                sp.dma_start(stage[n][:], down_src[:, n * DK:(n + 1) * DK, :]).then_inc(stage_loaded[n], 16)
            sp.dma_start(gamma_row[:], gamma.partition_broadcast(P)).then_inc(row_loaded, 16)
            sp.dma_start(beta_row[:], beta.partition_broadcast(P)).then_inc(row_loaded, 16)
            wait(sp, xln_ready, 4)
            sp.dma_start(xin[:], x_d[2]).then_inc(x_loaded, 16)
            for p in range(2):
                sp.dma_start(xres[:, p, :], x_d[0][:, p, :]).then_inc(res_loaded[p], 16)

            def slot(d):
                if not isinstance(d, int) or d < DUOS - 3:
                    wait(sp, xln_ready, 2 * d + 6)
                    sp.dma_start(xin[:], x_d[d + 3]).then_inc(x_loaded, 16)
                for p in range(2):
                    wait(sp, y_ready[p], d + 1)
                    sp.dma_start(y_t[d * 2 + p], yo[:, p, :]).then_inc(y_stored[p], 16)
                    if not isinstance(d, int) or d < DUOS - 1:
                        sp.dma_start(xres[:, p, :], x_d[d + 1][:, p, :]).then_inc(res_loaded[p], 16)

            steps(sp, slot, DUOS - 4, DUOS - 1)
            for p in range(2):
                sp.wait_ge(y_stored[p], 16 * DUOS)

        @block.gpsimd
        def _(pool):
            pool.memset(pow_half[:], -0.5).then_inc(const_step, 1)
            pool.memset(eps[:], LN_EPS).then_inc(const_step, 1)
            pool.memset(ident[:], 0.0).then_inc(const_step, 1)
            pool.memset(logitsT[:], 0.0).then_inc(const_step, 1)
            pool.wait_ge(const_step, 4)
            pool.affine_select(out=ident[:], in_=ident[:], compare_op=ALU.not_equal, fill=1.0, base=0,
                               pattern=[[-1, P]], channel_multiplier=1).then_inc(const_step, 1)

            def rstd_of(m):
                wait(pool, aggr_done, 2 * m + 2)
                pool.tensor_tensor(veps[:], mv[:, :, 1], eps[:], ALU.add).then_inc(veps_done, 1)
                wait(pool, veps_done, m + 1)
                pool.tensor_tensor(rstd[:], veps[:], pow_half[:], ALU.pow).then_inc(rstd_done, 1)

            def hidden_lo(m, c):
                wait(pool, hhi_ready, 8 * m + c + 1)
                pool.tensor_tensor(hid[1][:, c, :], hidden[:, c % 2, :], hid[0][:, c, :].bitcast(F32), ALU.subtract)\
                    .then_inc(hlo_ready, 1)

            def bias_residual(m, p):
                wait(pool, res_loaded[p], 16 * m + 16)
                wait(pool, row_loaded, 32)
                pool.tensor_tensor(xres[:, p, :], xres[:, p, :], beta_row[:], ALU.add).then_inc(res_biased[p], 1)

            def z_rstd(m, p):
                wait(pool, zaggr_done, 2 * m + p + 1)
                pool.tensor_tensor(zveps[:, p:p + 1], zmv[:, p, 1:2], eps[:, 0:1], ALU.add).then_inc(zveps_done, 1)
                wait(pool, zveps_done, 2 * m + p + 1)
                pool.tensor_tensor(zrstd[:, p:p + 1], zveps[:, p:p + 1], pow_half[:, 0:1], ALU.pow).then_inc(zrstd_done, 1)

            def z_gamma(m, p):
                wait(pool, z_norm, 2 * m + p + 1)
                pool.tensor_tensor(z[:, p, :], z[:, p, :], gamma_row[:], ALU.mult).then_inc(z_scaled, 1)

            rstd_of(0)
            rstd_of(1)

            def slot(d):
                for c in range(IC):
                    hidden_lo(d, c)
                for p in range(2):
                    bias_residual(d, p)
                z_rstd(d, 0)
                z_gamma(d, 0)
                if not isinstance(d, int) or d < DUOS - 2:
                    rstd_of(d + 2)
                z_rstd(d, 1)
                z_gamma(d, 1)

            steps(pool, slot, DUOS - 3, DUOS - 1)

        @block.scalar
        def _(act):
            def x_hi(m, p):
                if not (isinstance(m, int) and m == 0):
                    work.wait_full(act, "R1", m - 1)
                work.wait_full(act, f"X{p}", m)
                act.activation(xT[0][:, :, p * P:(p + 1) * P], work.tile(f"X{p}")[:].rearrange("p (k t) -> p k t", k=KC),
                               ACT.Copy).then_inc(xhi_ready, 1)

            def split_high(n):
                wait(act, stage_loaded[n], 16)
                act.activation(down_w[0][:, n * DK:(n + 1) * DK, :], stage[n][:], ACT.Copy).then_inc(w_hi, 1)

            for p in range(2):
                x_hi(0, p)
            act.wait_ge(gate_loaded, 16)
            act.activation(gate_w[0][:], gate_f[:], ACT.Copy).then_inc(gate_hi, 1)

            def relu_out(m, c):
                work.wait_full(act, f"H{c}", m)
                act.activation(relu[:, c % 2, :], work.tile(f"H{c}")[:, 0:2 * P], ACT.Relu).then_inc(relu_done, 1)

            def hidden_hi(m, c):
                work.wait_read(act, f"H{c}", m)
                act.activation(hid[0][:, c, :], hidden[:, c % 2, :], ACT.Copy).then_inc(hhi_ready, 1)

            def logits_out(m):
                work.wait_full(act, "G", m)
                if isinstance(m, int):
                    act.wait_ge(const_step, 5)
                act.activation(logitsT[0:NE, :], work.tile("G")[0:NE, 0:2 * P], ACT.Copy).then_inc(work.freed_sem("G"), 1)

            def routed_out(m, p):
                work.wait_full(act, f"R{p}", m)
                wait(act, route_ready, m + 1)
                act.activation(routed[:, p, :], work.tile(f"R{p}")[:], ACT.Copy, scale=route[:, p:p + 1])\
                   .then_inc(work.freed_sem(f"R{p}"), 1)

            def slot(d):
                relu_out(d, 0)
                for c in range(1, IC):
                    relu_out(d, c)
                    hidden_hi(d, c - 1)
                    if isinstance(d, int) and d == 0 and c >= IC - DPARTS:
                        split_high(c - IC + DPARTS)
                hidden_hi(d, IC - 1)
                logits_out(d)
                for p in range(2):
                    routed_out(d, p)
                if not isinstance(d, int) or d < DUOS - 1:
                    for p in range(2):
                        x_hi(d + 1, p)

            steps(act, slot, DUOS - 2, DUOS - 1)

        @block.vector
        def _(dve):
            def layernorm(m):
                wait(dve, x_loaded, 16 * m + 16)
                for p in range(2):
                    dve.bn_stats(stats[:, p, :], xin[:, p, :]).then_inc(stats_done, 1)
                wait(dve, stats_done, 2 * m + 2)
                dve.memset(carrier[:, 0:1], 0.0)
                for p in range(2):
                    dve.bn_aggr(mv[:, p, :], stats[:, p, :]).then_inc(aggr_done, 1)

            def apply_norm(m):
                wait(dve, rstd_done, m + 1)
                wait(dve, xhi_ready, 2 * m)
                for p in range(2):
                    dve.tensor_scalar(xln[:, p, :], xin[:, p, :], mv[:, p, 0:1], rstd[:, p:p + 1],
                                      ALU.subtract, ALU.mult).then_inc(xln_ready, 1)

            def x_lo(m, p):
                wait(dve, xhi_ready, 2 * m + p + 1)
                dve.tensor_tensor(xT[1][:, :, p * P:(p + 1) * P], work.tile(f"X{p}")[:].rearrange("p (k t) -> p k t", k=KC),
                                  xT[0][:, :, p * P:(p + 1) * P].bitcast(F32), ALU.subtract)\
                   .then_inc(work.freed_sem(f"X{p}"), 1)

            def split_low(n):
                wait(dve, w_hi, n + 1)
                part = slice(n * DK, (n + 1) * DK)
                dve.tensor_tensor(down_w[1][:, part, :], stage[n][:], down_w[0][:, part, :].bitcast(F32), ALU.subtract)\
                   .then_inc(w_lo, 1)

            layernorm(0)
            apply_norm(0)
            for p in range(2):
                x_lo(0, p)
            wait(dve, gate_hi, 1)
            dve.tensor_tensor(gate_w[1][:], gate_f[:], gate_w[0][:].bitcast(F32), ALU.subtract).then_inc(gate_lo, 1)
            layernorm(1)
            apply_norm(1)

            def square(m, c):
                u = f"H{c}"
                wait(dve, relu_done, 8 * m + c + 1)
                if c >= 2:
                    wait(dve, hlo_ready, 8 * m + c - 1)
                dve.scalar_tensor_tensor(hidden[:, c % 2, :], work.tile(u)[:, 0:2 * P], 0.0, relu[:, c % 2, :],
                                         ALU.max, ALU.mult).then_inc(work.freed_sem(u), 1)

            def gate_top(m):
                work.wait_full(dve, "L", m)
                dve.memset(carrier[:, 3:4], 0.0)
                dve.max(top[:, 0, :], work.tile("L")[:, 0:NE]).then_inc(top_ready, 1)
                dve.max(top[:, 1, :], work.tile("L")[:, P:P + NE]).then_inc(work.freed_sem("L"), 1)
                wait(dve, top_ready, m + 1)
                work.wait_read(dve, "L", m)
                dve.tensor_tensor(route[:], top[:, :, 0], top[:, :, 1], ALU.add).then_inc(route_ready, 1)

            def sum_out(m, p):
                u = f"D{p}"
                work.wait_full(dve, u, m)
                work.wait_read(dve, f"R{p}", m)
                dve.tensor_tensor(z[:, p, :], work.tile(u)[:], routed[:, p, :], ALU.add).then_inc(work.freed_sem(u), 1)
                work.wait_read(dve, u, m)
                dve.bn_stats(zstats[:, p, :], z[:, p, :]).then_inc(zstats_done, 1)
                wait(dve, zstats_done, 2 * m + p + 1)
                dve.memset(carrier[:, 1 + p:2 + p], 0.0)
                dve.bn_aggr(zmv[:, p, :], zstats[:, p, :]).then_inc(zaggr_done, 1)

            def z_normalise(m, p):
                wait(dve, zrstd_done, 2 * m + p + 1)
                dve.tensor_scalar(z[:, p, :], z[:, p, :], zmv[:, p, 0:1], zrstd[:, p:p + 1],
                                  ALU.subtract, ALU.mult).then_inc(z_norm, 1)

            def y_out(m, p):
                wait(dve, z_scaled, 2 * m + p + 1)
                wait(dve, res_biased[p], m + 1)
                wait(dve, y_stored[p], 16 * m)
                dve.tensor_tensor(yo[:, p, :], z[:, p, :], xres[:, p, :], ALU.add).then_inc(y_ready[p], 1)

            def slot(d):
                behind = not isinstance(d, int) or d > 0
                for c in range(IC):
                    square(d, c)
                    if c == 0 and behind:
                        z_normalise(d - 1, 1)
                    if c in (1, 3) and behind:
                        y_out(d - 1, c // 2)
                if isinstance(d, int) and d == 0:
                    for n in range(DPARTS):
                        split_low(n)
                gate_top(d)
                if not isinstance(d, int) or d < DUOS - 1:
                    for p in range(2):
                        x_lo(d + 1, p)
                sum_out(d, 0)
                if not isinstance(d, int) or d < DUOS - 2:
                    layernorm(d + 2)
                z_normalise(d, 0)
                if not isinstance(d, int) or d < DUOS - 2:
                    apply_norm(d + 2)
                sum_out(d, 1)

            steps(dve, slot, DUOS - 3, DUOS - 1, first_full=2)
            z_normalise(DUOS - 1, 1)
            for p in range(2):
                y_out(DUOS - 1, p)

        @block.tensor
        def _(pe):
            def x_transposes(m, p):
                u = f"X{p}"
                wait(pe, xln_ready, 2 * m + p + 1)
                work.wait_free(pe, u, m)
                for c in range(KC):
                    ins = pe.transpose(work.tile(u)[:, c * P:(c + 1) * P], xln[:, p, c * P:(c + 1) * P], ident[:])
                ins.then_inc(work.full_sem(u), 1)

            def up_chunk(m, c):
                u = f"H{c}"
                work.wait_free(pe, u, m)
                if c == 0:
                    for p in range(2):
                        work.wait_read(pe, f"X{p}", m)
                split3(pe, work.tile(u)[:, 0:2 * P], lambda a, k: up_w[a][:, k, c * P:(c + 1) * P],
                       lambda b, k: xT[b][:, k, :], KC).then_inc(work.full_sem(u), 1)

            def gate_logits(m):
                work.wait_free(pe, "G", m)
                split3(pe, work.tile("G")[0:NE, 0:2 * P], lambda a, k: gate_w[a][:, k, :],
                       lambda b, k: xT[b][:, k, :], KC).then_inc(work.full_sem("G"), 1)

            def turn_logits(m):
                work.wait_read(pe, "G", m)
                work.wait_free(pe, "L", m)
                for p in range(2):
                    ins = pe.transpose(work.tile("L")[:, p * P:(p + 1) * P], logitsT[:, p * P:(p + 1) * P],
                                       ident[:])
                ins.then_inc(work.full_sem("L"), 1)

            def from_tokens(m, p, u, w, n, left, chunks):
                work.wait_free(pe, u, m)
                split3(pe, work.tile(u)[:, 0:n], lambda a, k: left[a][:, k, p * P:(p + 1) * P],
                       lambda b, k: w[b][:, k, :], chunks).then_inc(work.full_sem(u), 1)

            pe.wait_ge(const_step, 5)
            for p in range(2):
                x_transposes(0, p)
            pe.wait_ge(early.up_lo, KC)

            def slot(d):
                for c in range(IC):
                    up_chunk(d, c)
                if not isinstance(d, int) or d < DUOS - 1:
                    for p in range(2):
                        x_transposes(d + 1, p)
                if isinstance(d, int):
                    pe.wait_ge(gate_lo, 1)
                    pe.wait_ge(early.lat_lo, KC)
                gate_logits(d)
                from_tokens(d, 0, "R0", lat_w, DIM, xT, KC)
                turn_logits(d)
                from_tokens(d, 1, "R1", lat_w, DIM, xT, KC)
                for p in range(2):
                    if p == 0:
                        wait(pe, hlo_ready, 8 * d + IC)
                        if isinstance(d, int):
                            pe.wait_ge(w_lo, DPARTS)
                    from_tokens(d, p, f"D{p}", down_w, DIM, hid, IC)

            steps(pe, slot, DUOS - 2, DUOS - 1)


def decoder_layer(nc, x, ctx_4096, a_wqT, a_bq, a_wkT, a_bk, a_wvT, a_bv, a_woT, a_bo,
                  x_w, x_b,
                  gate, up, down, fc1T, expertT, fc2, gamma, beta, out):
    after_attention = nc.dram_tensor("after_attention", [TOKENS, DIM], F32, kind="Internal").ap()
    after_window = nc.dram_tensor("after_window", [TOKENS, DIM], F32, kind="Internal").ap()
    with ExitStack() as ctx:
        psum = [ctx.enter_context(nc.psum_tensor(f"bank{b}", [P, 512], F32)) for b in range(8)]
        attention_out, window_out = RowsOut(nc, ctx, "a", 2), RowsOut(nc, ctx, "b", 1)
        window = WindowInputs(nc, ctx, after_attention, ctx_4096, x_w, x_b)
        attention_phase(nc, psum, x, a_wqT, a_bq, a_wkT, a_bk, a_wvT, a_bv, a_woT, a_bo,
                        after_attention, attention_out, window)
        early = ExpertWeights(nc, ctx, psum, up, fc1T, expertT, fc2, after_window)
        window_phase(nc, psum, after_attention, ctx_4096, window, attention_out.stored, after_window, window_out, early)
        expert_phase(nc, psum, after_window, window_out.stored[0], early, gate, down, gamma, beta, out)


def kernel(**inputs):
    import numpy as _np
    import concourse.bacc as _bacc
    from concourse import mybir as _mybir
    from concourse.bass_utils import run_bass_kernel_spmd as _run

    given = {n: _np.asarray(a) for n, a in inputs.items()}

    def turned(name):
        return _np.ascontiguousarray(given[name].T)

    x_w = _np.zeros((P, 4, P), _np.float32)
    x_b = _np.zeros((P, 4), _np.float32)
    for i, n in enumerate("qkvo"):
        for rows in (slice(0, SEQ), slice(SEQ, P)):
            x_w[rows, i, rows] = turned(f"L0_xattn_W{n}")
            x_b[rows, i] = given[f"L0_xattn_b{n}"]

    laid = {
        "x": given["x"].reshape(TOKENS, DIM),
        "ctx_4096": given["ctx_4096"].reshape(TOKENS, DIM),
        "a_wqT": turned("L0_attn_Wq"), "a_bq": _np.ascontiguousarray(given["L0_attn_bq"].reshape(GROUPS, P).T),
        "a_wkT": turned("L0_attn_Wk"), "a_bk": _np.ascontiguousarray(given["L0_attn_bk"].reshape(GROUPS, P).T),
        "a_wvT": turned("L0_attn_Wv"), "a_bv": given["L0_attn_bv"],
        "a_woT": turned("L0_attn_Wo"), "a_bo": given["L0_attn_bo"],
        "x_w": x_w, "x_b": x_b,
        "gate": given["L0_ffn_gate_w"], "up": given["L0_ffn_up_w"], "down": given["L0_ffn_down_w"],
        "fc1T": turned("L0_ffn_fc1_w"), "expertT": turned("L0_ffn_expert_w"), "fc2": given["L0_ffn_fc2_w"],
        "gamma": given["L0_ffn_ln_gamma"], "beta": given["L0_ffn_ln_beta"],
    }
    nc = _bacc.Bacc("TRN2", target_bir_lowering=False, num_devices=1)
    arrays, args = {}, []
    for name, a in laid.items():
        arrays[f"in_{name}"] = a
        args.append(nc.dram_tensor(f"in_{name}", a.shape, _mybir.dt.from_np(a.dtype), kind="ExternalInput").ap())
    args.append(nc.dram_tensor("out_rows", [TOKENS, DIM], F32, kind="ExternalOutput").ap())
    decoder_layer(nc, *args)
    r = _run(nc, [arrays], core_ids=[0])
    return r.results[0]["out_rows"].reshape(BATCH, SEQ, DIM)
```
